# Optimizing a Trainium2 kernel written in Bass

```python
import numpy as np
import jax
import jax.numpy as jnp

def _softmax(x, axis=-1):
    return jax.nn.softmax(x, axis=axis)

def _gelu(x):
    return jax.nn.gelu(x, approximate=True)

def _silu(x):
    return jax.nn.silu(x)

def _sigmoid(x):
    return jax.nn.sigmoid(x)

def _layernorm(x, axis=-1, eps=1e-05):
    m = jnp.mean(x, axis=axis, keepdims=True)
    v = jnp.var(x, axis=axis, keepdims=True)
    return (x - m) / jnp.sqrt(v + eps)

def _scatter_add(tgt, idx, src, axis=0):
    return tgt.at[idx].add(src)

def _segment_sum(src, seg, n):
    return jax.ops.segment_sum(src, seg, n)
kernel_name = 'mk_xattn_ffn_d2_seqx_r8_e02067'

def setup_inputs(seed: int=0):
    np.random.seed(seed)
    _w = jnp.asarray

    def _rec_inputs():
        import jax
        import jax.numpy as jnp
        _rk = jax.random.key(seed)
        x = -0.0002928 + 1 * jax.random.normal(jax.random.fold_in(_rk, 1), (8, 128, 256), jnp.float32)
        _lenS = 128 - jax.random.randint(jax.random.fold_in(_rk, 7), (8,), 0, max(1, 128 // 4) + 1, jnp.int32)
        _lenS2 = 128 - jax.random.randint(jax.random.fold_in(_rk, 8), (8,), 0, max(1, 128 // 4) + 1, jnp.int32)
        _ctx_2048P = jax.random.normal(jax.random.fold_in(_rk, 11), (8, 16, 256), jnp.float32)
        _ctx_2048c = jax.random.dirichlet(jax.random.fold_in(_rk, 511), 0.3 * jnp.ones((16,), jnp.float32), (8, 128))
        _ctx_2048t = jnp.einsum('bsk,bkd->bsd', _ctx_2048c, _ctx_2048P)
        _ctx_2048t = _ctx_2048t * jax.lax.rsqrt(jnp.mean(jnp.square(_ctx_2048t)) + 1e-12) * 0.953939
        ctx_2048 = -1.39393e-06 + 0.999914 * (_ctx_2048t + 0.3 * jax.random.normal(jax.random.fold_in(_rk, 611), (8, 128, 256), jnp.float32))
        return (x, ctx_2048)
    x, ctx_2048 = _rec_inputs()

    def _L0_xattn_setup():
        import jax, jax.numpy as jnp
        import numpy as np
        HID = 256
        H = 32
        HK = 8
        G = H // HK
        D = HID // H
        T = 128
        W_ATT = 32
        W_SSM = 64

        def _heads(x, n):
            B, Tt, _ = x.shape
            return x.reshape(B, Tt, n, D).transpose(0, 2, 1, 3)

        def _attend(q, k, v):
            pos = jnp.arange(T)
            rel = pos[None, :] - pos[:, None]
            slopes = jnp.power(2.0, -8.0 * jnp.arange(H, dtype=jnp.float32) / H)
            alibi = slopes[:, None, None] * rel.astype(jnp.float32)
            bias = jnp.concatenate([alibi, alibi], axis=-1)
            delta = -rel
            ssm_mask = (delta >= 0) & (delta < W_SSM)
            att_mask = (delta >= 0) & (delta < W_ATT)
            mask = jnp.concatenate([ssm_mask, att_mask], axis=-1)
            scores = jnp.einsum('bhqd,bhkd->bhqk', q, k) / np.sqrt(D).astype(np.float32)
            scores = scores + bias[None]
            scores = jnp.where(mask[None, None], scores, -jnp.inf)
            wei = jax.nn.softmax(scores, axis=-1)
            return jnp.einsum('bhqk,bhkd->bhqd', wei, v)
        key = jax.random.key(seed)
        ks = jax.random.split(key, 8)
        s = lambda fan_in: 1.0 / np.sqrt(fan_in)
        return {'hidden_states': jax.random.normal(ks[0], (2, T, HID), jnp.float32), 'ssm_states': jax.random.normal(ks[1], (2, T, HID), jnp.float32), 'Wq': jax.random.normal(ks[2], (2 * HID, HID), jnp.float32) * s(2 * HID), 'Wk': jax.random.normal(ks[3], (HID, HK * D), jnp.float32) * s(HID), 'Wv': jax.random.normal(ks[4], (HID, HK * D), jnp.float32) * s(HID), 'Wsk': jax.random.normal(ks[5], (HID, HK * D), jnp.float32) * s(HID), 'Wsv': jax.random.normal(ks[6], (HID, HK * D), jnp.float32) * s(HID), 'Wo': jax.random.normal(ks[7], (HID, HID), jnp.float32) * s(HID)}
    _L0_xattn_all = _L0_xattn_setup()
    _L0_xattn_in = {k: v for k, v in _L0_xattn_all.items() if k in ('Wq', 'Wk', 'Wv', 'Wsk', 'Wsv', 'Wo')}
    del _L0_xattn_all

    def _L0_ffn_setup():
        import jax, jax.numpy as jnp
        import numpy as np
        NUM_EXPERTS = 16
        TOP_K = 2
        HIDDEN = 256
        D_FF = 512
        BATCH, SEQ = (4, 256)

        def _moe_forward(hidden, router_w, W1, W2):
            B, S, D = hidden.shape
            x = hidden.reshape(-1, D)
            T = x.shape[0]
            logits = x @ router_w
            top_vals, top_ids = jax.lax.top_k(logits, TOP_K)
            probs = jax.nn.softmax(top_vals, axis=-1)
            combine = jnp.zeros((T, NUM_EXPERTS), dtype=x.dtype)
            combine = combine.at[jnp.arange(T)[:, None], top_ids].add(probs)
            out = jnp.zeros_like(x)
            for e in range(NUM_EXPERTS):
                h = jax.nn.silu(x @ W1[e]) @ W2[e]
                out = out + combine[:, e:e + 1] * h
            return out.reshape(B, S, D)
        key = jax.random.key(seed)
        k_h, k_r, k_w1, k_w2 = jax.random.split(key, 4)
        hidden = jax.random.normal(k_h, (BATCH, SEQ, HIDDEN), dtype=jnp.float32)
        router_w = jax.random.normal(k_r, (HIDDEN, NUM_EXPERTS), dtype=jnp.float32) * HIDDEN ** (-0.5)
        W1 = jax.random.normal(k_w1, (NUM_EXPERTS, HIDDEN, D_FF), dtype=jnp.float32) * HIDDEN ** (-0.5)
        W2 = jax.random.normal(k_w2, (NUM_EXPERTS, D_FF, HIDDEN), dtype=jnp.float32) * D_FF ** (-0.5)
        return {'hidden': hidden, 'router_w': router_w, 'W1': W1, 'W2': W2}
    _L0_ffn_all = _L0_ffn_setup()
    _L0_ffn_in = {k: v for k, v in _L0_ffn_all.items() if k in ('router_w', 'W1', 'W2')}
    del _L0_ffn_all

    def _L1_xattn_setup():
        import jax, jax.numpy as jnp
        import numpy as np
        key = jax.random.key(seed)
        k1, k2, k3, k4, k5 = jax.random.split(key, 5)
        B, D_MODEL, L = (2, 128, 256)
        HEAD_DIM = 8
        H = D_MODEL // HEAD_DIM
        return {'k': jax.random.normal(k1, (B, D_MODEL, L), dtype=jnp.float32), 'v': jax.random.normal(k2, (B, D_MODEL, L), dtype=jnp.float32), 'q': jax.random.normal(k3, (B, D_MODEL, L), dtype=jnp.float32), 'ssm_kernel': jax.random.normal(k4, (H, L), dtype=jnp.float32), 'D': jax.random.normal(k5, (H,), dtype=jnp.float32), 'head_dim': HEAD_DIM}
    _L1_xattn_all = _L1_xattn_setup()
    _L1_xattn_in = {k: v for k, v in _L1_xattn_all.items() if k in ('ssm_kernel', 'D')}
    del _L1_xattn_all

    def _L1_ffn_setup():
        import jax, jax.numpy as jnp
        import numpy as np
        B, S, D = (4, 64, 256)
        E, K, H = (8, 2, 176)
        HS = 2 * 176
        ALPHA = 0.001
        W_SCALE = 0.02

        def _moe_forward(hidden_states, gate_w, w_gate, w_up, w_down, sw_gate, sw_up, sw_down):
            b, s, d = hidden_states.shape
            x = hidden_states.reshape(-1, d)
            T = x.shape[0]
            logits = x @ gate_w
            scores = jax.nn.softmax(logits, axis=-1)
            topk_w, topk_idx = jax.lax.top_k(scores, K)
            mask = jax.nn.one_hot(topk_idx, E, dtype=scores.dtype).sum(axis=1)
            ce = mask.mean(axis=0)
            Pi = scores.mean(axis=0)
            aux_loss = (Pi * ce * E).sum() * ALPHA
            comb = jnp.zeros((T, E), dtype=x.dtype)
            comb = comb.at[jnp.arange(T)[:, None], topk_idx].add(topk_w)
            g = jax.nn.silu(jnp.einsum('td,edh->teh', x, w_gate)) * jnp.einsum('td,edh->teh', x, w_up)
            routed = jnp.einsum('teh,ehd,te->td', g, w_down, comb)
            shared = jax.nn.silu(x @ sw_gate) * (x @ sw_up) @ sw_down
            out = (routed + shared).reshape(b, s, d)
            return (out, aux_loss)
        key = jax.random.key(seed)
        ks = jax.random.split(key, 8)
        rn = lambda k, sh: jax.random.normal(k, sh, dtype=jnp.float32)
        return {'hidden_states': rn(ks[0], (B, S, D)), 'gate_w': rn(ks[1], (D, E)) * W_SCALE, 'w_gate': rn(ks[2], (E, D, H)) * W_SCALE, 'w_up': rn(ks[3], (E, D, H)) * W_SCALE, 'w_down': rn(ks[4], (E, H, D)) * W_SCALE, 'sw_gate': rn(ks[5], (D, HS)) * W_SCALE, 'sw_up': rn(ks[6], (D, HS)) * W_SCALE, 'sw_down': rn(ks[7], (HS, D)) * W_SCALE}
    _L1_ffn_all = _L1_ffn_setup()
    _L1_ffn_in = {k: v for k, v in _L1_ffn_all.items() if k in ('gate_w', 'w_gate', 'w_up', 'w_down', 'sw_gate', 'sw_up', 'sw_down')}
    del _L1_ffn_all
    return {'x': x, 'ctx_2048': ctx_2048, 'L0_xattn_Wq': _L0_xattn_in['Wq'], 'L0_xattn_Wk': _L0_xattn_in['Wk'], 'L0_xattn_Wv': _L0_xattn_in['Wv'], 'L0_xattn_Wsk': _L0_xattn_in['Wsk'], 'L0_xattn_Wsv': _L0_xattn_in['Wsv'], 'L0_xattn_Wo': _L0_xattn_in['Wo'], 'L0_ffn_router_w': _L0_ffn_in['router_w'], 'L0_ffn_W1': _L0_ffn_in['W1'], 'L0_ffn_W2': _L0_ffn_in['W2'], 'L1_xattn_ssm_kernel': _L1_xattn_in['ssm_kernel'], 'L1_xattn_D': _L1_xattn_in['D'], 'L1_ffn_gate_w': _L1_ffn_in['gate_w'], 'L1_ffn_w_gate': _L1_ffn_in['w_gate'], 'L1_ffn_w_up': _L1_ffn_in['w_up'], 'L1_ffn_w_down': _L1_ffn_in['w_down'], 'L1_ffn_sw_gate': _L1_ffn_in['sw_gate'], 'L1_ffn_sw_up': _L1_ffn_in['sw_up'], 'L1_ffn_sw_down': _L1_ffn_in['sw_down']}

def reference(x, ctx_2048, L0_xattn_Wq, L0_xattn_Wk, L0_xattn_Wv, L0_xattn_Wsk, L0_xattn_Wsv, L0_xattn_Wo, L0_ffn_router_w, L0_ffn_W1, L0_ffn_W2, L1_xattn_ssm_kernel, L1_xattn_D, L1_ffn_gate_w, L1_ffn_w_gate, L1_ffn_w_up, L1_ffn_w_down, L1_ffn_sw_gate, L1_ffn_sw_up, L1_ffn_sw_down):
    import jax
    import jax.numpy as jnp

    def _L0_xattn_ref(hidden_states, ssm_states, Wq, Wk, Wv, Wsk, Wsv, Wo):
        import jax, jax.numpy as jnp
        import numpy as np
        HID = 256
        H = 32
        HK = 8
        G = H // HK
        D = HID // H
        T = 128
        W_ATT = 32
        W_SSM = 64

        def _heads(x, n):
            B, Tt, _ = x.shape
            return x.reshape(B, Tt, n, D).transpose(0, 2, 1, 3)

        def _attend(q, k, v):
            pos = jnp.arange(T)
            rel = pos[None, :] - pos[:, None]
            slopes = jnp.power(2.0, -8.0 * jnp.arange(H, dtype=jnp.float32) / H)
            alibi = slopes[:, None, None] * rel.astype(jnp.float32)
            bias = jnp.concatenate([alibi, alibi], axis=-1)
            delta = -rel
            ssm_mask = (delta >= 0) & (delta < W_SSM)
            att_mask = (delta >= 0) & (delta < W_ATT)
            mask = jnp.concatenate([ssm_mask, att_mask], axis=-1)
            scores = jnp.einsum('bhqd,bhkd->bhqk', q, k) / np.sqrt(D).astype(np.float32)
            scores = scores + bias[None]
            scores = jnp.where(mask[None, None], scores, -jnp.inf)
            wei = jax.nn.softmax(scores, axis=-1)
            return jnp.einsum('bhqk,bhkd->bhqd', wei, v)
        B = hidden_states.shape[0]
        q = _heads(jnp.concatenate([ssm_states, hidden_states], axis=-1) @ Wq, H)
        k = _heads(hidden_states @ Wk, HK)
        v = _heads(hidden_states @ Wv, HK)
        ssm_k = _heads(ssm_states @ Wsk, HK)
        ssm_v = _heads(ssm_states @ Wsv, HK)
        rep = lambda x: jnp.repeat(x, G, axis=1)
        kcat = jnp.concatenate([rep(ssm_k), rep(k)], axis=2)
        vcat = jnp.concatenate([rep(ssm_v), rep(v)], axis=2)
        o = _attend(q, kcat, vcat)
        o = o.transpose(0, 2, 1, 3).reshape(B, T, HID)
        return o @ Wo

    def _L0_ffn_ref(hidden, router_w, W1, W2):
        import jax, jax.numpy as jnp
        import numpy as np
        NUM_EXPERTS = 16
        TOP_K = 2
        HIDDEN = 256
        D_FF = 512
        BATCH, SEQ = (4, 256)

        def _moe_forward(hidden, router_w, W1, W2):
            B, S, D = hidden.shape
            x = hidden.reshape(-1, D)
            T = x.shape[0]
            logits = x @ router_w
            top_vals, top_ids = jax.lax.top_k(logits, TOP_K)
            probs = jax.nn.softmax(top_vals, axis=-1)
            combine = jnp.zeros((T, NUM_EXPERTS), dtype=x.dtype)
            combine = combine.at[jnp.arange(T)[:, None], top_ids].add(probs)
            out = jnp.zeros_like(x)
            for e in range(NUM_EXPERTS):
                h = jax.nn.silu(x @ W1[e]) @ W2[e]
                out = out + combine[:, e:e + 1] * h
            return out.reshape(B, S, D)
        return _moe_forward(hidden, router_w, W1, W2)

    def _L1_xattn_ref(k, v, q, ssm_kernel, D, head_dim):
        import jax, jax.numpy as jnp
        import numpy as np
        B, HD, L = k.shape
        H = HD // head_dim
        fft_size = 2 * L
        k_ = k.reshape(B, H, head_dim, L)
        v_ = v.reshape(B, H, head_dim, L)
        q_ = q.reshape(B, H, head_dim, L)
        kv = jnp.einsum('bhil,bhjl->bijhl', k_, v_)
        kv_f = jnp.fft.rfft(kv, n=fft_size)
        kernel_f = jnp.fft.rfft(ssm_kernel, n=fft_size)
        y = jnp.fft.irfft(kv_f * kernel_f, n=fft_size)[..., :L]
        out = y + kv * D[None, None, None, :, None]
        out = jnp.einsum('bijhl,bhil->bjhl', out, q_)
        out = jnp.transpose(out, (0, 2, 1, 3)).reshape(B, H * head_dim, L)
        return out.astype(k.dtype)

    def _L1_ffn_ref(hidden_states, gate_w, w_gate, w_up, w_down, sw_gate, sw_up, sw_down):
        import jax, jax.numpy as jnp
        import numpy as np
        B, S, D = (4, 64, 256)
        E, K, H = (8, 2, 176)
        HS = 2 * 176
        ALPHA = 0.001
        W_SCALE = 0.02

        def _moe_forward(hidden_states, gate_w, w_gate, w_up, w_down, sw_gate, sw_up, sw_down):
            b, s, d = hidden_states.shape
            x = hidden_states.reshape(-1, d)
            T = x.shape[0]
            logits = x @ gate_w
            scores = jax.nn.softmax(logits, axis=-1)
            topk_w, topk_idx = jax.lax.top_k(scores, K)
            mask = jax.nn.one_hot(topk_idx, E, dtype=scores.dtype).sum(axis=1)
            ce = mask.mean(axis=0)
            Pi = scores.mean(axis=0)
            aux_loss = (Pi * ce * E).sum() * ALPHA
            comb = jnp.zeros((T, E), dtype=x.dtype)
            comb = comb.at[jnp.arange(T)[:, None], topk_idx].add(topk_w)
            g = jax.nn.silu(jnp.einsum('td,edh->teh', x, w_gate)) * jnp.einsum('td,edh->teh', x, w_up)
            routed = jnp.einsum('teh,ehd,te->td', g, w_down, comb)
            shared = jax.nn.silu(x @ sw_gate) * (x @ sw_up) @ sw_down
            out = (routed + shared).reshape(b, s, d)
            return (out, aux_loss)
        out, _aux = _moe_forward(hidden_states, gate_w, w_gate, w_up, w_down, sw_gate, sw_up, sw_down)
        return out
    x = x + _L0_xattn_ref(_layernorm(x, axis=-1), ctx_2048, L0_xattn_Wq, L0_xattn_Wk, L0_xattn_Wv, L0_xattn_Wsk, L0_xattn_Wsv, L0_xattn_Wo)
    x = x + _L0_ffn_ref(_layernorm(x, axis=-1), L0_ffn_router_w, L0_ffn_W1, L0_ffn_W2)
    x = x + _L1_xattn_ref(ctx_2048, ctx_2048, _layernorm(x, axis=-1), L1_xattn_ssm_kernel, L1_xattn_D, 8)
    x = x + _L1_ffn_ref(_layernorm(x, axis=-1), L1_ffn_gate_w, L1_ffn_w_gate, L1_ffn_w_up, L1_ffn_w_down, L1_ffn_sw_gate, L1_ffn_sw_up, L1_ffn_sw_down)
    return x

_drawn_inputs = setup_inputs


def setup_inputs(seed=0):
    import zlib

    import numpy as np

    out = dict(_drawn_inputs(seed))
    spreads = {}
    factors = {'L1_ffn_gate_w': 8.0,
     'L1_ffn_w_gate': 8.0,
     'L1_ffn_w_up': 8.0,
     'L1_ffn_w_down': 8.0,
     'L1_ffn_sw_gate': 8.0,
     'L1_ffn_sw_up': 8.0,
     'L1_ffn_sw_down': 8.0}
    for name, (base, spread) in spreads.items():
        noise = np.random.default_rng([zlib.crc32(name.encode()), seed]).standard_normal(out[name].shape)
        drawn = base * np.exp(spread * noise) if base else spread * noise
        out[name] = jnp.asarray(drawn.astype(out[name].dtype))
    for name, factor in factors.items():
        out[name] = (out[name] * factor).astype(out[name].dtype)
    return out
```

```python
from contextlib import ExitStack

import numpy as np

import concourse.bass as bass
from concourse import mybir

F32 = mybir.dt.float32
BF16 = mybir.dt.bfloat16
I32 = mybir.dt.int32
U32 = mybir.dt.uint32
ALU = mybir.AluOpType
ACT = mybir.ActivationFunctionType
AX = mybir.AxisListType

P = 128
B = 8
D = 256
KD = D // P
T = B * P

H0 = 32
G0 = 8
HG = H0 // G0
HD = 8
NQ = 54
NS = 51
WIN_SSM, WIN_ATT = 64, 32
SCALE = 1.0 / float(np.sqrt(HD))
NEG = -1e30
VW = G0 * (HD + 1)

HC = 16
CW = 8
NPAIR = B * CW * CW

EPS = 1e-5
HALF = T // 2


def slots_of(experts, ffn, chunk_rows, tiles):
    return dict(E=experts, F=ffn, rows=chunk_rows, tiles=tiles)


MOE = [
    dict(E=16, W=512, rows=[128, 128, 128, 128], tiles=2 * T // P + 15, wide=2048),
    dict(E=8, W=352, rows=[128, 48], tiles=2 * T // P + 7, wide=1216),
]
XS_ROWS = MOE[0]["tiles"] * P


def build(nc, a, out):
    with ExitStack() as ctx:
        def sb(name, shape, dt=F32):
            return ctx.enter_context(nc.sbuf_tensor(name, shape, dt))

        def sem(name):
            return ctx.enter_context(nc.semaphore(name))

        bank = [ctx.enter_context(nc.psum_tensor(f"bank{i}", [P, 512], F32)) for i in range(4)]
        st_ps = [ctx.enter_context(nc.psum_tensor(f"st_ps{i}", [P, 2, 512], F32)) for i in range(2)]
        banks = [bank[0], bank[1], bank[2], bank[3], st_ps[0][:, 0, :], st_ps[0][:, 1, :],
                 st_ps[1][:, 0, :], st_ps[1][:, 1, :]]

        def bk(i):
            return banks[i][:, :] if i < 4 else banks[i]

        qd = nc.dram_tensor("q_parts", [B, 3, HD, H0, P], BF16, kind="Internal").ap()
        kd = nc.dram_tensor("k_parts", [B, 3, HD, G0, 2, P], BF16, kind="Internal").ap()
        xs = nc.dram_tensor("rows_by_slot", [XS_ROWS, D], F32, kind="Internal").ap()
        ys = nc.dram_tensor("results_by_slot", [XS_ROWS, D], F32, kind="Internal").ap()

        wall = sb("wall", [P, 16 * 2048])
        x_sb = sb("x_sb", [P, B, D])
        h_sb = sb("h_sb", [P, B, D])
        hT = sb("hT", [P, KD, T])
        cT = sb("cT", [P, KD, T])
        parts = sb("parts", [P, 4608])
        q_parts = parts[:, 0:3072].bitcast(BF16).rearrange("p (j c t) -> p j c t", j=3, c=2)
        k_parts = parts[:, 3072:4608].bitcast(BF16).rearrange("p (j t) -> p j t", j=3)
        v_all = sb("v_all", [P, B, 2, G0, HD + 1])
        v_buf = sb("v_buf", [P, 2, 2, G0, HD + 1])
        wq = sb("wq", [P, 4, D])
        wk = sb("wk", [P, 4, 64])
        wv = sb("wv", [P, 4, 64])
        wo = sb("wo", [P, KD, D])
        masks = sb("masks", [P, 3, 512], BF16)
        identf = sb("identf", [P, P])
        identb = sb("identb", [P, P], BF16)
        anti = sb("anti", [P, P])
        tri = sb("tri", [P, P], BF16)
        onesb = sb("onesb", [P, P], BF16)
        iota = sb("iota", [P, 32])
        stats = sb("stats", [P, B, 6])
        mv = sb("mv", [P, B, 2])
        vare = sb("vare", [P, B])
        rstd = sb("rstd", [P, B])
        neghalf = sb("neghalf", [P, B])
        mx = sb("mx", [P, 2, H0])
        mneg = sb("mneg", [H0, P])
        mres = sb("mres", [H0, P])
        msplit = sb("msplit", [H0, 2, 3, P], BF16)
        rden = sb("rden", [P, H0])
        onorm = sb("onorm", [P, H0, HD])
        oTs = sb("oTs", [P, KD, P])

        att = 12 * 2048
        q_stack = [wall[:, att + 2048 * i: att + 2048 * (i + 1)].bitcast(BF16) for i in range(2)]
        k_stack = [wall[:, att + 4096 + 1024 * i: att + 4096 + 1024 * (i + 1)].bitcast(BF16)
                   .rearrange("p (g s t) -> p g s t", g=G0, s=2) for i in range(2)]
        p_buf = [wall[:, att + 6144 + 1024 * i: att + 6144 + 1024 * (i + 1)] for i in range(2)]
        pf = [wall[:, att + 6144 + 1024 * i: att + 6144 + 1024 * i + 512] for i in range(2)]
        pr = [wall[:, att + 6144 + 1024 * i + 512: att + 6144 + 1024 * (i + 1)] for i in range(2)]

        at = [0]

        def carve(n):
            at[0] += n
            assert at[0] <= 4608
            return parts[:, at[0] - n: at[0]]

        xt = [carve(D) for _ in range(2)]
        xTs = [carve(D) for _ in range(2)]
        act_h = [carve(512) for _ in range(2)]
        hTs = [carve(512) for _ in range(2)]
        y_sb = [carve(D) for _ in range(2)]
        gs = [carve(176) for _ in range(2)]
        logits = sb("logits", [P, B, 16])
        top = sb("top", [P, B, 8])
        topi = sb("topi", [P, B, 8], U32)
        idxf = sb("idxf", [P, 2, B])
        hot = sb("hot", [P, 2, B, 16])
        hotb = sb("hotb", [P, B, 16], BF16)
        pw = sb("pw", [P, 2, B])
        ptmp = sb("ptmp", [P, 4, B])
        cmp = parts[:, 0:31 * 16]
        cnt = sb("cnt", [P, 4, 16])
        base = sb("base", [P, B, 16])
        slotf = sb("slotf", [P, 2, B])
        slot = sb("slot", [P, 2, B], U32)
        etf = sb("etf", [P, 32])
        et = sb("et", [P, 32], I32)
        router = sb("router", [P, KD, 16])
        router1 = sb("router1", [P, KD, 8])
        y_in = [parts[:, D * i: D * (i + 1)] for i in range(8)]

        w1_ = 0
        moe_w = [wall[:, :].rearrange("p (e n) -> p e n", e=16),
                 wall[:, 0:8 * 1216].rearrange("p (e n) -> p e n", e=8)]
        at1 = 8 * 1216
        sgu = wall[:, at1: at1 + 1408].rearrange("p (c n) -> p c n", c=2)
        sdn = wall[:, at1 + 1408: at1 + 2176].rearrange("p (c n) -> p c n", c=3)
        at1 += 2176
        ctx_l = wall[:, at1: at1 + 2048].rearrange("p (c b n) -> p c b n", c=2, b=B)
        kv = [wall[:, at1 + 2048 + 1024 * i: at1 + 3072 + 1024 * i].rearrange("p (c n) -> p c n", c=2)
              for i in range(2)]
        toep = [wall[:, at1 + 4096 + 256 * i: at1 + 4352 + 256 * i] for i in range(2)]
        prod = [wall[:, at1 + 4608 + 512 * i: at1 + 5120 + 512 * i] for i in range(2)]
        convT = wall[:, at1 + 5632: at1 + 7680].rearrange("p (c b n) -> p c b n", c=2, b=B)
        at1 += 7680
        sh_g = [wall[:, at1 + 352 * i: at1 + 352 * (i + 1)] for i in range(2)]
        sh_h = [wall[:, at1 + 704 + 352 * i: at1 + 704 + 352 * (i + 1)] for i in range(2)]
        sh_T = [wall[:, at1 + 1408 + 384 * i: at1 + 1408 + 384 * (i + 1)] for i in range(2)]
        d_bc = sb("d_bc", [P, HC])

        names = ("x_in const_in ctx_in proj_in late_in wo_in zero_set zero_out neg_set stats_done var_done rstd_done "
                 "h_done tr_done tr_copied qk_proj qk_copied qk_split v_proj v_copied parts_out parts_out_0 "
                 "s_done s_reduced mT_done mneg_done m_split st_done exp_done pv_done v_ready onorm_done "
                 "oT_done oT_copied wo_done x_added const_rows dve_chain pool_chain act_chain "
                 "lay1_in ctxl_in kv_done conv_done conv_used toep_fixed convT_done back_done back_added "
                 "x_final out_done sh_up sh_sil sh_act sh_tr sh_trc sh_dn sh_dn_used").split()
        S = {n: sem(n) for n in names}
        stack_in = [[sem(f"stack_in_{p}{h}") for h in range(2)] for p in range(2)]
        m_in = [sem(f"m_in_{p}") for p in range(2)]
        expert_in = sem("expert_in")
        toep_in = [sem(f"toep_in_{p}") for p in range(2)]
        M = []
        for L in range(2):
            mn = ("logit_done logit_copied top_done prob_exp hot_done rank_done cnt_done slot_done scattered "
                  "xT_done xT_copied w1_done sil_done act_done hT_done hT_copied w2_done y_done combined").split()
            m = {n: sem(f"moe{L}_{n}") for n in mn}
            m["xin"] = [sem(f"moe{L}_xin{p}") for p in range(2)]
            m["stored"] = [sem(f"moe{L}_stored{p}") for p in range(2)]
            m["gathered"] = [sem(f"moe{L}_gathered{p}") for p in range(4)]
            M.append(m)

        block = ctx.enter_context(nc.Block())

        class Chain:

            def __init__(self, eng, s):
                self.eng, self.s, self.n, self.dyn = eng, s, 0, 0

            def link(self, ins):
                self.n += 1
                ins.then_inc(self.s, 1)
                self.eng.wait_ge(self.s, self.dyn + self.n)

        def stack_load(sp, b, j, p, first=False):
            for hf in range(2):
                if not first:
                    sp.wait_ge(S["st_done"], 8 * b - 16 + 4 * hf + 4)
                hs = slice(16 * hf, 16 * hf + 16)
                gsl = slice(4 * hf, 4 * hf + 4)
                bb = slice(b, b + 1) if isinstance(b, int) else bass.ds(b, 1)
                for r0, n, rep in ((0, 3, (0, 3)), (24, 2, (1, 2)), (40, 1, (2, 1))):
                    sp.dma_start(q_stack[p][r0:r0 + 8 * n, 2048 * hf:2048 * (hf + 1)],
                                 qd[bb, 0:n, :, hs, :].rearrange("o j d h t -> (o j d) (h t)")
                                 ).then_inc(stack_in[p][hf], 16)
                    src = kd[bb, rep[0], :, gsl, :, :].rearrange("o d g s t -> (o d) (g s t)")
                    for m in range(n):
                        sp.dma_start(k_stack[p][r0 + 8 * m:r0 + 8 * m + 8, gsl].rearrange("p g s t -> p (g s t)"),
                                     src).then_inc(stack_in[p][hf], 16)

        STACKED = 16 * (3 + 6)

        def moe_loads(sp, L):
            m = M[L]
            sp.wait_ge(m["scattered"], 16 * 2 * B)

            def load(t, j, p, first=False):
                if not first:
                    sp.wait_ge(m["xT_done"], t - 1)
                src = xs[bass.ds(t * P, P), :] if not isinstance(t, int) else xs[t * P:(t + 1) * P, :]
                sp.dma_start(xt[p], src).then_inc(m["xin"][p], 16)

            n = MOE[L]["tiles"]
            load(0, 0, 0, True)
            load(1, 0, 1, True)
            with sp.Fori(1, (n - 1) // 2) as i:
                load(2 * i, i, 0)
                load(2 * i + 1, i, 1)
            load(n - 1, n // 2, 0)

        @block.sync
        def _(sp):
            for b in range(B):
                sp.dma_start(x_sb[:, b, :], a["x"][b]).then_inc(S["x_in"], 16)
            sp.dma_start(identf[:, :], a["identf"]).then_inc(S["const_in"], 16)
            sp.dma_start(cT[:, :, :], a["ctx_d"]).then_inc(S["ctx_in"], 16)
            sp.dma_start(wq[:, :, :], a["wq"]).then_inc(S["proj_in"], 16)
            sp.dma_start(wk[:, :, :], a["wk"]).then_inc(S["proj_in"], 16)
            sp.dma_start(wv[:, :, :], a["wv"]).then_inc(S["proj_in"], 16)
            sp.dma_start(wo[:, :, :], a["wo"]).then_inc(S["late_in"], 16)
            sp.dma_start(masks[:, :, :], a["masks"]).then_inc(S["late_in"], 16)
            sp.dma_start(identb[:, :], a["identb"]).then_inc(S["late_in"], 16)
            for p in range(2):
                sp.dma_start(q_stack[p][48:51, :], a["slope_rows"]).then_inc(S["const_rows"], 16)
                sp.dma_start(k_stack[p][48:54], a["key_rows"]).then_inc(S["const_rows"], 16)
            for b in range(B):
                if b % 4 == 0:
                    sp.wait_ge(S["qk_split"], 3 * (b // 4) + 3)
                for j in range(3):
                    for c in range(2):
                        done = S["parts_out_0"] if b == 0 else S["parts_out"]
                        sp.dma_start(qd[b, j, :, 16 * c:16 * c + 16, :].rearrange("d h t -> h d t"),
                                     q_parts[:, j, c, P * b:P * (b + 1)]).then_inc(done, 16)
                        sp.dma_start(kd[b, j, :, :, c, :].rearrange("d g t -> g d t"),
                                     k_parts[64 * c:64 * c + 64, j, P * b:P * (b + 1)]).then_inc(done, 16)
                if b == 3:
                    sp.wait_ge(S["parts_out_0"], 12 * 16)
                    stack_load(sp, 0, 0, 0, first=True)
            sp.wait_ge(S["parts_out"], 7 * 12 * 16)
            stack_load(sp, 1, 0, 1, first=True)

            def body_loads(b, j, p, two):
                if two:
                    stack_load(sp, b + 1, j, 1 - p)

            def experts(e):
                sp.dma_start(moe_w[0][:, bass.ds(e, 2), :] if not isinstance(e, int) else moe_w[0][:, e:e + 2, :],
                             a["w_moe0"][:, bass.ds(e, 2), :] if not isinstance(e, int) else a["w_moe0"][:, e:e + 2, :]
                             ).then_inc(expert_in, 16)

            experts(0)
            experts(2)
            with sp.Fori(0, 3) as i:
                body_loads(1 + 2 * i, i + 1, 1, True)
                experts(2 * i + 4)
                body_loads(2 + 2 * i, i + 1, 0, True)
            experts(10)
            sp.wait_ge(S["pv_done"], 8 * B)
            for e in (12, 14):
                experts(e)
            sp.dma_start(router[:, :, :], a["router"]).then_inc(S["late_in"], 16)
            sp.dma_start(router1[:, :, :], a["gate_w"]).then_inc(S["late_in"], 16)
            moe_loads(sp, 0)
            sp.wait_ge(M[0]["w2_done"], MOE[0]["tiles"])
            sp.dma_start(ctx_l, a["ctx_l"]).then_inc(S["ctxl_in"], 16)
            sp.dma_start(d_bc[:, :], a["D"].partition_broadcast(P)).then_inc(S["ctxl_in"], 16)

            def toep_load(h, j, p, first=False):
                if not first:
                    sp.wait_ge(S["conv_done"], 2 * (h - 1))
                kp = a["kpad"]
                sp.dma_start(toep[p], bass.AP(tensor=kp.tensor, offset=h * 383, ap=[[1, P], [1, 2 * P]])
                             ).then_inc(toep_in[p], 16)

            toep_load(0, 0, 0, True)
            toep_load(1, 0, 1, True)
            sp.dma_start(moe_w[1], a["w_moe1"]).then_inc(S["lay1_in"], 16)
            sp.dma_start(sgu, a["sgu"]).then_inc(S["lay1_in"], 16)
            sp.dma_start(sdn, a["sdn"]).then_inc(S["lay1_in"], 16)
            with sp.Fori(1, HC // 2) as i:
                toep_load(2 * i, i, 0)
                toep_load(2 * i + 1, i, 1)
            moe_loads(sp, 1)
            for b in range(B):
                sp.wait_ge(S["x_final"], b + 1)
                sp.dma_start(out[b], x_sb[:, b, :]).then_inc(S["out_done"], 16)
            sp.wait_ge(S["out_done"], 16 * B)

        def pow_rstd(pool, n):
            if n == 0:
                pool.wait_ge(S["neg_set"], 1)
            pool.wait_ge(S["var_done"], n + 1)
            pool.tensor_tensor(rstd[:, :], vare[:, :], neghalf[:, :], ALU.pow).then_inc(S["rstd_done"], 1)

        def moe_pool(pool, L):
            m = M[L]
            if L == 0:
                pool.wait_ge(S["zero_out"], 16)
            pool.wait_ge(m["slot_done"], 1)
            for k in range(2):
                for b in range(B):
                    pool.indirect_dma_start(xs[:, :], bass.IndirectOffsetOnAxis(slot[:, k, b:b + 1], 0),
                                            h_sb[:, b, :], None).then_inc(m["scattered"], 16)

            def store(t, p):
                pool.wait_ge(m["y_done"], t + 1)
                dst = ys[bass.ds(t * P, P), :] if not isinstance(t, int) else ys[t * P:(t + 1) * P, :]
                pool.dma_start(dst, y_sb[p]).then_inc(m["stored"][p], 16)

            n = MOE[L]["tiles"]
            with pool.Fori(0, (n - 1) // 2) as i:
                store(2 * i, 0)
                store(2 * i + 1, 1)
            store(n - 1, 0)
            pool.wait_ge(m["stored"][0], 16 * ((n + 1) // 2))
            pool.wait_ge(m["stored"][1], 16 * (n // 2))
            for b in range(B):
                if b >= 4:
                    pool.wait_ge(m["combined"], b - 3)
                for k in range(2):
                    pool.indirect_dma_start(y_in[2 * (b % 4) + k], None, ys[:, :],
                                            bass.IndirectOffsetOnAxis(slot[:, k, b:b + 1], 0)
                                            ).then_inc(m["gathered"][b % 4], 16)

        @block.gpsimd
        def _(pool):
            pool.memset(h_sb[:, 0, :], 0.0).then_inc(S["zero_set"], 1)
            pool.memset(neghalf[:, :], -0.5).then_inc(S["neg_set"], 1)
            pool.memset(onesb[:, :], 1.0).then_inc(S["neg_set"], 1)
            pool.memset(v_all[:, :, :, :, HD:HD + 1], 1.0).then_inc(S["neg_set"], 1)
            pool.dma_start(tri[:, :], a["tri"]).then_inc(S["wo_in"], 16)
            pool.dma_start(anti[:, :], a["anti"]).then_inc(S["wo_in"], 16)
            pool.dma_start(iota[:, :], a["iota"]).then_inc(S["wo_in"], 16)
            pool.wait_ge(S["zero_set"], 1)
            pool.dma_start(xs.rearrange("(n p) d -> p n d", p=P),
                           bass.AP(tensor=h_sb, offset=0, ap=[[B * D, P], [0, XS_ROWS // P], [1, D]])
                           ).then_inc(S["zero_out"], 16)
            pow_rstd(pool, 0)
            pool.wait_ge(S["neg_set"], 3)

            def v_copy(b, p, first=False):
                if not first:
                    pool.wait_ge(S["pv_done"], 8 * b - 8)
                src = v_all[:, b] if isinstance(b, int) else v_all[:, bass.ds(b, 1)].rearrange("p o s g d -> p (o s) g d")
                pool.tensor_copy(v_buf[:, p], src).then_inc(S["v_ready"], 1)

            pool.wait_ge(S["v_copied"], 2 * B)
            v_copy(0, 0, True)
            v_copy(1, 1, True)

            with pool.Fori(0, 3) as i:
                v_copy(2 + 2 * i, 0)
                v_copy(3 + 2 * i, 1)
            pow_rstd(pool, 1)
            moe_pool(pool, 0)
            pow_rstd(pool, 2)
            pool.wait_ge(S["ctxl_in"], 32)

            def products(h, p, first=False):
                if not first:
                    pool.wait_ge(S["conv_done"], 2 * (h - 1))
                cols = slice(CW * h, CW * h + CW) if isinstance(h, int) else bass.ds(h * CW, CW)
                for c in range(2):
                    k = ctx_l[:, c, :, cols]
                    pool.tensor_tensor(kv[p][:, c, :].rearrange("p (b i j) -> p b i j", b=B, i=CW),
                                       k.unsqueeze(3).to_broadcast([P, B, CW, CW]),
                                       k.unsqueeze(2).to_broadcast([P, B, CW, CW]),
                                       ALU.mult).then_inc(S["kv_done"], 1)

            products(0, 0, True)
            products(1, 1, True)
            with pool.Fori(1, HC // 2) as i:
                products(2 * i, 0)
                products(2 * i + 1, 1)
            pow_rstd(pool, 3)
            moe_pool(pool, 1)

        def norm_rows(dve, n):
            for b in range(B):
                dve.bn_stats(stats[:, b, :], x_sb[:, b, :]).then_inc(S["stats_done"], 1)
            dve.wait_ge(S["stats_done"], n * (2 * B) + B)
            for b in range(B):
                dve.bn_aggr(mv[:, b, :], stats[:, b, :]).then_inc(S["stats_done"], 1)
            dve.wait_ge(S["stats_done"], (n + 1) * (2 * B))
            dve.tensor_scalar(vare[:, :], mv[:, :, 1], EPS, None, ALU.add).then_inc(S["var_done"], 1)
            dve.wait_ge(S["rstd_done"], n + 1)
            if n == 0:
                dve.wait_ge(S["zero_out"], 16)
            if n == 3:
                dve.wait_ge(M[0]["scattered"], 16 * 2 * B)
            for b in range(B):
                dve.tensor_scalar(h_sb[:, b, :], x_sb[:, b, :], mv[:, b, 0:1], rstd[:, b:b + 1],
                                  ALU.subtract, ALU.mult).then_inc(S["h_done"], 1)

        def moe_vector(dve, chain, L):
            m, E, n = M[L], MOE[L]["E"], MOE[L]["tiles"]
            lg, ho, hb, ba = logits[:, :, 0:E], hot[:, :, :, 0:E], hotb[:, :, 0:E], base[:, :, 0:E]

            def over_e(ap):
                return ap.unsqueeze(2).to_broadcast([P, B, E])

            dve.wait_ge(S["wo_in"], 48)
            dve.wait_ge(m["logit_done"], 1)
            src = bk(0)[:, 0:B * E].rearrange("p (b e) -> p b e", b=B)
            if L == 0:
                chain.link(dve.tensor_copy(lg, src))
            else:
                chain.link(dve.tensor_reduce(ptmp[:, 0, :], src, AX.X, ALU.max))
                chain.link(dve.tensor_tensor(ba, src, over_e(ptmp[:, 0, :]), ALU.subtract))
                dve.tensor_copy(ptmp[:, 1, :], ptmp[:, 0, :]).then_inc(m["logit_copied"], 1)
                dve.wait_ge(m["prob_exp"], 1)
                chain.link(dve.tensor_reduce(ptmp[:, 2, :], lg, AX.X, ALU.add))
                chain.link(dve.reciprocal(ptmp[:, 3, :], ptmp[:, 2, :]))
                chain.link(dve.tensor_tensor(lg, lg, over_e(ptmp[:, 3, :]), ALU.mult))
            for b in range(B):
                dve.max(top[:, b, :], logits[:, b, 0:E]).then_inc(m["top_done"], 1)
            dve.wait_ge(m["top_done"], B)
            for b in range(B):
                dve.max_index(topi[:, b, :], top[:, b, :], logits[:, b, 0:E]).then_inc(m["top_done"], 1)
            dve.wait_ge(m["top_done"], 2 * B)
            if L == 0:
                dve.tensor_tensor(ptmp[:, 0, :], top[:, :, 1], top[:, :, 0], ALU.subtract
                                  ).then_inc(m["logit_copied"], 1)
            else:
                chain.link(dve.tensor_copy(pw[:, 0, :], top[:, :, 0]))
                chain.link(dve.tensor_copy(pw[:, 1, :], top[:, :, 1]))
            for k in range(2):
                chain.link(dve.tensor_copy(idxf[:, k, :], topi[:, :, k]))
                chain.link(dve.tensor_tensor(ho[:, k], iota[:, 0:E].unsqueeze(1).to_broadcast([P, B, E]),
                                             over_e(idxf[:, k, :]), ALU.is_equal))
            dve.tensor_tensor(hb, ho[:, 0], ho[:, 1], ALU.add).then_inc(m["hot_done"], 1)
            if L == 0:
                dve.wait_ge(m["prob_exp"], 1)
                chain.link(dve.tensor_scalar(ptmp[:, 2, :], ptmp[:, 1, :], 1.0, None, ALU.add))
                chain.link(dve.reciprocal(pw[:, 0, :], ptmp[:, 2, :]))
                chain.link(dve.tensor_tensor(pw[:, 1, :], ptmp[:, 1, :], pw[:, 0, :], ALU.mult))
            nst = T // P
            dve.wait_ge(m["cnt_done"], 1)
            chain.link(dve.tensor_copy(cnt[:, 0, 0:E], bk(2)[:, 0:E]))
            c3 = cmp[:, 0:E * nst].rearrange("p (e s) -> p e s", e=E)
            chain.link(dve.tensor_scalar(cnt[:, 1, 0:nst], iota[:, 0:nst], float(P), None, ALU.mult))
            chain.link(dve.tensor_tensor(c3, cnt[:, 0, 0:E].unsqueeze(2).to_broadcast([P, E, nst]),
                                         cnt[:, 1, 0:nst].unsqueeze(1).to_broadcast([P, E, nst]), ALU.is_gt))
            chain.link(dve.tensor_reduce(cnt[:, 2, 0:E], c3, AX.X, ALU.add))
            chain.link(dve.tensor_tensor_scan(cnt[:, 3, 0:E], cnt[:, 2, 0:E], cnt[:, 2, 0:E], 0.0,
                                              ALU.add, ALU.bypass))
            chain.link(dve.tensor_tensor(cnt[:, 2, 0:E], cnt[:, 3, 0:E], cnt[:, 2, 0:E], ALU.subtract))
            chain.link(dve.tensor_scalar(cnt[:, 2, 0:E], cnt[:, 2, 0:E], float(P), None, ALU.mult))
            dve.wait_ge(m["rank_done"], 1)
            rank = bk(1)[:, 0:B * E].rearrange("p (b e) -> p b e", b=B)
            chain.link(dve.tensor_tensor(ba, rank, cnt[:, 2, 0:E].unsqueeze(1).to_broadcast([P, B, E]), ALU.add))
            for k in range(2):
                chain.link(dve.tensor_tensor(ho[:, k], ho[:, k], ba, ALU.mult))
                chain.link(dve.tensor_reduce(slotf[:, k, :], ho[:, k], AX.X, ALU.add))
            if L == 1:
                dve.wait_ge(M[0]["gathered"][3], 64)
            chain.link(dve.tensor_copy(slot[:, :, :], slotf[:, :, :]))
            c3 = cmp[:, 0:n * E].rearrange("p (t e) -> p t e", t=n)
            chain.link(dve.tensor_tensor(c3, cnt[:, 3, 0:E].unsqueeze(1).to_broadcast([P, n, E]),
                                         iota[:, 0:n].unsqueeze(2).to_broadcast([P, n, E]), ALU.is_le))
            chain.link(dve.tensor_reduce(etf[:, 0:n], c3, AX.X, ALU.add))
            chain.link(dve.tensor_scalar(etf[:, 0:n], etf[:, 0:n], float(E - 1), None, ALU.min))
            dve.tensor_copy(et[:, 0:n], etf[:, 0:n]).then_inc(m["slot_done"], 1)
            if L == 1:
                shared_vector(dve)

            def hT_copy(t, j, p, first=False):
                dve.wait_ge(m["hT_done"], t + 1)
                if not first:
                    dve.wait_ge(m["w2_done"], t - 1)
                w = 512 if L == 0 else 2 * P
                if L == 0:
                    dve.tensor_copy(hTs[p], bk(2 + p)).then_inc(m["hT_copied"], 1)
                else:
                    dve.tensor_copy(hTs[p][:, 0:P], bk(2 + p)[:, 0:P]).then_inc(m["hT_copied"], 1)
                    dve.tensor_copy(hTs[p][0:48, P:2 * P], bk(2 + p)[0:48, P:2 * P]).then_inc(m["hT_copied"], 1)

            def gate(t, j, p, first=False):
                dve.wait_ge(m["sil_done"], t + 1)
                if not first:
                    dve.wait_ge(m["hT_done"], t - 1)
                dve.tensor_tensor(act_h[p][:, 0:176], gs[p], bk(p)[:, 176:352], ALU.mult
                                  ).then_inc(m["act_done"], 1)

            def step(t, j, p, first=False, last=False):
                hT_copy(t, j, p, first)
                if L == 1 and not last:
                    gate(t + 1, j, 1 - p, first and p == 0)

            if L == 1:
                gate(0, 0, 0, True)
            step(0, 0, 0, True)
            if L == 0:
                step(1, 0, 1, True)
            else:
                step(1, 0, 1, True)
            with dve.Fori(1, (n - 1) // 2) as i:
                step(2 * i, i, 0)
                step(2 * i + 1, i, 1)
            step(n - 1, n // 2, 0, last=True)
            for b in range(B):
                dve.wait_ge(m["gathered"][b % 4], 32 * (b // 4 + 1))
                chain.link(dve.scalar_tensor_tensor(x_sb[:, b, :], y_in[2 * (b % 4)], pw[:, 0, b:b + 1],
                                                    x_sb[:, b, :], ALU.mult, ALU.add))
                ins = dve.scalar_tensor_tensor(x_sb[:, b, :], y_in[2 * (b % 4) + 1], pw[:, 1, b:b + 1],
                                               x_sb[:, b, :], ALU.mult, ALU.add)
                ins.then_inc(m["combined"], 1)
                if L == 1:
                    dve.wait_ge(m["combined"], b + 1)
                    dve.sem_inc(S["x_final"], 1)
            if L == 0:
                dve.wait_ge(m["combined"], B)

        def shared_vector(dve):
            for b in range(B):
                p = b % 2
                dve.wait_ge(S["sh_sil"], b + 1)
                if b >= 2:
                    dve.wait_ge(S["sh_tr"], b - 1)
                dve.tensor_tensor(sh_h[p], sh_g[p], bk(4)[:, 0:352] if p == 0 else bk(6)[:, 0:352], ALU.mult
                                  ).then_inc(S["sh_act"], 1)
                if b >= 1:
                    shared_add(dve, b - 1)
            shared_add(dve, B - 1)

        def shared_add(dve, b):
            dve.wait_ge(S["sh_dn"], b + 1)
            dve.tensor_tensor(x_sb[:, b, :], x_sb[:, b, :], bk(0)[:, 256:512], ALU.add
                              ).then_inc(S["sh_dn_used"], 1)

        @block.vector
        def _(dve):
            chain = Chain(dve, S["dve_chain"])
            dve.wait_ge(S["x_in"], 16 * B)
            norm_rows(dve, 0)
            for u in range(6):
                hf, m = divmod(u, 3)
                ts = slice(HALF * hf, HALF * (hf + 1))
                part = [q_parts[:, j, m, ts] if m < 2 else k_parts[:, j, ts] for j in range(3)]
                dve.wait_ge(S["qk_copied"], u + 1)
                chain.link(dve.tensor_copy(part[0], pf[u % 2]))
                chain.link(dve.tensor_tensor(pr[u % 2], pf[u % 2], part[0], ALU.subtract))
                chain.link(dve.tensor_copy(part[1], pr[u % 2]))
                dve.tensor_tensor(part[2], pr[u % 2], part[1], ALU.subtract).then_inc(S["qk_split"], 1)
            dve.wait_ge(S["neg_set"], 3)
            for u in range(2):
                dve.wait_ge(S["v_proj"], u + 1)
                for b in range(4 * u, 4 * u + 4):
                    for s in range(2):
                        dve.tensor_copy(v_all[:, b, s, :, 0:HD],
                                        bk(6 + u)[:, P * (b % 4) + 64 * s: P * (b % 4) + 64 * s + 64]
                                        .rearrange("p (g d) -> p g d", g=G0)).then_inc(S["v_copied"], 1)

            def reduce(b, p, u):
                dve.wait_ge(S["s_done"], 16 * b + u + 1)
                dve.tensor_reduce(mx[:, p, 2 * u:2 * u + 2],
                                  bk(u % 2).rearrange("p (h k) -> p h k", h=2), AX.X, ALU.max
                                  ).then_inc(S["s_reduced"], 1)

            def split_max(b, j, p, first=False):
                dve.wait_ge(S["mT_done"], b + 1)
                ins = dve.tensor_scalar(mneg[:, :], bk(3)[0:H0, 0:P], -1.0, None, ALU.mult)
                ins.then_inc(S["mneg_done"], 1)
                dve.wait_ge(S["mneg_done"], b + 1)
                if not first:
                    dve.wait_ge(m_in[p], 48 * j)
                chain.link(dve.tensor_copy(msplit[:, p, 0, :], mneg[:, :]))
                chain.link(dve.tensor_tensor(mres[:, :], mneg[:, :], msplit[:, p, 0, :], ALU.subtract))
                chain.link(dve.tensor_copy(msplit[:, p, 1, :], mres[:, :]))
                dve.tensor_tensor(msplit[:, p, 2, :], mres[:, :], msplit[:, p, 1, :],
                                  ALU.subtract).then_inc(S["m_split"], 1)

            def normalise(b):
                o = bk(2)[:, 0:H0 * (HD + 1)].rearrange("p (h d) -> p h d", h=H0)
                dve.wait_ge(S["pv_done"], 8 * b + 8)
                dve.wait_ge(S["oT_done"], b)
                chain.link(dve.reciprocal(rden[:, :], o[:, :, HD:HD + 1].rearrange("p h o -> p (h o)")))
                dve.tensor_tensor(onorm[:, :, :], o[:, :, 0:HD],
                                  rden[:, :].unsqueeze(2).to_broadcast([P, H0, HD]), ALU.mult
                                  ).then_inc(S["onorm_done"], 1)

            def add_attention(b):
                dve.wait_ge(S["wo_done"], b + 1)
                xb = x_sb[:, b, :] if isinstance(b, int) else x_sb[:, bass.ds(b, 1), :].rearrange("p o d -> p (o d)")
                dve.tensor_tensor(xb, xb, bk(3)[:, 256:512], ALU.add).then_inc(S["x_added"], 1)

            UNITS = [3, 3, 3, 3, 2, 2, 0, 0]

            def body(b, j, p, first=False, last=False):
                u = 0
                for g in range(G0):
                    if not last:
                        for _ in range(UNITS[g]):
                            reduce(b + 1, 1 - p, u)
                            u += 1
                    if g == 0 and not first:
                        normalise(b - 1)
                    if g == 3 and not first:
                        add_attention(b - 1)
                if not last:
                    split_max(b + 1, j + (p == 1) if not isinstance(j, int) else j + (p == 1), 1 - p, first=first)

            for u in range(16):
                reduce(0, 0, u)
            split_max(0, 0, 0, True)
            body(0, 0, 0, first=True)
            n0 = chain.n
            with dve.Fori(0, 3) as i:
                per = 8
                chain.dyn = i * per
                body(1 + 2 * i, i, 1)
                body(2 + 2 * i, i + 1, 0)
                assert chain.n == n0 + per, (chain.n, n0)
            chain.n, chain.dyn = n0 + 3 * per, 0
            body(7, 3, 1, last=True)
            normalise(7)
            add_attention(7)
            dve.wait_ge(S["x_added"], B)
            norm_rows(dve, 1)
            moe_vector(dve, chain, 0)
            norm_rows(dve, 2)
            dve.wait_ge(S["ctxl_in"], 32)
            dve.wait_ge(S["wo_in"], 48)

            def diagonal(h, j, p):
                dve.wait_ge(toep_in[p], 16 * (j + 1))
                dcol = d_bc[:, h:h + 1] if isinstance(h, int) else d_bc[:, bass.ds(h, 1)]
                dve.scalar_tensor_tensor(toep[p][:, 0:P], anti[:, :], dcol, toep[p][:, 0:P],
                                         ALU.mult, ALU.add).then_inc(S["toep_fixed"], 1)

            def weigh(h, p):
                for c in range(2):
                    dve.wait_ge(S["conv_done"], 2 * h + c + 1)
                    cols = slice(CW * h, CW * h + CW) if isinstance(h, int) else bass.ds(h * CW, CW)
                    q = hT[:, c, :].rearrange("p (b n) -> p b n", b=B)[:, :, cols]
                    y = bk(2 * p + c).rearrange("p (b i j) -> p b j i", b=B, i=CW)
                    pv = prod[c].rearrange("p (b j i) -> p b j i", b=B, j=CW)
                    dve.tensor_tensor(pv, y, q.unsqueeze(2).to_broadcast([P, B, CW, CW]), ALU.mult
                                      ).then_inc(S["conv_used"], 1)
                    dve.wait_ge(S["conv_used"], 2 * h + c + 1)
                    dve.tensor_reduce(convT[:, c, :, cols], pv, AX.X, ALU.add).then_inc(S["convT_done"], 1)

            diagonal(0, 0, 0)
            diagonal(1, 0, 1)
            dve.wait_ge(S["tr_copied"], 3 * B)
            with dve.Fori(0, HC // 2 - 1) as i:
                weigh(2 * i, 0)
                diagonal(2 * i + 2, i + 1, 0)
                weigh(2 * i + 1, 1)
                diagonal(2 * i + 3, i + 1, 1)
            weigh(HC - 2, 0)
            weigh(HC - 1, 1)
            for b in range(B):
                dve.wait_ge(S["back_done"], b + 1)
                dve.tensor_tensor(x_sb[:, b, :], x_sb[:, b, :], bk(4 + b % 2)[:, 0:D], ALU.add
                                  ).then_inc(S["back_added"], 1)
            dve.wait_ge(S["back_added"], B)
            norm_rows(dve, 3)
            moe_vector(dve, chain, 1)

        def copy_rows(act, n):
            for b in range(B):
                act.wait_ge(S["tr_done"], n * B + b + 1)
                act.activation(hT[:, :, P * b:P * (b + 1)],
                               bk(6 + b % 2)[:, 0:2 * P].rearrange("p (c t) -> p c t", c=KD),
                               ACT.Copy).then_inc(S["tr_copied"], 1)

        def moe_scalar(act, L):
            m, n, E = M[L], MOE[L]["tiles"], MOE[L]["E"]
            act.wait_ge(m["logit_copied"], 1)
            if L == 0:
                act.activation(ptmp[:, 1, :], ptmp[:, 0, :], ACT.Exp).then_inc(m["prob_exp"], 1)
            else:
                act.activation(logits[:, :, 0:E], base[:, :, 0:E], ACT.Exp).then_inc(m["prob_exp"], 1)
                for b in range(B):
                    p = b % 2
                    act.wait_ge(S["sh_up"], b + 1)
                    if b >= 2:
                        act.wait_ge(S["sh_act"], b - 1)
                    act.activation(sh_g[p], bk(5)[:, 0:352] if p == 0 else bk(7)[:, 0:352], ACT.Silu
                                   ).then_inc(S["sh_sil"], 1)
                    act.wait_ge(S["sh_tr"], b + 1)
                    if b >= 2:
                        act.wait_ge(S["sh_dn"], b - 1)
                    act.activation(sh_T[p][:, 0:2 * P], bk(1)[:, 0:2 * P], ACT.Copy).then_inc(S["sh_trc"], 1)
                    act.activation(sh_T[p][0:96, 2 * P:3 * P], bk(1)[0:96, 2 * P:3 * P], ACT.Copy
                                   ).then_inc(S["sh_trc"], 1)

            def xT_copy(t, j, p, first=False):
                act.wait_ge(m["xT_done"], t + 1)
                if not first:
                    act.wait_ge(m["w1_done"], t - 1)
                act.activation(xTs[p], bk(4 + p)[:, 0:D], ACT.Copy).then_inc(m["xT_copied"], 1)

            def silu(t, j, p, first=False):
                act.wait_ge(m["w1_done"], t + 1)
                if L == 0:
                    if not first:
                        act.wait_ge(m["hT_done"], t - 1)
                    act.activation(act_h[p], bk(p), ACT.Silu).then_inc(m["act_done"], 1)
                else:
                    if not first:
                        act.wait_ge(m["act_done"], t - 1)
                    act.activation(gs[p], bk(p)[:, 0:176], ACT.Silu).then_inc(m["sil_done"], 1)

            def y_copy(t, j, p, first=False):
                act.wait_ge(m["w2_done"], t + 1)
                if not first:
                    act.wait_ge(m["stored"][p], 16 * j)
                act.activation(y_sb[p], bk(6 + p)[:, 0:D], ACT.Copy).then_inc(m["y_done"], 1)

            def step(t, j, p, first=False, left=9):
                if left > 1:
                    silu(t + 1, j, 1 - p, first and p == 0)
                y_copy(t, j, p, first)
                if left > 2:
                    xT_copy(t + 2, j + 1, p)

            xT_copy(0, 0, 0, True)
            silu(0, 0, 0, True)
            xT_copy(1, 0, 1, True)
            step(0, 0, 0, True)
            step(1, 0, 1, True)
            with act.Fori(1, (n - 3) // 2) as i:
                step(2 * i, i, 0)
                step(2 * i + 1, i, 1)
            for t in range(n - 3, n):
                step(t, t // 2, t % 2, left=n - t)

        @block.scalar
        def _(act):
            copy_rows(act, 0)
            for u in range(6):
                hf, m = divmod(u, 3)
                act.wait_ge(S["qk_proj"], u + 1)
                if u >= 2:
                    act.wait_ge(S["qk_split"], u - 1)
                act.activation(pf[u % 2], bk(u), ACT.Copy, scale=SCALE if m < 2 else 1.0
                               ).then_inc(S["qk_copied"], 1)
            act.wait_ge(S["qk_split"], 6)

            def exps(b, p, g):
                act.wait_ge(S["st_done"], 8 * b + g + 1)
                if not (isinstance(b, int) and b == 0 and g < 2):
                    act.wait_ge(S["pv_done"], 8 * b + g - 1)
                act.activation(p_buf[g % 2], st_ps[g % 2][:, :, :].rearrange("p s n -> p (s n)"), ACT.Exp
                               ).then_inc(S["exp_done"], 1)

            def m_rows(b, j, p, first=False):
                act.wait_ge(S["m_split"], b + 1)
                if not first:
                    act.wait_ge(S["st_done"], 8 * b - 8)
                for r in range(3):
                    act.dma_start(q_stack[p][NS + r:NS + r + 1, :].rearrange("o (h t) -> o h t", h=H0),
                                   msplit[:, p, r, :]).then_inc(m_in[p], 16)

            def copy_oT(b):
                act.wait_ge(S["oT_done"], b + 1)
                if not (isinstance(b, int) and b == 0):
                    act.wait_ge(S["wo_done"], b)
                act.activation(oTs[:, :, :].rearrange("p c t -> p (c t)"), bk(3)[:, 0:2 * P], ACT.Copy
                               ).then_inc(S["oT_copied"], 1)

            def body(b, j, p, first=False, last=False):
                for g in range(G0):
                    exps(b, p, g)
                    if g == 2 and not first:
                        copy_oT(b - 1)
                    if g == 6 and not last:
                        m_rows(b + 1, j + (1 if p else 0), 1 - p, first)

            m_rows(0, 0, 0, True)
            body(0, 0, 0, first=True)
            with act.Fori(0, 3) as i:
                body(1 + 2 * i, i, 1)
                body(2 + 2 * i, i + 1, 0)
            body(7, 3, 1, last=True)
            copy_oT(7)
            copy_rows(act, 1)
            moe_scalar(act, 0)
            copy_rows(act, 2)
            copy_rows(act, 3)
            moe_scalar(act, 1)

        def turn_rows(pe, n):
            for b in range(B):
                pe.wait_ge(S["h_done"], n * B + b + 1)
                if n * B + b >= 2:
                    pe.wait_ge(S["tr_copied"], n * B + b - 1)
                for c in range(KD):
                    ins = pe.transpose(bk(6 + b % 2)[:, P * c:P * (c + 1)], h_sb[:, b, P * c:P * (c + 1)],
                                       identf[:, :])
                ins.then_inc(S["tr_done"], 1)

        def moe_tensor(pe, L):
            m, E, n = M[L], MOE[L]["E"], MOE[L]["tiles"]
            rows, W = MOE[L]["rows"], MOE[L]["W"]
            rw = router if L == 0 else router1
            weights = moe_w[L]
            pe.wait_ge(S["tr_copied"], (1 + 2 * L) * B + B)
            pe.wait_ge(S["late_in"], 80)
            pe.wait_ge(S["wo_in"], 48)
            for b in range(B):
                for c in range(KD):
                    ins = pe.matmul(bk(0)[:, E * b:E * (b + 1)], hT[:, c, P * b:P * (b + 1)], rw[:, c, :],
                                    start=(c == 0), stop=(c == KD - 1))
            ins.then_inc(m["logit_done"], 1)
            pe.wait_ge(m["hot_done"], 1)
            hb = hotb[:, :, 0:E]
            rk = bk(1)[:, 0:B * E].rearrange("p (b e) -> p b e", b=B)
            pe.matmul(rk, tri[:, :], hb, start=True, stop=True)
            for s in range(1, B):
                ins = pe.matmul(rk[:, s:B, :], onesb[:, :], hb[:, 0:B - s, :], start=False, stop=True,
                                skip_group_check=True)
            ins.then_inc(m["rank_done"], 1)
            for b in range(B):
                ins = pe.matmul(bk(2)[:, 0:E], onesb[:, :], hb[:, b, :], start=(b == 0), stop=(b == B - 1))
            ins.then_inc(m["cnt_done"], 1)
            pe.wait_ge(m["slot_done"], 1)
            if L == 0:
                pe.wait_ge(expert_in, 16 * 8)
            else:
                pe.wait_ge(S["lay1_in"], 48)
                shared_tensor(pe)

            def turn_x(t, j, p, first=False):
                pe.wait_ge(m["xin"][p], 16 * (j + 1))
                if not first:
                    pe.wait_ge(m["xT_copied"], t - 1)
                for c in range(KD):
                    ins = pe.transpose(bk(4 + p)[:, P * c:P * (c + 1)], xt[p][:, P * c:P * (c + 1)], identf[:, :])
                ins.then_inc(m["xT_done"], 1)

            def expert(t):
                col = et[0:1, t:t + 1] if isinstance(t, int) else et[0:1, bass.ds(t, 1)]
                return pe.value_load(col, min_val=0, max_val=E - 1)

            def up(t, j, p, first=False):
                e = expert(t)
                pe.wait_ge(m["xT_copied"], t + 1)
                if not first:
                    pe.wait_ge(m["act_done"], t - 1)
                for c in range(KD):
                    ins = pe.matmul(bk(p)[:, 0:W], xTs[p][:, P * c:P * (c + 1)],
                                    weights[:, bass.ds(e, 1), W * c:W * (c + 1)].rearrange("p o n -> p (o n)"),
                                    start=(c == 0), stop=(c == KD - 1))
                ins.then_inc(m["w1_done"], 1)

            def turn_h(t, j, p, first=False):
                pe.wait_ge(m["act_done"], t + 1)
                if not first:
                    pe.wait_ge(m["hT_copied"], (t - 1) * (1 + L))
                for c, r in enumerate(rows):
                    ins = pe.transpose(bk(2 + p)[0:r, P * c:P * (c + 1)], act_h[p][:, P * c:P * c + r], identf[:, :])
                ins.then_inc(m["hT_done"], 1)

            def down(t, j, p, first=False):
                e = expert(t)
                pe.wait_ge(m["hT_copied"], (t + 1) * (1 + L))
                if not first:
                    pe.wait_ge(m["y_done"], t - 1)
                for c, r in enumerate(rows):
                    w0 = KD * W + D * c
                    ins = pe.matmul(bk(6 + p)[:, 0:D], hTs[p][0:r, P * c:P * (c + 1)],
                                    weights[0:r, bass.ds(e, 1), w0:w0 + D].rearrange("p o n -> p (o n)"),
                                    start=(c == 0), stop=(c == len(rows) - 1))
                ins.then_inc(m["w2_done"], 1)

            def step(t, j, p, first=False, left=9):
                turn_h(t, j, p, first)
                if left > 1:
                    up(t + 1, j, 1 - p, first and p == 0)
                down(t, j, p, first)
                if left > 2:
                    turn_x(t + 2, j + 1, p)

            turn_x(0, 0, 0, True)
            up(0, 0, 0, True)
            turn_x(1, 0, 1, True)
            step(0, 0, 0, True)
            step(1, 0, 1, True)
            with pe.Fori(1, (n - 3) // 2) as i:
                step(2 * i, i, 0)
                step(2 * i + 1, i, 1)
            for t in range(n - 3, n):
                step(t, t // 2, t % 2, left=n - t)

        def shared_tensor(pe):
            def up(b):
                if b >= 2:
                    pe.wait_ge(S["sh_act"], b - 1)
                for n in range(2):
                    for c in range(KD):
                        ins = pe.matmul(bk(4 + 2 * (b % 2) + 1 - n)[:, 0:352], hT[:, c, P * b:P * (b + 1)],
                                        sgu[:, c, 352 * n:352 * (n + 1)], start=(c == 0), stop=(c == KD - 1))
                ins.then_inc(S["sh_up"], 1)

            up(0)
            for b in range(B):
                p = b % 2
                if b + 1 < B:
                    up(b + 1)
                pe.wait_ge(S["sh_act"], b + 1)
                if b >= 1:
                    pe.wait_ge(S["sh_trc"], 2 * b)
                for c, r in enumerate([P, P, 96]):
                    ins = pe.transpose(bk(1)[0:r, P * c:P * (c + 1)], sh_h[p][:, P * c:P * c + r], identf[:, :])
                ins.then_inc(S["sh_tr"], 1)
                pe.wait_ge(S["sh_trc"], 2 * b + 2)
                if b >= 1:
                    pe.wait_ge(S["sh_dn_used"], b)
                for c, r in enumerate([P, P, 96]):
                    ins = pe.matmul(bk(0)[:, 256:512], sh_T[p][0:r, P * c:P * (c + 1)], sdn[0:r, c, :],
                                    start=(c == 0), stop=(c == 2))
                ins.then_inc(S["sh_dn"], 1)
            pe.wait_ge(S["sh_dn_used"], B)

        @block.tensor
        def _(pe):
            pe.wait_ge(S["const_in"], 16)
            turn_rows(pe, 0)
            pe.wait_ge(S["tr_copied"], B)
            pe.wait_ge(S["ctx_in"], 16)
            pe.wait_ge(S["proj_in"], 48)

            def src(c):
                return cT[:, c, :] if c < 2 else hT[:, c - 2, :]

            for hf in range(2):
                ts = slice(HALF * hf, HALF * (hf + 1))
                for mm in range(2):
                    for c in range(4):
                        ins = pe.matmul(bk(3 * hf + mm), wq[:, c, P * mm:P * (mm + 1)], src(c)[:, ts],
                                        start=(c == 0), stop=(c == 3))
                    ins.then_inc(S["qk_proj"], 1)
                for s in range(2):
                    for c in range(2):
                        ins = pe.matmul(bk(3 * hf + 2)[64 * s:64 * s + 64, :], wk[:, 2 * s + c, :],
                                        src(2 * s + c)[:, ts], start=(c == 0), stop=(c == 1))
                ins.then_inc(S["qk_proj"], 1)
            for u in range(2):
                for b in range(4 * u, 4 * u + 4):
                    for s in range(2):
                        for c in range(2):
                            ins = pe.matmul(bk(6 + u)[:, P * (b % 4) + 64 * s:P * (b % 4) + 64 * s + 64],
                                            src(2 * s + c)[:, P * b:P * (b + 1)], wv[:, 2 * s + c, :],
                                            start=(c == 0), stop=(c == 1))
                ins.then_inc(S["v_proj"], 1)

            pe.wait_ge(S["late_in"], 48)
            pe.wait_ge(S["const_rows"], 64)
            pe.wait_ge(S["qk_copied"], 6)
            pe.wait_ge(S["v_copied"], 2 * B)

            def scores_q(b, p, u, first=False):
                if not (first and u < 2):
                    pe.wait_ge(S["s_reduced"], 16 * b + u - 1)
                o = bk(u % 2)
                pe.matmul(o, identb[:, :], masks[:, 0, :], start=True, stop=True)
                for h in (2 * u, 2 * u + 1):
                    ins = pe.matmul(o[:, 256 * (h % 2):256 * (h % 2) + 256],
                                    q_stack[p][0:NS, P * h:P * (h + 1)],
                                    k_stack[p][0:NS, h // HG].rearrange("p s t -> p (s t)"),
                                    start=False, stop=True, skip_group_check=True)
                ins.then_inc(S["s_done"], 1)

            def turn_max(b, p, first=False):
                pe.wait_ge(S["s_reduced"], 16 * b + 16)
                if not first:
                    pe.wait_ge(S["x_added"], b - 1)
                    pe.wait_ge(S["mneg_done"], b)
                pe.transpose(bk(3)[0:H0, 0:P], mx[:, p, :], identf[:, :]).then_inc(S["mT_done"], 1)

            def scores_k(b, p, g, first=False):
                if not (first and g < 2):
                    pe.wait_ge(S["exp_done"], 8 * b + g - 1)
                for s in range(2):
                    pe.matmul(st_ps[g % 2][:, s, :], identb[:, :], masks[:, 1 + s, :], start=True, stop=False)
                    ins = pe.matmul(st_ps[g % 2][:, s, :], k_stack[p][0:NQ, g, s, :],
                                    q_stack[p][0:NQ, 512 * g:512 * (g + 1)], start=False, stop=True)
                ins.then_inc(S["st_done"], 1)

            def values(b, p, g, first=False):
                pe.wait_ge(S["exp_done"], 8 * b + g + 1)
                if g == 0:
                    pe.wait_ge(S["v_ready"], b + 1)
                    if not first:
                        pe.wait_ge(S["onorm_done"], b)
                W = HD + 1
                for q in range(HG):
                    h = HG * g + q
                    for s in range(2):
                        ins = pe.matmul(bk(2)[:, W * h:W * h + W], p_buf[g % 2][:, 512 * s + P * q:512 * s + P * q + P],
                                        v_buf[:, p, s, g, :], start=(s == 0), stop=(s == 1))
                ins.then_inc(S["pv_done"], 1)

            def turn_o(b):
                pe.wait_ge(S["onorm_done"], b + 1)
                pe.wait_ge(S["mneg_done"], b + 2 if not (isinstance(b, int) and b == B - 1) else B)
                for c in range(KD):
                    ins = pe.transpose(bk(3)[:, P * c:P * (c + 1)],
                                       onorm[:, 16 * c:16 * c + 16, :].rearrange("p h d -> p (h d)"), identf[:, :])
                ins.then_inc(S["oT_done"], 1)

            def project_o(b):
                pe.wait_ge(S["oT_copied"], b + 1)
                for c in range(KD):
                    ins = pe.matmul(bk(3)[:, 256:512], oTs[:, c, :], wo[:, c, :], start=(c == 0), stop=(c == 1))
                ins.then_inc(S["wo_done"], 1)

            UNITS = [3, 3, 3, 3, 2, 2, 0, 0]

            def body(b, j, p, first=False, last=False):
                jn = j + (1 if p == 1 else 0)
                u = 0
                for g in range(G0):
                    if not last:
                        if g == 0:
                            pe.wait_ge(stack_in[1 - p][0], STACKED * (jn + 1))
                        for _ in range(UNITS[g]):
                            if u == 8:
                                pe.wait_ge(stack_in[1 - p][1], STACKED * (jn + 1))
                            scores_q(b + 1, 1 - p, u)
                            u += 1
                    if g == 0:
                        pe.wait_ge(m_in[p], 48 * (j + 1))
                    scores_k(b, p, g, first)
                    if g > 0:
                        values(b, p, g - 1, first)
                    elif not first:
                        values(b - 1, 1 - p, G0 - 1)
                    if g == 2 and not first:
                        turn_o(b - 1)
                    if g == 3 and not first:
                        project_o(b - 1)
                    if g == 6 and not last:
                        turn_max(b + 1, 1 - p, first=first and 0)

            pe.wait_ge(stack_in[0][0], STACKED)
            pe.wait_ge(stack_in[0][1], STACKED)
            for u in range(16):
                scores_q(0, 0, u, first=True)
            turn_max(0, 0, first=True)
            body(0, 0, 0, first=True)
            with pe.Fori(0, 3) as i:
                body(1 + 2 * i, i, 1)
                body(2 + 2 * i, i + 1, 0)
            body(7, 3, 1, last=True)
            values(7, 1, 7)
            turn_o(7)
            project_o(7)
            turn_rows(pe, 1)
            moe_tensor(pe, 0)
            turn_rows(pe, 2)

            def convolve(h, j, p, first=False):
                pe.wait_ge(S["toep_fixed"], h + 1)
                pe.wait_ge(S["kv_done"], 2 * h + 2)
                if not first:
                    pe.wait_ge(S["conv_used"], 2 * h - 2)
                pe.matmul(bk(2 * p), toep[p][:, 0:P], kv[p][:, 0, :], start=True, stop=True
                          ).then_inc(S["conv_done"], 1)
                pe.matmul(bk(2 * p + 1), toep[p][:, P:2 * P], kv[p][:, 0, :], start=True, stop=False)
                pe.matmul(bk(2 * p + 1), toep[p][:, 0:P], kv[p][:, 1, :], start=False, stop=True
                          ).then_inc(S["conv_done"], 1)

            convolve(0, 0, 0, True)
            convolve(1, 0, 1, True)
            with pe.Fori(1, HC // 2) as i:
                convolve(2 * i, i, 0)
                convolve(2 * i + 1, i, 1)
            pe.wait_ge(S["convT_done"], 2 * HC)
            for b in range(B):
                if b >= 2:
                    pe.wait_ge(S["back_added"], b - 1)
                for c in range(2):
                    ins = pe.transpose(bk(4 + b % 2)[:, P * c:P * (c + 1)], convT[:, c, b, :], identf[:, :])
                ins.then_inc(S["back_done"], 1)
            turn_rows(pe, 3)
            moe_tensor(pe, 1)


def constants():
    bf = np.dtype("bfloat16")
    c = {}
    c["identf"] = np.eye(P, dtype=np.float32)
    c["identb"] = np.eye(P).astype(bf)
    c["anti"] = np.ascontiguousarray(np.eye(P, dtype=np.float32)[::-1])
    q, k = np.arange(P)[:, None], np.arange(P)[None, :]
    ssm = np.where((q - k >= 0) & (q - k < WIN_SSM), 0.0, NEG)
    att = np.where((q - k >= 0) & (q - k < WIN_ATT), 0.0, NEG)
    c["masks"] = np.stack([np.concatenate([ssm, att, ssm, att], 1), np.tile(ssm.T, (1, 4)),
                           np.tile(att.T, (1, 4))], 1).astype(bf)
    c["tri"] = (np.arange(P)[:, None] < np.arange(P)[None, :]).astype(bf)
    c["iota"] = np.tile(np.arange(32, dtype=np.float32), (P, 1))
    slopes = np.power(np.float32(2.0), -8.0 * np.arange(H0, dtype=np.float32) / H0).astype(np.float32)
    parts, left = [], slopes.copy()
    for _ in range(3):
        parts.append(left.astype(bf))
        left = left - parts[-1].astype(np.float32)
    c["slope_rows"] = np.stack([np.repeat(s, P) for s in parts]).astype(bf)
    pos = np.arange(P) - P // 2
    c["key_rows"] = np.concatenate([np.tile(pos, (3, G0, 2, 1)), np.ones((3, G0, 2, P))]).astype(bf)
    return c


def layouts(i):
    f = {k: np.asarray(v) for k, v in i.items()}
    ctx = f["ctx_2048"]
    w = {"x": f["x"]}

    def chunked(m, rows=P):
        return m.reshape(-1, rows, m.shape[-1]).transpose(1, 0, 2)

    w["ctx_d"] = ctx.reshape(T, KD, P).transpose(2, 1, 0)
    w["ctx_l"] = ctx.reshape(B, P, 2, P)[:, :, :, ::-1].transpose(3, 2, 0, 1)
    w["wq"] = chunked(f["L0_xattn_Wq"])
    w["wk"] = np.concatenate([chunked(f["L0_xattn_Wsk"]), chunked(f["L0_xattn_Wk"])], 1)
    w["wv"] = np.concatenate([chunked(f["L0_xattn_Wsv"]), chunked(f["L0_xattn_Wv"])], 1)
    w["wo"] = chunked(f["L0_xattn_Wo"])
    w["router"] = chunked(f["L0_ffn_router_w"])
    w1 = f["L0_ffn_W1"].reshape(16, 2, P, 512).transpose(2, 0, 1, 3).reshape(P, 16, 1024)
    w2 = f["L0_ffn_W2"].reshape(16, 4, P, D).transpose(2, 0, 1, 3).reshape(P, 16, 1024)
    w["w_moe0"] = np.concatenate([w1, w2], 2)
    w["kpad"] = np.pad(f["L1_xattn_ssm_kernel"], ((0, 0), (P - 1, 0)))
    w["D"] = f["L1_xattn_D"]
    w["gate_w"] = chunked(f["L1_ffn_gate_w"])
    gu = np.concatenate([f["L1_ffn_w_gate"], f["L1_ffn_w_up"]], 2)
    gu = gu.reshape(8, 2, P, 352).transpose(2, 0, 1, 3).reshape(P, 8, 704)
    dn = np.pad(f["L1_ffn_w_down"], ((0, 0), (0, 2 * P - 176), (0, 0)))
    dn = dn.reshape(8, 2, P, D).transpose(2, 0, 1, 3).reshape(P, 8, 512)
    w["w_moe1"] = np.concatenate([gu, dn], 2)
    w["sgu"] = chunked(np.concatenate([f["L1_ffn_sw_gate"], f["L1_ffn_sw_up"]], 1))
    w["sdn"] = chunked(np.pad(f["L1_ffn_sw_down"], ((0, 3 * P - 352), (0, 0))))
    w.update(constants())
    return {k: np.ascontiguousarray(v) for k, v in w.items()}


def kernel(**inputs):
    import concourse.bacc as bacc
    from concourse.bass_utils import run_bass_kernel_spmd

    arrays = layouts(inputs)
    nc = bacc.Bacc("TRN2", target_bir_lowering=False, num_devices=1)
    aps = {k: nc.dram_tensor(f"in_{k}", v.shape, mybir.dt.from_np(v.dtype), kind="ExternalInput").ap()
           for k, v in arrays.items()}
    out = nc.dram_tensor("out", (B, P, D), F32, kind="ExternalOutput").ap()
    build(nc, aps, out)
    r = run_bass_kernel_spmd(nc, [{f"in_{k}": v for k, v in arrays.items()}], core_ids=[0])
    return r.results[0]["out"]
```

```python
from contextlib import ExitStack

import numpy as np

import concourse.bass as bass
from concourse import mybir

F32 = mybir.dt.float32
BF16 = mybir.dt.bfloat16
I32 = mybir.dt.int32
U32 = mybir.dt.uint32
ALU = mybir.AluOpType
ACT = mybir.ActivationFunctionType
AX = mybir.AxisListType

P = 128
B = 8
D = 256
KD = D // P
T = B * P

H0 = 32
G0 = 8
HG = H0 // G0
HD = 8
SLOPE, NS, NQ = 48, 96, 99
WIN_SSM, WIN_ATT = 64, 32
SCALE = 1.0 / float(np.sqrt(HD))
NEG = -1e30
VC = 32

HC = 16
CW = 8
NPAIR = B * CW * CW

EPS = 1e-5
BUFS = 3
LATE = 9
HALF = T // 2


def slots_of(experts, ffn, chunk_rows, tiles):
    return dict(E=experts, F=ffn, rows=chunk_rows, tiles=tiles)


MOE = [
    dict(E=16, W=512, rows=[128, 128, 128, 128], tiles=2 * T // P + 15, wide=2048),
    dict(E=8, W=352, rows=[128, 48], tiles=2 * T // P + 7, wide=1216),
]
XS_ROWS = MOE[0]["tiles"] * P


def build(nc, a, out):
    with ExitStack() as ctx:
        def sb(name, shape, dt=F32):
            return ctx.enter_context(nc.sbuf_tensor(name, shape, dt))

        def sem(name):
            return ctx.enter_context(nc.semaphore(name))

        bank = [ctx.enter_context(nc.psum_tensor(f"bank{i}", [P, 512], F32)) for i in range(4)]
        st_ps = [ctx.enter_context(nc.psum_tensor(f"st_ps{i}", [P, 2, 512], F32)) for i in range(2)]
        banks = [bank[0], bank[1], bank[2], bank[3], st_ps[0][:, 0, :], st_ps[0][:, 1, :],
                 st_ps[1][:, 0, :], st_ps[1][:, 1, :]]

        def bk(i):
            return banks[i][:, :] if i < 4 else banks[i]

        qd = nc.dram_tensor("q_parts_by_row", [3, HD, H0, T], BF16, kind="Internal").ap()
        kd = nc.dram_tensor("k_parts_by_row", [6, HD, G0, 2, T], BF16, kind="Internal").ap()
        xs = nc.dram_tensor("rows_by_slot", [XS_ROWS, D], F32, kind="Internal").ap()
        ys = nc.dram_tensor("results_by_slot", [XS_ROWS, D], F32, kind="Internal").ap()

        wall = sb("wall", [P, 16 * 2048])
        x_sb = sb("x_sb", [P, B, D])
        h_sb = sb("h_sb", [P, B, D])
        hT = sb("hT", [P, KD, T])
        cT = sb("cT", [P, KD, T])
        parts = sb("parts", [P, 4608])
        q_parts = parts[:, 0:3072].bitcast(BF16).rearrange("p (j c t) -> p j c t", j=3, c=2)
        k_parts = parts[:, 3072:4608].bitcast(BF16).rearrange("p (j t) -> p j t", j=3)
        v_all = sb("v_all", [P, B, 2, G0, HD])
        v_buf = sb("v_buf", [P, BUFS, 2, G0, VC])
        wq = sb("wq", [P, 4, D])
        wk = sb("wk", [P, 4, 64])
        wv = sb("wv", [P, 4, 64])
        wo = sb("wo", [P, KD, D])
        masks = sb("masks", [P, 3, 512], BF16)
        identf = sb("identf", [P, P])
        identb = sb("identb", [P, P], BF16)
        anti = sb("anti", [P, P])
        tri = sb("tri", [P, P], BF16)
        onesb = sb("onesb", [P, P], BF16)
        iota = sb("iota", [P, 32])
        stats = sb("stats", [P, B, 6])
        mv = sb("mv", [P, B, 2])
        vare = sb("vare", [P, B])
        rstd = sb("rstd", [P, B])
        neghalf = sb("neghalf", [P, B])
        mx = sb("mx", [P, BUFS, H0])
        c_flat = cT[:, :, :].rearrange("p c t -> p (c t)")
        mneg = c_flat[0:H0, 0:P]
        mres = c_flat[0:H0, P:2 * P]
        half_T = c_flat[:, 256:768]
        onorm = c_flat[:, 768:1024].rearrange("p (h d) -> p h d", h=H0)
        oTs = c_flat[:, 1024:1280].rearrange("p (c t) -> p c t", c=KD)
        msplit = sb("msplit", [H0, BUFS, 3, P], BF16)
        rden = sb("rden", [P, H0])

        att = LATE * 2048
        q_stack = [wall[:, att + 2048 * i: att + 2048 * (i + 1)].bitcast(BF16) for i in range(BUFS)]
        at_k = att + 2048 * BUFS
        k_stack = [wall[:, at_k + 1024 * i: at_k + 1024 * (i + 1)].bitcast(BF16)
                   .rearrange("p (g s t) -> p g s t", g=G0, s=2) for i in range(BUFS)]
        at_p = at_k + 1024 * BUFS
        p_buf = ([h_sb[:, 4 * i:4 * i + 4, :].rearrange("p b d -> p (b d)") for i in range(2)]
                 + [hT[:, i, :] for i in range(2)]
                 + [wall[:, at_p + 1024 * i: at_p + 1024 * (i + 1)] for i in range(4)])
        pf = [p_buf[4 + i][:, 0:512] for i in range(2)]
        pr = [p_buf[4 + i][:, 512:1024] for i in range(2)]

        at = [0]

        def carve(n):
            at[0] += n
            assert at[0] <= 4608, at[0]
            return parts[:, at[0] - n: at[0]]

        xt = [carve(D) for _ in range(2)]
        xTs = [carve(D) for _ in range(2)]
        act_h = [carve(512) for _ in range(2)]
        hTs = [carve(512) for _ in range(2)]
        y_sb = [carve(D) for _ in range(2)]
        gs = [carve(176) for _ in range(2)]
        logits = sb("logits", [P, B, 16])
        top = sb("top", [P, B, 8])
        topi = sb("topi", [P, B, 8], U32)
        idxf = sb("idxf", [P, 2, B])
        hot = carve(2 * B * 16).rearrange("p (k b e) -> p k b e", k=2, b=B)
        hotb = sb("hotb", [P, B, 16], BF16)
        pw = sb("pw", [P, 2, B])
        ptmp = sb("ptmp", [P, 4, B])
        cmp = parts[:, 0:31 * 16]
        cnt = sb("cnt", [P, 4, 16])
        base = carve(B * 16).rearrange("p (b e) -> p b e", b=B)
        slotf = sb("slotf", [P, 2, B])
        slot = sb("slot", [P, 2, B], U32)
        etf = sb("etf", [P, 32])
        et = sb("et", [P, 32], I32)
        router = sb("router", [P, KD, 16])
        router1 = sb("router1", [P, KD, 8])
        y_in = [parts[:, D * i: D * (i + 1)] for i in range(8)]

        w1_ = 0
        moe_w = [wall[:, :].rearrange("p (e n) -> p e n", e=16),
                 wall[:, 0:8 * 1216].rearrange("p (e n) -> p e n", e=8)]
        at1 = 8 * 1216
        sgu = wall[:, at1: at1 + 1408].rearrange("p (c n) -> p c n", c=2)
        sdn = wall[:, at1 + 1408: at1 + 2176].rearrange("p (c n) -> p c n", c=3)
        at1 += 2176
        ctx_l = wall[:, at1: at1 + 2048].rearrange("p (c b n) -> p c b n", c=2, b=B)
        kv = [wall[:, at1 + 2048 + 1024 * i: at1 + 3072 + 1024 * i].rearrange("p (c n) -> p c n", c=2)
              for i in range(2)]
        toep = [wall[:, at1 + 4096 + 256 * i: at1 + 4352 + 256 * i] for i in range(2)]
        prod = [wall[:, at1 + 4608 + 512 * i: at1 + 5120 + 512 * i] for i in range(2)]
        convT = wall[:, at1 + 5632: at1 + 7680].rearrange("p (c b n) -> p c b n", c=2, b=B)
        at1 += 7680
        sh_g = [wall[:, at1 + 352 * i: at1 + 352 * (i + 1)] for i in range(2)]
        sh_h = [wall[:, at1 + 704 + 352 * i: at1 + 704 + 352 * (i + 1)] for i in range(2)]
        sh_T = [wall[:, at1 + 1408 + 384 * i: at1 + 1408 + 384 * (i + 1)] for i in range(2)]
        d_bc = sb("d_bc", [P, HC])

        names = ("x_in const_in ctx_in proj_in late_in wo_in zero_out stack_zero neg_set stats_done var_done rstd_done "
                 "h_done tr_done tr_copied qk_proj qk_copied qk_split v_proj v_copied half_copied half_turned "
                 "s_done s_reduced mT_done mneg_done m_split st_done exp_done pv_done v_ready norm_done "
                 "oT_done oT_copied wo_done x_added const_rows dve_chain pool_chain act_chain "
                 "lay1_in ctxl_in kv_done conv_done conv_used toep_fixed convT_done back_done back_added "
                 "x_final out_done sh_up sh_sil sh_act sh_tr sh_trc sh_dn sh_dn_used").split()
        S = {n: sem(n) for n in names}
        stack_in = [sem(f"stack_in_{p}") for p in range(BUFS)]
        parts_out = [sem(f"parts_out_{h}") for h in range(2)]
        m_in = [sem(f"m_in_{p}") for p in range(BUFS)]
        expert_in = sem("expert_in")
        toep_in = [sem(f"toep_in_{p}") for p in range(2)]
        M = []
        for L in range(2):
            mn = ("logit_done logit_copied top_done prob_exp hot_done rank_done cnt_done slot_done scattered "
                  "xT_done xT_copied w1_done sil_done act_done hT_done hT_copied w2_done y_done combined").split()
            m = {n: sem(f"moe{L}_{n}") for n in mn}
            m["xin"] = [sem(f"moe{L}_xin{p}") for p in range(2)]
            m["stored"] = [sem(f"moe{L}_stored{p}") for p in range(2)]
            m["gathered"] = [sem(f"moe{L}_gathered{p}") for p in range(4)]
            M.append(m)

        block = ctx.enter_context(nc.Block())

        class Chain:

            def __init__(self, eng, s):
                self.eng, self.s, self.n, self.dyn = eng, s, 0, 0

            def link(self, ins):
                self.n += 1
                ins.then_inc(self.s, 1)
                self.eng.wait_ge(self.s, self.dyn + self.n)

        def stack_load(sp, b, p, wait=True):
            if wait:
                sp.wait_ge(S["s_done"], 16 * b - 15)
            ts = slice(P * b, P * b + P) if isinstance(b, int) else bass.ds(b * P, P)
            sp.dma_start(k_stack[p][0:6 * HD].rearrange("p g s t -> p (g s) t"),
                         kd[:, :, :, :, ts].rearrange("r d g s t -> (r d) (g s) t")).then_inc(stack_in[p], 16)
            for r0, n in ((0, 3), (24, 2), (40, 1)):
                sp.dma_start(q_stack[p][r0:r0 + HD * n, :].rearrange("p (h t) -> p h t", h=H0),
                             qd[0:n, :, :, ts].rearrange("j d h t -> (j d) h t")).then_inc(stack_in[p], 16)

        STACKED = 16 * 4

        def moe_loads(sp, L):
            m = M[L]
            sp.wait_ge(m["scattered"], 16 * 2 * B)

            def load(t, j, p, first=False):
                if not first:
                    sp.wait_ge(m["xT_done"], t - 1)
                src = xs[bass.ds(t * P, P), :] if not isinstance(t, int) else xs[t * P:(t + 1) * P, :]
                sp.dma_start(xt[p], src).then_inc(m["xin"][p], 16)

            n = MOE[L]["tiles"]
            load(0, 0, 0, True)
            load(1, 0, 1, True)
            with sp.Fori(1, (n - 1) // 2) as i:
                load(2 * i, i, 0)
                load(2 * i + 1, i, 1)
            load(n - 1, n // 2, 0)

        @block.sync
        def _(sp):
            for b in range(B):
                sp.dma_start(x_sb[:, b, :], a["x"][b]).then_inc(S["x_in"], 16)
            sp.dma_start(identf[:, :], a["identf"]).then_inc(S["const_in"], 16)
            sp.dma_start(cT[:, :, :], a["ctx_d"]).then_inc(S["ctx_in"], 16)
            sp.dma_start(wq[:, :, :], a["wq"]).then_inc(S["proj_in"], 16)
            sp.dma_start(wk[:, :, :], a["wk"]).then_inc(S["proj_in"], 16)
            sp.dma_start(wv[:, :, :], a["wv"]).then_inc(S["proj_in"], 16)
            sp.dma_start(wo[:, :, :], a["wo"]).then_inc(S["late_in"], 16)
            sp.dma_start(masks[:, :, :], a["masks"]).then_inc(S["late_in"], 16)
            sp.dma_start(identb[:, :], a["identb"]).then_inc(S["late_in"], 16)
            sp.wait_ge(S["stack_zero"], 2)
            sp.wait_ge(S["zero_out"], 16)
            for p in range(BUFS):
                sp.dma_start(q_stack[p][SLOPE:SLOPE + 3, :], a["slope_rows"]).then_inc(S["const_rows"], 16)
                sp.dma_start(k_stack[p][SLOPE:SLOPE + 3], a["key_rows"][0:3]).then_inc(S["const_rows"], 16)
                sp.dma_start(k_stack[p][NS:NQ], a["key_rows"][3:6]).then_inc(S["const_rows"], 16)
            for u in range(6):
                hf, m = divmod(u, 3)
                ts = slice(HALF * hf, HALF * (hf + 1))
                sp.wait_ge(S["qk_split"], u + 1)
                if m < 2:
                    for j in range(3):
                        sp.dma_start(qd[j, :, 16 * m:16 * m + 16, ts].rearrange("d h t -> h d t"),
                                     q_parts[:, j, m, ts]).then_inc(parts_out[hf], 16)
                else:
                    for r, j in enumerate((0, 0, 0, 1, 1, 2)):
                        for c in range(2):
                            sp.dma_start(kd[r, :, :, c, ts].rearrange("d g t -> g d t"),
                                         k_parts[64 * c:64 * c + 64, j, ts]).then_inc(parts_out[hf], 16)
                if u == 2:
                    sp.wait_ge(parts_out[0], 18 * 16)
                    stack_load(sp, 0, 0, wait=False)
                    stack_load(sp, 1, 1, wait=False)
            sp.wait_ge(parts_out[1], 18 * 16)

            def experts(e, n):
                es = slice(e, e + n) if isinstance(e, int) else bass.ds(e, n)
                sp.dma_start(moe_w[0][:, es, :], a["w_moe0"][:, es, :]).then_inc(expert_in, 16)

            experts(0, 3)
            with sp.Fori(0, 2) as i:
                stack_load(sp, 2 + BUFS * i, 2)
                stack_load(sp, 3 + BUFS * i, 0)
                experts(3 * i + 3, 3)
                stack_load(sp, 4 + BUFS * i, 1)
            sp.wait_ge(S["pv_done"], 2 * B)
            experts(9, 4)
            experts(13, 3)
            sp.dma_start(router[:, :, :], a["router"]).then_inc(S["late_in"], 16)
            sp.dma_start(router1[:, :, :], a["gate_w"]).then_inc(S["late_in"], 16)
            moe_loads(sp, 0)
            sp.wait_ge(M[0]["w2_done"], MOE[0]["tiles"])
            sp.dma_start(ctx_l, a["ctx_l"]).then_inc(S["ctxl_in"], 16)
            sp.dma_start(d_bc[:, :], a["D"].partition_broadcast(P)).then_inc(S["ctxl_in"], 16)

            def toep_load(h, j, p, first=False):
                if not first:
                    sp.wait_ge(S["conv_done"], 2 * (h - 1))
                kp = a["kpad"]
                sp.dma_start(toep[p], bass.AP(tensor=kp.tensor, offset=h * 383, ap=[[1, P], [1, 2 * P]])
                             ).then_inc(toep_in[p], 16)

            toep_load(0, 0, 0, True)
            toep_load(1, 0, 1, True)
            sp.dma_start(moe_w[1], a["w_moe1"]).then_inc(S["lay1_in"], 16)
            sp.dma_start(sgu, a["sgu"]).then_inc(S["lay1_in"], 16)
            sp.dma_start(sdn, a["sdn"]).then_inc(S["lay1_in"], 16)
            with sp.Fori(1, HC // 2) as i:
                toep_load(2 * i, i, 0)
                toep_load(2 * i + 1, i, 1)
            moe_loads(sp, 1)
            for b in range(B):
                sp.wait_ge(S["x_final"], b + 1)
                sp.dma_start(out[b], x_sb[:, b, :]).then_inc(S["out_done"], 16)
            sp.wait_ge(S["out_done"], 16 * B)

        def pow_rstd(pool, n):
            if n == 0:
                pool.wait_ge(S["neg_set"], 1)
            pool.wait_ge(S["var_done"], n + 1)
            pool.tensor_tensor(rstd[:, :], vare[:, :], neghalf[:, :], ALU.pow).then_inc(S["rstd_done"], 1)

        def moe_pool(pool, L):
            m = M[L]
            if L == 0:
                pool.wait_ge(S["zero_out"], 16)
            pool.wait_ge(m["slot_done"], 1)
            for k in range(2):
                for b in range(B):
                    pool.indirect_dma_start(xs[:, :], bass.IndirectOffsetOnAxis(slot[:, k, b:b + 1], 0),
                                            h_sb[:, b, :], None).then_inc(m["scattered"], 16)

            def store(t, p):
                pool.wait_ge(m["y_done"], t + 1)
                dst = ys[bass.ds(t * P, P), :] if not isinstance(t, int) else ys[t * P:(t + 1) * P, :]
                pool.dma_start(dst, y_sb[p]).then_inc(m["stored"][p], 16)

            n = MOE[L]["tiles"]
            with pool.Fori(0, (n - 1) // 2) as i:
                store(2 * i, 0)
                store(2 * i + 1, 1)
            store(n - 1, 0)
            pool.wait_ge(m["stored"][0], 16 * ((n + 1) // 2))
            pool.wait_ge(m["stored"][1], 16 * (n // 2))
            for b in range(B):
                if b >= 4:
                    pool.wait_ge(m["combined"], b - 3)
                for k in range(2):
                    pool.indirect_dma_start(y_in[2 * (b % 4) + k], None, ys[:, :],
                                            bass.IndirectOffsetOnAxis(slot[:, k, b:b + 1], 0)
                                            ).then_inc(m["gathered"][b % 4], 16)

        @block.gpsimd
        def _(pool):
            pool.memset(neghalf[:, :], -0.5).then_inc(S["neg_set"], 1)
            pool.memset(onesb[:, :], 1.0).then_inc(S["neg_set"], 1)
            pool.memset(v_buf[:, :, :, :, HD + 1:VC], 0.0).then_inc(S["neg_set"], 1)
            pool.memset(v_buf[:, :, :, :, HD:HD + 1], 1.0).then_inc(S["neg_set"], 1)
            pool.memset(wall[:, att:at_k], 0.0).then_inc(S["stack_zero"], 1)
            pool.memset(wall[:, at_k:at_p], 0.0).then_inc(S["stack_zero"], 1)
            pool.dma_start(tri[:, :], a["tri"]).then_inc(S["wo_in"], 16)
            pool.dma_start(anti[:, :], a["anti"]).then_inc(S["wo_in"], 16)
            pool.dma_start(iota[:, :], a["iota"]).then_inc(S["wo_in"], 16)
            pool.wait_ge(S["stack_zero"], 1)
            pool.dma_start(xs.rearrange("(n p) d -> p n d", p=P),
                           bass.AP(tensor=wall, offset=att, ap=[[16 * 2048, P], [0, XS_ROWS // P], [1, D]])
                           ).then_inc(S["zero_out"], 16)
            pow_rstd(pool, 0)
            pool.wait_ge(S["neg_set"], 4)

            def v_copy(b, p, first=False):
                if not first:
                    pool.wait_ge(S["pv_done"], 2 * b - 3)
                src = v_all[:, b] if isinstance(b, int) else v_all[:, bass.ds(b, 1)].rearrange("p o s g d -> p (o s) g d")
                pool.tensor_copy(v_buf[:, p, :, :, 0:HD], src).then_inc(S["v_ready"], 1)

            pool.wait_ge(S["v_copied"], 2 * B)
            v_copy(0, 0, True)
            v_copy(1, 1, True)
            with pool.Fori(0, 2) as i:
                for o in (2, 3, 4):
                    v_copy(o + BUFS * i, o % BUFS)
            pow_rstd(pool, 1)
            moe_pool(pool, 0)
            pow_rstd(pool, 2)
            pool.wait_ge(S["ctxl_in"], 32)

            def products(h, p, first=False):
                if not first:
                    pool.wait_ge(S["conv_done"], 2 * (h - 1))
                cols = slice(CW * h, CW * h + CW) if isinstance(h, int) else bass.ds(h * CW, CW)
                for c in range(2):
                    k = ctx_l[:, c, :, cols]
                    pool.tensor_tensor(kv[p][:, c, :].rearrange("p (b i j) -> p b i j", b=B, i=CW),
                                       k.unsqueeze(3).to_broadcast([P, B, CW, CW]),
                                       k.unsqueeze(2).to_broadcast([P, B, CW, CW]),
                                       ALU.mult).then_inc(S["kv_done"], 1)

            products(0, 0, True)
            products(1, 1, True)
            with pool.Fori(1, HC // 2) as i:
                products(2 * i, 0)
                products(2 * i + 1, 1)
            pow_rstd(pool, 3)
            moe_pool(pool, 1)

        UNITS = [4, 4, 4, 4, 0, 0, 0, 0]

        def norm_rows(dve, n):
            for b in range(B):
                dve.bn_stats(stats[:, b, :], x_sb[:, b, :]).then_inc(S["stats_done"], 1)
            dve.wait_ge(S["stats_done"], n * (2 * B) + B)
            for b in range(B):
                dve.bn_aggr(mv[:, b, :], stats[:, b, :]).then_inc(S["stats_done"], 1)
            dve.wait_ge(S["stats_done"], (n + 1) * (2 * B))
            dve.tensor_scalar(vare[:, :], mv[:, :, 1], EPS, None, ALU.add).then_inc(S["var_done"], 1)
            dve.wait_ge(S["rstd_done"], n + 1)
            if n == 3:
                dve.wait_ge(M[0]["scattered"], 16 * 2 * B)
            for b in range(B):
                dve.tensor_scalar(h_sb[:, b, :], x_sb[:, b, :], mv[:, b, 0:1], rstd[:, b:b + 1],
                                  ALU.subtract, ALU.mult).then_inc(S["h_done"], 1)

        def moe_vector(dve, chain, L):
            m, E, n = M[L], MOE[L]["E"], MOE[L]["tiles"]
            lg, ho, hb, ba = logits[:, :, 0:E], hot[:, :, :, 0:E], hotb[:, :, 0:E], base[:, :, 0:E]

            def over_e(ap):
                return ap.unsqueeze(2).to_broadcast([P, B, E])

            dve.wait_ge(S["wo_in"], 48)
            dve.wait_ge(m["logit_done"], 1)
            src = bk(0)[:, 0:B * E].rearrange("p (b e) -> p b e", b=B)
            if L == 0:
                chain.link(dve.tensor_copy(lg, src))
            else:
                chain.link(dve.tensor_reduce(ptmp[:, 0, :], src, AX.X, ALU.max))
                chain.link(dve.tensor_tensor(ba, src, over_e(ptmp[:, 0, :]), ALU.subtract))
                dve.tensor_copy(ptmp[:, 1, :], ptmp[:, 0, :]).then_inc(m["logit_copied"], 1)
                dve.wait_ge(m["prob_exp"], 1)
                chain.link(dve.tensor_reduce(ptmp[:, 2, :], lg, AX.X, ALU.add))
                chain.link(dve.reciprocal(ptmp[:, 3, :], ptmp[:, 2, :]))
                chain.link(dve.tensor_tensor(lg, lg, over_e(ptmp[:, 3, :]), ALU.mult))
            for b in range(B):
                dve.max(top[:, b, :], logits[:, b, 0:E]).then_inc(m["top_done"], 1)
            dve.wait_ge(m["top_done"], B)
            for b in range(B):
                dve.max_index(topi[:, b, :], top[:, b, :], logits[:, b, 0:E]).then_inc(m["top_done"], 1)
            dve.wait_ge(m["top_done"], 2 * B)
            if L == 0:
                dve.tensor_tensor(ptmp[:, 0, :], top[:, :, 1], top[:, :, 0], ALU.subtract
                                  ).then_inc(m["logit_copied"], 1)
            else:
                chain.link(dve.tensor_copy(pw[:, 0, :], top[:, :, 0]))
                chain.link(dve.tensor_copy(pw[:, 1, :], top[:, :, 1]))
            for k in range(2):
                chain.link(dve.tensor_copy(idxf[:, k, :], topi[:, :, k]))
                chain.link(dve.tensor_tensor(ho[:, k], iota[:, 0:E].unsqueeze(1).to_broadcast([P, B, E]),
                                             over_e(idxf[:, k, :]), ALU.is_equal))
            dve.tensor_tensor(hb, ho[:, 0], ho[:, 1], ALU.add).then_inc(m["hot_done"], 1)
            if L == 0:
                dve.wait_ge(m["prob_exp"], 1)
                chain.link(dve.tensor_scalar(ptmp[:, 2, :], ptmp[:, 1, :], 1.0, None, ALU.add))
                chain.link(dve.reciprocal(pw[:, 0, :], ptmp[:, 2, :]))
                chain.link(dve.tensor_tensor(pw[:, 1, :], ptmp[:, 1, :], pw[:, 0, :], ALU.mult))
            nst = T // P
            dve.wait_ge(m["cnt_done"], 1)
            chain.link(dve.tensor_copy(cnt[:, 0, 0:E], bk(2)[:, 0:E]))
            c3 = cmp[:, 0:E * nst].rearrange("p (e s) -> p e s", e=E)
            chain.link(dve.tensor_scalar(cnt[:, 1, 0:nst], iota[:, 0:nst], float(P), None, ALU.mult))
            chain.link(dve.tensor_tensor(c3, cnt[:, 0, 0:E].unsqueeze(2).to_broadcast([P, E, nst]),
                                         cnt[:, 1, 0:nst].unsqueeze(1).to_broadcast([P, E, nst]), ALU.is_gt))
            chain.link(dve.tensor_reduce(cnt[:, 2, 0:E], c3, AX.X, ALU.add))
            chain.link(dve.tensor_tensor_scan(cnt[:, 3, 0:E], cnt[:, 2, 0:E], cnt[:, 2, 0:E], 0.0,
                                              ALU.add, ALU.bypass))
            chain.link(dve.tensor_tensor(cnt[:, 2, 0:E], cnt[:, 3, 0:E], cnt[:, 2, 0:E], ALU.subtract))
            chain.link(dve.tensor_scalar(cnt[:, 2, 0:E], cnt[:, 2, 0:E], float(P), None, ALU.mult))
            dve.wait_ge(m["rank_done"], 1)
            rank = bk(1)[:, 0:B * E].rearrange("p (b e) -> p b e", b=B)
            chain.link(dve.tensor_tensor(ba, rank, cnt[:, 2, 0:E].unsqueeze(1).to_broadcast([P, B, E]), ALU.add))
            for k in range(2):
                chain.link(dve.tensor_tensor(ho[:, k], ho[:, k], ba, ALU.mult))
                chain.link(dve.tensor_reduce(slotf[:, k, :], ho[:, k], AX.X, ALU.add))
            if L == 1:
                dve.wait_ge(M[0]["gathered"][3], 64)
            chain.link(dve.tensor_copy(slot[:, :, :], slotf[:, :, :]))
            c3 = cmp[:, 0:n * E].rearrange("p (t e) -> p t e", t=n)
            chain.link(dve.tensor_tensor(c3, cnt[:, 3, 0:E].unsqueeze(1).to_broadcast([P, n, E]),
                                         iota[:, 0:n].unsqueeze(2).to_broadcast([P, n, E]), ALU.is_le))
            chain.link(dve.tensor_reduce(etf[:, 0:n], c3, AX.X, ALU.add))
            chain.link(dve.tensor_scalar(etf[:, 0:n], etf[:, 0:n], float(E - 1), None, ALU.min))
            dve.tensor_copy(et[:, 0:n], etf[:, 0:n]).then_inc(m["slot_done"], 1)
            if L == 1:
                shared_vector(dve)

            def hT_copy(t, j, p, first=False):
                dve.wait_ge(m["hT_done"], t + 1)
                if not first:
                    dve.wait_ge(m["w2_done"], t - 1)
                w = 512 if L == 0 else 2 * P
                if L == 0:
                    dve.tensor_copy(hTs[p], bk(2 + p)).then_inc(m["hT_copied"], 1)
                else:
                    dve.tensor_copy(hTs[p][:, 0:P], bk(2 + p)[:, 0:P]).then_inc(m["hT_copied"], 1)
                    dve.tensor_copy(hTs[p][0:48, P:2 * P], bk(2 + p)[0:48, P:2 * P]).then_inc(m["hT_copied"], 1)

            def gate(t, j, p, first=False):
                dve.wait_ge(m["sil_done"], t + 1)
                if not first:
                    dve.wait_ge(m["hT_done"], t - 1)
                dve.tensor_tensor(act_h[p][:, 0:176], gs[p], bk(p)[:, 176:352], ALU.mult
                                  ).then_inc(m["act_done"], 1)

            def step(t, j, p, first=False, last=False):
                hT_copy(t, j, p, first)
                if L == 1 and not last:
                    gate(t + 1, j, 1 - p, first and p == 0)

            if L == 1:
                gate(0, 0, 0, True)
            step(0, 0, 0, True)
            if L == 0:
                step(1, 0, 1, True)
            else:
                step(1, 0, 1, True)
            with dve.Fori(1, (n - 1) // 2) as i:
                step(2 * i, i, 0)
                step(2 * i + 1, i, 1)
            step(n - 1, n // 2, 0, last=True)
            for b in range(B):
                dve.wait_ge(m["gathered"][b % 4], 32 * (b // 4 + 1))
                chain.link(dve.scalar_tensor_tensor(x_sb[:, b, :], y_in[2 * (b % 4)], pw[:, 0, b:b + 1],
                                                    x_sb[:, b, :], ALU.mult, ALU.add))
                ins = dve.scalar_tensor_tensor(x_sb[:, b, :], y_in[2 * (b % 4) + 1], pw[:, 1, b:b + 1],
                                               x_sb[:, b, :], ALU.mult, ALU.add)
                ins.then_inc(m["combined"], 1)
                if L == 1:
                    dve.wait_ge(m["combined"], b + 1)
                    dve.sem_inc(S["x_final"], 1)
            if L == 0:
                dve.wait_ge(m["combined"], B)

        def shared_vector(dve):
            for b in range(B):
                p = b % 2
                dve.wait_ge(S["sh_sil"], b + 1)
                if b >= 2:
                    dve.wait_ge(S["sh_tr"], b - 1)
                dve.tensor_tensor(sh_h[p], sh_g[p], bk(4)[:, 0:352] if p == 0 else bk(6)[:, 0:352], ALU.mult
                                  ).then_inc(S["sh_act"], 1)
                if b >= 1:
                    shared_add(dve, b - 1)
            shared_add(dve, B - 1)

        def shared_add(dve, b):
            dve.wait_ge(S["sh_dn"], b + 1)
            dve.tensor_tensor(x_sb[:, b, :], x_sb[:, b, :], bk(0)[:, 256:512], ALU.add
                              ).then_inc(S["sh_dn_used"], 1)

        @block.vector
        def _(dve):
            chain = Chain(dve, S["dve_chain"])
            dve.wait_ge(S["x_in"], 16 * B)
            norm_rows(dve, 0)
            for u in range(6):
                hf, m = divmod(u, 3)
                ts = slice(HALF * hf, HALF * (hf + 1))
                part = [q_parts[:, j, m, ts] if m < 2 else k_parts[:, j, ts] for j in range(3)]
                dve.wait_ge(S["qk_copied"], u + 1)
                chain.link(dve.tensor_copy(part[0], pf[u % 2]))
                chain.link(dve.tensor_tensor(pr[u % 2], pf[u % 2], part[0], ALU.subtract))
                chain.link(dve.tensor_copy(part[1], pr[u % 2]))
                dve.tensor_tensor(part[2], pr[u % 2], part[1], ALU.subtract).then_inc(S["qk_split"], 1)
            for u in range(2):
                dve.wait_ge(S["v_proj"], u + 1)
                for b in range(4 * u, 4 * u + 4):
                    for s in range(2):
                        dve.tensor_copy(v_all[:, b, s, :, :],
                                        bk(6 + u)[:, P * (b % 4) + 64 * s: P * (b % 4) + 64 * s + 64]
                                        .rearrange("p (g d) -> p g d", g=G0)).then_inc(S["v_copied"], 1)

            def reduce(b, p, u):
                dve.wait_ge(S["s_done"], 16 * b + u + 1)
                dve.tensor_reduce(mx[:, p, 2 * u:2 * u + 2],
                                  bk(u % 2).rearrange("p (h k) -> p h k", h=2), AX.X, ALU.max
                                  ).then_inc(S["s_reduced"], 1)

            def split_max(b, p):
                dve.wait_ge(S["mT_done"], b + 1)
                ins = dve.tensor_scalar(mneg[:, :], bk(3)[0:H0, 0:P], -1.0, None, ALU.mult)
                ins.then_inc(S["mneg_done"], 1)
                dve.wait_ge(S["mneg_done"], b + 1)
                chain.link(dve.tensor_copy(msplit[:, p, 0, :], mneg[:, :]))
                chain.link(dve.tensor_tensor(mres[:, :], mneg[:, :], msplit[:, p, 0, :], ALU.subtract))
                chain.link(dve.tensor_copy(msplit[:, p, 1, :], mres[:, :]))
                dve.tensor_tensor(msplit[:, p, 2, :], mres[:, :], msplit[:, p, 1, :],
                                  ALU.subtract).then_inc(S["m_split"], 1)

            def normalise(b, hh):
                o = bk(2).rearrange("p (j g d) -> p g j d", j=HG, g=4)
                dve.wait_ge(S["half_turned"], 2 * b + hh + 1)
                if hh == 0:
                    dve.wait_ge(S["oT_done"], b)
                rd = rden[:, 16 * hh:16 * hh + 16].rearrange("p (g j) -> p g j", g=4)
                chain.link(dve.reciprocal(rd, o[:, :, :, HD]))
                dve.tensor_tensor(onorm[:, 16 * hh:16 * hh + 16, :].rearrange("p (g j) d -> p g j d", g=4),
                                  o[:, :, :, 0:HD], rd.unsqueeze(3).to_broadcast([P, 4, HG, HD]), ALU.mult
                                  ).then_inc(S["norm_done"], 1)

            def add_attention(b):
                dve.wait_ge(S["wo_done"], b + 1)
                xb = x_sb[:, b, :] if isinstance(b, int) else x_sb[:, bass.ds(b, 1), :].rearrange("p o d -> p (o d)")
                dve.tensor_tensor(xb, xb, bk(3)[:, 256:512], ALU.add).then_inc(S["x_added"], 1)

            def body(b, i, o, first=False, last=False):
                pn = (o + 1) % BUFS
                u = 0
                for g in range(G0):
                    if not last:
                        for _ in range(UNITS[g]):
                            reduce(b + 1, pn, u)
                            u += 1
                    if g == 1 and not first:
                        normalise(b - 1, 1)
                    if g == 3 and not first:
                        add_attention(b - 1)
                    if g == 4 and not last:
                        split_max(b + 1, pn)
                    if g == 5:
                        normalise(b, 0)

            for u in range(16):
                reduce(0, 0, u)
            split_max(0, 0)
            body(0, 0, 0, first=True)
            n0 = chain.n
            with dve.Fori(0, 2) as i:
                per = 15
                chain.dyn = i * per
                for o in (1, 2, 3):
                    body(o + BUFS * i, i, o)
                assert chain.n == n0 + per, (chain.n, n0)
            chain.n, chain.dyn = n0 + 2 * per, 0
            body(7, 2, 1, last=True)
            normalise(7, 1)
            add_attention(7)
            dve.wait_ge(S["x_added"], B)
            norm_rows(dve, 1)
            moe_vector(dve, chain, 0)
            norm_rows(dve, 2)
            dve.wait_ge(S["ctxl_in"], 32)
            dve.wait_ge(S["wo_in"], 48)

            def diagonal(h, j, p):
                dve.wait_ge(toep_in[p], 16 * (j + 1))
                dcol = d_bc[:, h:h + 1] if isinstance(h, int) else d_bc[:, bass.ds(h, 1)]
                dve.scalar_tensor_tensor(toep[p][:, 0:P], anti[:, :], dcol, toep[p][:, 0:P],
                                         ALU.mult, ALU.add).then_inc(S["toep_fixed"], 1)

            def weigh(h, p):
                for c in range(2):
                    dve.wait_ge(S["conv_done"], 2 * h + c + 1)
                    cols = slice(CW * h, CW * h + CW) if isinstance(h, int) else bass.ds(h * CW, CW)
                    q = hT[:, c, :].rearrange("p (b n) -> p b n", b=B)[:, :, cols]
                    y = bk(2 * p + c).rearrange("p (b i j) -> p b j i", b=B, i=CW)
                    pv = prod[c].rearrange("p (b j i) -> p b j i", b=B, j=CW)
                    dve.tensor_tensor(pv, y, q.unsqueeze(2).to_broadcast([P, B, CW, CW]), ALU.mult
                                      ).then_inc(S["conv_used"], 1)
                    dve.wait_ge(S["conv_used"], 2 * h + c + 1)
                    dve.tensor_reduce(convT[:, c, :, cols], pv, AX.X, ALU.add).then_inc(S["convT_done"], 1)

            diagonal(0, 0, 0)
            diagonal(1, 0, 1)
            dve.wait_ge(S["tr_copied"], 3 * B)
            with dve.Fori(0, HC // 2 - 1) as i:
                weigh(2 * i, 0)
                diagonal(2 * i + 2, i + 1, 0)
                weigh(2 * i + 1, 1)
                diagonal(2 * i + 3, i + 1, 1)
            weigh(HC - 2, 0)
            weigh(HC - 1, 1)
            for b in range(B):
                dve.wait_ge(S["back_done"], b + 1)
                dve.tensor_tensor(x_sb[:, b, :], x_sb[:, b, :], bk(4 + b % 2)[:, 0:D], ALU.add
                                  ).then_inc(S["back_added"], 1)
            dve.wait_ge(S["back_added"], B)
            norm_rows(dve, 3)
            moe_vector(dve, chain, 1)

        def copy_rows(act, n):
            for b in range(B):
                act.wait_ge(S["tr_done"], n * B + b + 1)
                act.activation(hT[:, :, P * b:P * (b + 1)],
                               bk(6 + b % 2)[:, 0:2 * P].rearrange("p (c t) -> p c t", c=KD),
                               ACT.Copy).then_inc(S["tr_copied"], 1)

        def moe_scalar(act, L):
            m, n, E = M[L], MOE[L]["tiles"], MOE[L]["E"]
            act.wait_ge(m["logit_copied"], 1)
            if L == 0:
                act.activation(ptmp[:, 1, :], ptmp[:, 0, :], ACT.Exp).then_inc(m["prob_exp"], 1)
            else:
                act.activation(logits[:, :, 0:E], base[:, :, 0:E], ACT.Exp).then_inc(m["prob_exp"], 1)
                for b in range(B):
                    p = b % 2
                    act.wait_ge(S["sh_up"], b + 1)
                    if b >= 2:
                        act.wait_ge(S["sh_act"], b - 1)
                    act.activation(sh_g[p], bk(5)[:, 0:352] if p == 0 else bk(7)[:, 0:352], ACT.Silu
                                   ).then_inc(S["sh_sil"], 1)
                    act.wait_ge(S["sh_tr"], b + 1)
                    if b >= 2:
                        act.wait_ge(S["sh_dn"], b - 1)
                    act.activation(sh_T[p][:, 0:2 * P], bk(1)[:, 0:2 * P], ACT.Copy).then_inc(S["sh_trc"], 1)
                    act.activation(sh_T[p][0:96, 2 * P:3 * P], bk(1)[0:96, 2 * P:3 * P], ACT.Copy
                                   ).then_inc(S["sh_trc"], 1)

            def xT_copy(t, j, p, first=False):
                act.wait_ge(m["xT_done"], t + 1)
                if not first:
                    act.wait_ge(m["w1_done"], t - 1)
                act.activation(xTs[p], bk(4 + p)[:, 0:D], ACT.Copy).then_inc(m["xT_copied"], 1)

            def silu(t, j, p, first=False):
                act.wait_ge(m["w1_done"], t + 1)
                if L == 0:
                    if not first:
                        act.wait_ge(m["hT_done"], t - 1)
                    act.activation(act_h[p], bk(p), ACT.Silu).then_inc(m["act_done"], 1)
                else:
                    if not first:
                        act.wait_ge(m["act_done"], t - 1)
                    act.activation(gs[p], bk(p)[:, 0:176], ACT.Silu).then_inc(m["sil_done"], 1)

            def y_copy(t, j, p, first=False):
                act.wait_ge(m["w2_done"], t + 1)
                if not first:
                    act.wait_ge(m["stored"][p], 16 * j)
                act.activation(y_sb[p], bk(6 + p)[:, 0:D], ACT.Copy).then_inc(m["y_done"], 1)

            def step(t, j, p, first=False, left=9):
                if left > 1:
                    silu(t + 1, j, 1 - p, first and p == 0)
                y_copy(t, j, p, first)
                if left > 2:
                    xT_copy(t + 2, j + 1, p)

            xT_copy(0, 0, 0, True)
            silu(0, 0, 0, True)
            xT_copy(1, 0, 1, True)
            step(0, 0, 0, True)
            step(1, 0, 1, True)
            with act.Fori(1, (n - 3) // 2) as i:
                step(2 * i, i, 0)
                step(2 * i + 1, i, 1)
            for t in range(n - 3, n):
                step(t, t // 2, t % 2, left=n - t)

        @block.scalar
        def _(act):
            copy_rows(act, 0)
            for u in range(6):
                hf, m = divmod(u, 3)
                act.wait_ge(S["qk_proj"], u + 1)
                if u >= 2:
                    act.wait_ge(S["qk_split"], u - 1)
                act.activation(pf[u % 2], bk(u), ACT.Copy, scale=SCALE if m < 2 else 1.0
                               ).then_inc(S["qk_copied"], 1)
            act.wait_ge(S["qk_split"], 6)

            def exps(b, g):
                act.wait_ge(S["st_done"], 8 * b + g + 1)
                if not (isinstance(b, int) and b == 0):
                    act.wait_ge(S["pv_done"], 2 * b - 1 + g // 4)
                act.activation(p_buf[g], st_ps[g % 2][:, :, :].rearrange("p s n -> p (s n)"), ACT.Exp
                               ).then_inc(S["exp_done"], 1)

            def m_rows(b, p):
                act.wait_ge(S["m_split"], b + 1)
                for r in range(3):
                    act.dma_start(q_stack[p][NS + r:NS + r + 1, :].rearrange("o (h t) -> o h t", h=H0),
                                   msplit[:, p, r, :]).then_inc(m_in[p], 16)

            def copy_half(b, hh, first=False):
                act.wait_ge(S["pv_done"], 2 * b + hh + 1)
                if not first:
                    act.wait_ge(S["half_turned"], 2 * b + hh)
                act.activation(half_T, bk(2), ACT.Copy).then_inc(S["half_copied"], 1)

            def copy_oT(b):
                act.wait_ge(S["oT_done"], b + 1)
                if not (isinstance(b, int) and b == 0):
                    act.wait_ge(S["wo_done"], b)
                act.activation(oTs[:, :, :].rearrange("p c t -> p (c t)"), bk(3)[:, 0:2 * P], ACT.Copy
                               ).then_inc(S["oT_copied"], 1)

            def body(b, o, first=False, last=False):
                for g in range(G0):
                    exps(b, g)
                    if g == 0 and not first:
                        copy_half(b - 1, 1)
                    if g == 2 and not first:
                        copy_oT(b - 1)
                    if g == 4:
                        copy_half(b, 0, first)
                    if g == 5 and not last:
                        m_rows(b + 1, (o + 1) % BUFS)

            m_rows(0, 0)
            body(0, 0, first=True)
            with act.Fori(0, 2) as i:
                for o in (1, 2, 3):
                    body(o + BUFS * i, o)
            body(7, 1, last=True)
            copy_half(7, 1)
            copy_oT(7)
            copy_rows(act, 1)
            moe_scalar(act, 0)
            copy_rows(act, 2)
            copy_rows(act, 3)
            moe_scalar(act, 1)

        def turn_rows(pe, n):
            for b in range(B):
                pe.wait_ge(S["h_done"], n * B + b + 1)
                if n * B + b >= 2:
                    pe.wait_ge(S["tr_copied"], n * B + b - 1)
                for c in range(KD):
                    ins = pe.transpose(bk(6 + b % 2)[:, P * c:P * (c + 1)], h_sb[:, b, P * c:P * (c + 1)],
                                       identf[:, :])
                ins.then_inc(S["tr_done"], 1)

        def moe_tensor(pe, L):
            m, E, n = M[L], MOE[L]["E"], MOE[L]["tiles"]
            rows, W = MOE[L]["rows"], MOE[L]["W"]
            rw = router if L == 0 else router1
            weights = moe_w[L]
            pe.wait_ge(S["tr_copied"], (1 + 2 * L) * B + B)
            pe.wait_ge(S["late_in"], 80)
            pe.wait_ge(S["wo_in"], 48)
            for b in range(B):
                for c in range(KD):
                    ins = pe.matmul(bk(0)[:, E * b:E * (b + 1)], hT[:, c, P * b:P * (b + 1)], rw[:, c, :],
                                    start=(c == 0), stop=(c == KD - 1))
            ins.then_inc(m["logit_done"], 1)
            pe.wait_ge(m["hot_done"], 1)
            hb = hotb[:, :, 0:E]
            rk = bk(1)[:, 0:B * E].rearrange("p (b e) -> p b e", b=B)
            pe.matmul(rk, tri[:, :], hb, start=True, stop=True)
            for s in range(1, B):
                ins = pe.matmul(rk[:, s:B, :], onesb[:, :], hb[:, 0:B - s, :], start=False, stop=True,
                                skip_group_check=True)
            ins.then_inc(m["rank_done"], 1)
            for b in range(B):
                ins = pe.matmul(bk(2)[:, 0:E], onesb[:, :], hb[:, b, :], start=(b == 0), stop=(b == B - 1))
            ins.then_inc(m["cnt_done"], 1)
            pe.wait_ge(m["slot_done"], 1)
            if L == 0:
                pe.wait_ge(expert_in, 16 * 5)
            else:
                pe.wait_ge(S["lay1_in"], 48)
                shared_tensor(pe)

            def turn_x(t, j, p, first=False):
                pe.wait_ge(m["xin"][p], 16 * (j + 1))
                if not first:
                    pe.wait_ge(m["xT_copied"], t - 1)
                for c in range(KD):
                    ins = pe.transpose(bk(4 + p)[:, P * c:P * (c + 1)], xt[p][:, P * c:P * (c + 1)], identf[:, :])
                ins.then_inc(m["xT_done"], 1)

            def expert(t):
                col = et[0:1, t:t + 1] if isinstance(t, int) else et[0:1, bass.ds(t, 1)]
                return pe.value_load(col, min_val=0, max_val=E - 1)

            def up(t, j, p, first=False):
                e = expert(t)
                pe.wait_ge(m["xT_copied"], t + 1)
                if not first:
                    pe.wait_ge(m["act_done"], t - 1)
                for c in range(KD):
                    ins = pe.matmul(bk(p)[:, 0:W], xTs[p][:, P * c:P * (c + 1)],
                                    weights[:, bass.ds(e, 1), W * c:W * (c + 1)].rearrange("p o n -> p (o n)"),
                                    start=(c == 0), stop=(c == KD - 1))
                ins.then_inc(m["w1_done"], 1)

            def turn_h(t, j, p, first=False):
                pe.wait_ge(m["act_done"], t + 1)
                if not first:
                    pe.wait_ge(m["hT_copied"], (t - 1) * (1 + L))
                for c, r in enumerate(rows):
                    ins = pe.transpose(bk(2 + p)[0:r, P * c:P * (c + 1)], act_h[p][:, P * c:P * c + r], identf[:, :])
                ins.then_inc(m["hT_done"], 1)

            def down(t, j, p, first=False):
                e = expert(t)
                pe.wait_ge(m["hT_copied"], (t + 1) * (1 + L))
                if not first:
                    pe.wait_ge(m["y_done"], t - 1)
                for c, r in enumerate(rows):
                    w0 = KD * W + D * c
                    ins = pe.matmul(bk(6 + p)[:, 0:D], hTs[p][0:r, P * c:P * (c + 1)],
                                    weights[0:r, bass.ds(e, 1), w0:w0 + D].rearrange("p o n -> p (o n)"),
                                    start=(c == 0), stop=(c == len(rows) - 1))
                ins.then_inc(m["w2_done"], 1)

            def step(t, j, p, first=False, left=9):
                turn_h(t, j, p, first)
                if left > 1:
                    up(t + 1, j, 1 - p, first and p == 0)
                down(t, j, p, first)
                if left > 2:
                    turn_x(t + 2, j + 1, p)

            turn_x(0, 0, 0, True)
            up(0, 0, 0, True)
            turn_x(1, 0, 1, True)
            step(0, 0, 0, True)
            step(1, 0, 1, True)
            with pe.Fori(1, (n - 3) // 2) as i:
                step(2 * i, i, 0)
                step(2 * i + 1, i, 1)
            for t in range(n - 3, n):
                step(t, t // 2, t % 2, left=n - t)

        def shared_tensor(pe):
            def up(b):
                if b >= 2:
                    pe.wait_ge(S["sh_act"], b - 1)
                for n in range(2):
                    for c in range(KD):
                        ins = pe.matmul(bk(4 + 2 * (b % 2) + 1 - n)[:, 0:352], hT[:, c, P * b:P * (b + 1)],
                                        sgu[:, c, 352 * n:352 * (n + 1)], start=(c == 0), stop=(c == KD - 1))
                ins.then_inc(S["sh_up"], 1)

            up(0)
            for b in range(B):
                p = b % 2
                if b + 1 < B:
                    up(b + 1)
                pe.wait_ge(S["sh_act"], b + 1)
                if b >= 1:
                    pe.wait_ge(S["sh_trc"], 2 * b)
                for c, r in enumerate([P, P, 96]):
                    ins = pe.transpose(bk(1)[0:r, P * c:P * (c + 1)], sh_h[p][:, P * c:P * c + r], identf[:, :])
                ins.then_inc(S["sh_tr"], 1)
                pe.wait_ge(S["sh_trc"], 2 * b + 2)
                if b >= 1:
                    pe.wait_ge(S["sh_dn_used"], b)
                for c, r in enumerate([P, P, 96]):
                    ins = pe.matmul(bk(0)[:, 256:512], sh_T[p][0:r, P * c:P * (c + 1)], sdn[0:r, c, :],
                                    start=(c == 0), stop=(c == 2))
                ins.then_inc(S["sh_dn"], 1)
            pe.wait_ge(S["sh_dn_used"], B)

        @block.tensor
        def _(pe):
            pe.wait_ge(S["const_in"], 16)
            turn_rows(pe, 0)
            pe.wait_ge(S["tr_copied"], B)
            pe.wait_ge(S["ctx_in"], 16)
            pe.wait_ge(S["proj_in"], 48)

            def src(c):
                return cT[:, c, :] if c < 2 else hT[:, c - 2, :]

            for hf in range(2):
                ts = slice(HALF * hf, HALF * (hf + 1))
                for mm in range(2):
                    for c in range(4):
                        ins = pe.matmul(bk(3 * hf + mm), wq[:, c, P * mm:P * (mm + 1)], src(c)[:, ts],
                                        start=(c == 0), stop=(c == 3))
                    ins.then_inc(S["qk_proj"], 1)
                for s in range(2):
                    for c in range(2):
                        ins = pe.matmul(bk(3 * hf + 2)[64 * s:64 * s + 64, :], wk[:, 2 * s + c, :],
                                        src(2 * s + c)[:, ts], start=(c == 0), stop=(c == 1))
                ins.then_inc(S["qk_proj"], 1)
            for u in range(2):
                for b in range(4 * u, 4 * u + 4):
                    for s in range(2):
                        for c in range(2):
                            ins = pe.matmul(bk(6 + u)[:, P * (b % 4) + 64 * s:P * (b % 4) + 64 * s + 64],
                                            src(2 * s + c)[:, P * b:P * (b + 1)], wv[:, 2 * s + c, :],
                                            start=(c == 0), stop=(c == 1))
                ins.then_inc(S["v_proj"], 1)

            pe.wait_ge(S["late_in"], 48)
            pe.wait_ge(S["const_rows"], 16 * 3 * BUFS)
            pe.wait_ge(S["qk_copied"], 6)
            pe.wait_ge(S["v_copied"], 2 * B)

            def scores_q(b, p, u, first=False):
                if not (first and u < 2):
                    pe.wait_ge(S["s_reduced"], 16 * b + u - 1)
                o = bk(u % 2)
                pe.matmul(o, identb[:, :], masks[:, 0, :], start=True, stop=True)
                for h in (2 * u, 2 * u + 1):
                    ins = pe.matmul(o[:, 256 * (h % 2):256 * (h % 2) + 256],
                                    q_stack[p][0:NS, P * h:P * (h + 1)],
                                    k_stack[p][0:NS, h // HG].rearrange("p s t -> p (s t)"),
                                    start=False, stop=True, skip_group_check=True)
                ins.then_inc(S["s_done"], 1)

            def turn_max(b, p, first=False):
                pe.wait_ge(S["s_reduced"], 16 * b + 16)
                if not first:
                    if not (isinstance(b, int) and b == 1):
                        pe.wait_ge(S["x_added"], b - 1)
                    pe.wait_ge(S["mneg_done"], b)
                pe.transpose(bk(3)[0:H0, 0:P], mx[:, p, :], identf[:, :]).then_inc(S["mT_done"], 1)

            def scores_k(b, p, g, first=False):
                if not (first and g < 2):
                    pe.wait_ge(S["exp_done"], 8 * b + g - 1)
                for s in range(2):
                    pe.matmul(st_ps[g % 2][:, s, :], identb[:, :], masks[:, 1 + s, :], start=True, stop=False)
                    ins = pe.matmul(st_ps[g % 2][:, s, :], k_stack[p][0:NQ, g, s, :],
                                    q_stack[p][0:NQ, 512 * g:512 * (g + 1)], start=False, stop=True)
                ins.then_inc(S["st_done"], 1)

            def values(b, p, hh, first=False):
                pe.wait_ge(S["exp_done"], 8 * b + 4 * hh + 4)
                if hh == 0:
                    pe.wait_ge(S["v_ready"], b + 1)
                if not first:
                    pe.wait_ge(S["norm_done"], 2 * b + hh)
                for s in range(2):
                    for c in range(4):
                        g = 4 * hh + c
                        ins = pe.matmul(bk(2)[VC * c:VC * (c + 1), :], v_buf[:, p, s, g, :],
                                        p_buf[g][:, 512 * s:512 * (s + 1)], start=(s == 0), stop=(s == 1))
                ins.then_inc(S["pv_done"], 1)

            def turn_half(b, hh):
                pe.wait_ge(S["half_copied"], 2 * b + hh + 1)
                for j in range(HG):
                    ins = pe.transpose(bk(2)[:, P * j:P * (j + 1)], half_T[:, P * j:P * (j + 1)], identf[:, :])
                ins.then_inc(S["half_turned"], 1)

            def turn_o(b):
                pe.wait_ge(S["norm_done"], 2 * b + 2)
                pe.wait_ge(S["mneg_done"], b + 2 if not (isinstance(b, int) and b == B - 1) else B)
                for c in range(KD):
                    ins = pe.transpose(bk(3)[:, P * c:P * (c + 1)],
                                       onorm[:, 16 * c:16 * c + 16, :].rearrange("p h d -> p (h d)"), identf[:, :])
                ins.then_inc(S["oT_done"], 1)

            def project_o(b):
                pe.wait_ge(S["oT_copied"], b + 1)
                for c in range(KD):
                    ins = pe.matmul(bk(3)[:, 256:512], oTs[:, c, :], wo[:, c, :], start=(c == 0), stop=(c == 1))
                ins.then_inc(S["wo_done"], 1)

            def body(b, i, o, first=False, last=False):
                p, pn = o % BUFS, (o + 1) % BUFS
                u = 0
                for g in range(G0):
                    if not last:
                        if g == 0:
                            pe.wait_ge(stack_in[pn], STACKED * (i + (o + 1) // BUFS + 1))
                        for _ in range(UNITS[g]):
                            scores_q(b + 1, pn, u)
                            u += 1
                    if g == 0:
                        pe.wait_ge(m_in[p], 48 * (i + o // BUFS + 1))
                    if g == 4 and not last:
                        turn_max(b + 1, pn)
                    scores_k(b, p, g, first)
                    if g == 0 and not first:
                        values(b - 1, (o - 1) % BUFS, 1)
                    if g == 1 and not first:
                        turn_half(b - 1, 1)
                    if g == 4:
                        values(b, p, 0, first)
                    if g == 5:
                        turn_half(b, 0)
                    if g == 2 and not first:
                        turn_o(b - 1)
                    if g == 3 and not first:
                        project_o(b - 1)

            pe.wait_ge(stack_in[0], STACKED)
            for u in range(16):
                scores_q(0, 0, u, first=True)
            turn_max(0, 0, first=True)
            body(0, 0, 0, first=True)
            with pe.Fori(0, 2) as i:
                for o in (1, 2, 3):
                    body(o + BUFS * i, i, o)
            body(7, 2, 1, last=True)
            values(7, 1, 1)
            turn_half(7, 1)
            turn_o(7)
            project_o(7)
            turn_rows(pe, 1)
            moe_tensor(pe, 0)
            turn_rows(pe, 2)

            def convolve(h, j, p, first=False):
                pe.wait_ge(S["toep_fixed"], h + 1)
                pe.wait_ge(S["kv_done"], 2 * h + 2)
                if not first:
                    pe.wait_ge(S["conv_used"], 2 * h - 2)
                pe.matmul(bk(2 * p), toep[p][:, 0:P], kv[p][:, 0, :], start=True, stop=True
                          ).then_inc(S["conv_done"], 1)
                pe.matmul(bk(2 * p + 1), toep[p][:, P:2 * P], kv[p][:, 0, :], start=True, stop=False)
                pe.matmul(bk(2 * p + 1), toep[p][:, 0:P], kv[p][:, 1, :], start=False, stop=True
                          ).then_inc(S["conv_done"], 1)

            convolve(0, 0, 0, True)
            convolve(1, 0, 1, True)
            with pe.Fori(1, HC // 2) as i:
                convolve(2 * i, i, 0)
                convolve(2 * i + 1, i, 1)
            pe.wait_ge(S["convT_done"], 2 * HC)
            for b in range(B):
                if b >= 2:
                    pe.wait_ge(S["back_added"], b - 1)
                for c in range(2):
                    ins = pe.transpose(bk(4 + b % 2)[:, P * c:P * (c + 1)], convT[:, c, b, :], identf[:, :])
                ins.then_inc(S["back_done"], 1)
            turn_rows(pe, 3)
            moe_tensor(pe, 1)


def constants():
    bf = np.dtype("bfloat16")
    c = {}
    c["identf"] = np.eye(P, dtype=np.float32)
    c["identb"] = np.eye(P).astype(bf)
    c["anti"] = np.ascontiguousarray(np.eye(P, dtype=np.float32)[::-1])
    q, k = np.arange(P)[:, None], np.arange(P)[None, :]
    ssm = np.where((q - k >= 0) & (q - k < WIN_SSM), 0.0, NEG)
    att = np.where((q - k >= 0) & (q - k < WIN_ATT), 0.0, NEG)
    c["masks"] = np.stack([np.concatenate([ssm, att, ssm, att], 1), np.tile(ssm.T, (1, 4)),
                           np.tile(att.T, (1, 4))], 1).astype(bf)
    c["tri"] = (np.arange(P)[:, None] < np.arange(P)[None, :]).astype(bf)
    c["iota"] = np.tile(np.arange(32, dtype=np.float32), (P, 1))
    slopes = np.power(np.float32(2.0), -8.0 * np.arange(H0, dtype=np.float32) / H0).astype(np.float32)
    parts, left = [], slopes.copy()
    for _ in range(3):
        parts.append(left.astype(bf))
        left = left - parts[-1].astype(np.float32)
    c["slope_rows"] = np.stack([np.repeat(s, P) for s in parts]).astype(bf)
    pos = np.arange(P) - P // 2
    c["key_rows"] = np.concatenate([np.tile(pos, (3, G0, 2, 1)), np.ones((3, G0, 2, P))]).astype(bf)
    return c


def layouts(i):
    f = {k: np.asarray(v) for k, v in i.items()}
    ctx = f["ctx_2048"]
    w = {"x": f["x"]}

    def chunked(m, rows=P):
        return m.reshape(-1, rows, m.shape[-1]).transpose(1, 0, 2)

    w["ctx_d"] = ctx.reshape(T, KD, P).transpose(2, 1, 0)
    w["ctx_l"] = ctx.reshape(B, P, 2, P)[:, :, :, ::-1].transpose(3, 2, 0, 1)
    w["wq"] = chunked(f["L0_xattn_Wq"])
    w["wk"] = np.concatenate([chunked(f["L0_xattn_Wsk"]), chunked(f["L0_xattn_Wk"])], 1)
    w["wv"] = np.concatenate([chunked(f["L0_xattn_Wsv"]), chunked(f["L0_xattn_Wv"])], 1)
    w["wo"] = chunked(f["L0_xattn_Wo"])
    w["router"] = chunked(f["L0_ffn_router_w"])
    w1 = f["L0_ffn_W1"].reshape(16, 2, P, 512).transpose(2, 0, 1, 3).reshape(P, 16, 1024)
    w2 = f["L0_ffn_W2"].reshape(16, 4, P, D).transpose(2, 0, 1, 3).reshape(P, 16, 1024)
    w["w_moe0"] = np.concatenate([w1, w2], 2)
    w["kpad"] = np.pad(f["L1_xattn_ssm_kernel"], ((0, 0), (P - 1, 0)))
    w["D"] = f["L1_xattn_D"]
    w["gate_w"] = chunked(f["L1_ffn_gate_w"])
    gu = np.concatenate([f["L1_ffn_w_gate"], f["L1_ffn_w_up"]], 2)
    gu = gu.reshape(8, 2, P, 352).transpose(2, 0, 1, 3).reshape(P, 8, 704)
    dn = np.pad(f["L1_ffn_w_down"], ((0, 0), (0, 2 * P - 176), (0, 0)))
    dn = dn.reshape(8, 2, P, D).transpose(2, 0, 1, 3).reshape(P, 8, 512)
    w["w_moe1"] = np.concatenate([gu, dn], 2)
    w["sgu"] = chunked(np.concatenate([f["L1_ffn_sw_gate"], f["L1_ffn_sw_up"]], 1))
    w["sdn"] = chunked(np.pad(f["L1_ffn_sw_down"], ((0, 3 * P - 352), (0, 0))))
    w.update(constants())
    return {k: np.ascontiguousarray(v) for k, v in w.items()}


def kernel(**inputs):
    import concourse.bacc as bacc
    from concourse.bass_utils import run_bass_kernel_spmd

    arrays = layouts(inputs)
    nc = bacc.Bacc("TRN2", target_bir_lowering=False, num_devices=1)
    aps = {k: nc.dram_tensor(f"in_{k}", v.shape, mybir.dt.from_np(v.dtype), kind="ExternalInput").ap()
           for k, v in arrays.items()}
    out = nc.dram_tensor("out", (B, P, D), F32, kind="ExternalOutput").ap()
    build(nc, aps, out)
    r = run_bass_kernel_spmd(nc, [{f"in_{k}": v for k, v in arrays.items()}], core_ids=[0])
    return r.results[0]["out"]
```

```python
from contextlib import ExitStack

import numpy as np

import concourse.bass as bass
from concourse import mybir

F32 = mybir.dt.float32
BF16 = mybir.dt.bfloat16
I32 = mybir.dt.int32
U32 = mybir.dt.uint32
ALU = mybir.AluOpType
ACT = mybir.ActivationFunctionType
AX = mybir.AxisListType

P = 128
B = 8
D = 256
KD = D // P
T = B * P

H0 = 32
G0 = 8
HG = H0 // G0
HD = 8
SLOPE, NS, NQ = 48, 96, 99
WIN_SSM, WIN_ATT = 64, 32
SCALE = 1.0 / float(np.sqrt(HD))
NEG = -1e30
VC = 32

HC = 16
CW = 8
LC = 2 * P
TB = 4

EPS = 1e-5
BUFS = 3
LATE = 9
HALF = T // 2


MOE = [
    dict(E=16, W=512, rows=[128, 128, 128, 128]),
    dict(E=8, W=352, rows=[128, 48]),
]
for _m in MOE:
    _m["tiles"] = 2 * T // P + _m["E"] - 1
NT = MOE[0]["tiles"]
TU = 4
assert all(_m["tiles"] % TU == 3 for _m in MOE)
RAMP = P + 1 + 2 * B + NT


def build(nc, a, out):
    with ExitStack() as ctx:
        def sb(name, shape, dt=F32):
            return ctx.enter_context(nc.sbuf_tensor(name, shape, dt))

        def sem(name):
            return ctx.enter_context(nc.semaphore(name))

        bank = [ctx.enter_context(nc.psum_tensor(f"bank{i}", [P, 512], F32)) for i in range(4)]
        st_ps = [ctx.enter_context(nc.psum_tensor(f"st_ps{i}", [P, 2, 512], F32)) for i in range(2)]
        banks = [bank[0], bank[1], bank[2], bank[3], st_ps[0][:, 0, :], st_ps[0][:, 1, :],
                 st_ps[1][:, 0, :], st_ps[1][:, 1, :]]

        def bk(i):
            return banks[i][:, :] if i < 4 else banks[i]

        qd = nc.dram_tensor("q_parts_by_row", [3, HD, H0, T], BF16, kind="Internal").ap()
        kd = nc.dram_tensor("k_parts_by_row", [6, HD, G0, 2, T], BF16, kind="Internal").ap()
        hd = nc.dram_tensor("rows", [T, D], F32, kind="Internal").ap()
        yd = nc.dram_tensor("results", [2 * T + NT * P, D], F32, kind="Internal").ap()
        kc = nc.dram_tensor("kernels_with_d", [HC, P - 1 + LC], F32, kind="Internal").ap()

        wall = sb("wall", [P, 16 * 2048])
        x_sb = sb("x_sb", [P, B, D])
        h_sb = sb("h_sb", [P, B, D])
        hT = sb("hT", [P, KD, T])
        cT = sb("cT", [P, KD, T])
        parts = sb("parts", [P, 4608])
        q_parts = parts[:, 0:3072].bitcast(BF16).rearrange("p (j c t) -> p j c t", j=3, c=2)
        k_parts = parts[:, 3072:4608].bitcast(BF16).rearrange("p (j t) -> p j t", j=3)
        v_all = sb("v_all", [P, B, 2, G0, HD])
        v_buf = sb("v_buf", [P, BUFS, 2, G0, VC])
        at_w = 5 * 2048
        wq = wall[:, at_w:at_w + 1024].rearrange("p (c n) -> p c n", c=4)
        wk = wall[:, at_w + 1024:at_w + 1536].rearrange("p (c n) -> p c n", c=4)
        wv = wall[:, at_w + 1536:at_w + 1792].rearrange("p (c n) -> p c n", c=4)
        wo = sb("wo", [P, KD, D])
        masks = sb("masks", [P, 3, 512], BF16)
        identf = sb("identf", [P, P])
        identb = sb("identb", [P, P], BF16)
        tri = sb("tri", [P, P], BF16)
        onesb = sb("onesb", [P, P], BF16)
        ramp = sb("ramp", [P, RAMP])
        iota = ramp[:, 0:P]
        iotab = sb("iotab", [P, P], BF16)
        row_no = ramp[:, P:P + 1]
        choice_no = ramp[:, P + 1:P + 1 + 2 * B]
        unused = ramp[:, P + 1 + 2 * B:RAMP]
        stats = sb("stats", [P, B, 6])
        mv = sb("mv", [P, B, 2])
        vare = sb("vare", [P, B])
        rstd = sb("rstd", [P, B])
        neghalf = sb("neghalf", [P, B])
        mx = sb("mx", [P, BUFS, H0])
        c_flat = cT[:, :, :].rearrange("p c t -> p (c t)")
        mneg = c_flat[0:H0, 0:P]
        mres = c_flat[0:H0, P:2 * P]
        half_T = c_flat[:, 256:768]
        onorm = c_flat[:, 768:1024].rearrange("p (h d) -> p h d", h=H0)
        oTs = c_flat[:, 1024:1280].rearrange("p (c t) -> p c t", c=KD)
        msplit = sb("msplit", [H0, BUFS, 3, P], BF16)
        rden = sb("rden", [P, H0])

        att = LATE * 2048
        q_stack = [wall[:, att + 2048 * i: att + 2048 * (i + 1)].bitcast(BF16) for i in range(BUFS)]
        at_k = att + 2048 * BUFS
        k_stack = [wall[:, at_k + 1024 * i: at_k + 1024 * (i + 1)].bitcast(BF16)
                   .rearrange("p (g s t) -> p g s t", g=G0, s=2) for i in range(BUFS)]
        at_p = at_k + 1024 * BUFS
        p_buf = ([h_sb[:, 4 * i:4 * i + 4, :].rearrange("p b d -> p (b d)") for i in range(2)]
                 + [hT[:, i, :] for i in range(2)]
                 + [wall[:, at_p + 1024 * i: at_p + 1024 * (i + 1)] for i in range(4)])
        pf = [p_buf[4 + i][:, 0:512] for i in range(2)]
        pr = [p_buf[4 + i][:, 512:1024] for i in range(2)]

        at = [0]

        def carve(n):
            at[0] += n
            assert at[0] <= 4608, at[0]
            return parts[:, at[0] - n: at[0]]

        xt = [carve(D) for _ in range(2)]
        xTs = [carve(D) for _ in range(2)]
        act_h = [carve(512) for _ in range(2)]
        hTs = [carve(512) for _ in range(2)]
        y_sb = [carve(D) for _ in range(2)]
        w1_now = [h_sb[:, 4 * i:4 * i + 4, :].rearrange("p b d -> p (b d)") for i in range(2)]
        gs = [carve(176) for _ in range(2)]
        logits = sb("logits", [P, B, 16])
        top = sb("top", [P, B, 8])
        topi = sb("topi", [P, B, 8], U32)
        idxf = sb("idxf", [P, 2, B])
        hot = carve(2 * B * 16).rearrange("p (k b e) -> p k b e", k=2, b=B)
        hotb = sb("hotb", [P, B, 16], BF16)
        pw = sb("pw", [P, 2, B])
        ptmp = sb("ptmp", [P, 4, B])
        cmp = parts[:, 3072:3072 + NT * 16]
        tile_hot = parts[:, 512:512 + B * NT].bitcast(BF16).rearrange("p (c n) -> p c n", c=2 * B)
        tile_rows = parts[:, 768:768 + 2 * B * NT].bitcast(BF16).rearrange("p (c v n) -> p c v n", c=2 * B, v=2)
        place_hot = parts[:, 2048:3072].bitcast(BF16).rearrange("p (c r) -> p c r", c=2 * B)
        cnt = sb("cnt", [P, 4, 32])
        base = carve(B * 16).rearrange("p (b e) -> p b e", b=B)
        slotf = sb("slotf", [P, 2, B])
        in_tile = sb("in_tile", [P, 2, 2 * B])
        by_slot = sb("by_slot", [P, 6, NT])
        src_row = sb("src_row", [P, NT], U32)
        dst_row = sb("dst_row", [P, NT], U32)
        etf = sb("etf", [P, NT])
        et = sb("et", [P, NT], I32)
        router = sb("router", [P, KD, 16])
        router1 = sb("router1", [P, KD, 8])
        y_in = [parts[:, B * D * k: B * D * (k + 1)].rearrange("p (b d) -> p b d", b=B) for k in range(2)]

        moe_w = [wall[:, :].rearrange("p (e n) -> p e n", e=16),
                 wall[:, 0:8 * 1216].rearrange("p (e n) -> p e n", e=8)]
        at1 = 8 * 1216
        sgu = wall[:, at1: at1 + 1408].rearrange("p (c n) -> p c n", c=2)
        sdn = wall[:, at1 + 1408: at1 + 2176].rearrange("p (c n) -> p c n", c=3)
        at1 += 2176
        ctx_l = cT[:, :, :].rearrange("p c (b n) -> p c b n", b=B)
        kv = [wall[:, at1 + 2048 + 1024 * i: at1 + 3072 + 1024 * i].rearrange("p (c n) -> p c n", c=2)
              for i in range(2)]
        toep = [wall[:, at1 + 4096 + 256 * i: at1 + 4352 + 256 * i] for i in range(TB)]
        prod = [wall[:, at1 + 5120 + 512 * i: at1 + 5632 + 512 * i] for i in range(2)]
        convT = wall[:, at1 + 6144: at1 + 8192].rearrange("p (c b n) -> p c b n", c=2, b=B)
        at1 += 8192
        sh_g = [wall[:, at1 + 352 * i: at1 + 352 * (i + 1)] for i in range(2)]
        sh_h = [wall[:, at1 + 704 + 352 * i: at1 + 704 + 352 * (i + 1)] for i in range(2)]
        sh_T = [wall[:, at1 + 1408 + 384 * i: at1 + 1408 + 384 * (i + 1)] for i in range(2)]
        x_tiles = wall[:, at1 + 2176: at1 + 2176 + D * MOE[1]["tiles"]].rearrange("p (t d) -> p t d", d=D)
        at_c = 6 * 2048
        kpad = wall[0:HC, at_c:at_c + P - 1 + LC]
        d_col = wall[0:HC, at_c + 384:at_c + 385]

        names = ("x_in const_in ctx_in proj_in attn_const_in route_const_in stack_zero h_out neg_set "
                 "stats_done var_done rstd_done "
                 "h_done tr_done tr_copied qk_proj qk_copied qk_split v_proj v_copied half_copied half_turned "
                 "s_done s_reduced mT_done mneg_done m_split st_done exp_done pv_done v_ready norm_done "
                 "oT_done oT_copied wo_done x_added const_rows dve_chain pool_chain act_chain "
                 "lay1_in ctxl_in kv_done conv_done conv_used kpad_in kpad_done kpad_out convT_done back_done back_added "
                 "out_done sh_up sh_sil sh_act sh_tr sh_trc sh_dn sh_dn_used").split()
        S = {n: sem(n) for n in names}
        stack_in = [sem(f"stack_in_{p}") for p in range(BUFS)]
        parts_out = [sem(f"parts_out_{h}") for h in range(2)]
        m_in = [sem(f"m_in_{p}") for p in range(BUFS)]
        expert_in = sem("expert_in")
        toep_in = [sem(f"toep_in_{p}") for p in range(TB)]
        M = []
        for L in range(2):
            mn = ("logit_done logit_copied top_done prob_exp hot_done rank_done cnt_done places_done "
                  "rows_done slot_done rows_in "
                  "experts_found w1_staged xT_done xT_copied w1_done sil_done act_done hT_done hT_copied "
                  "w2_done y_done combined").split()
            m = {n: sem(f"moe{L}_{n}") for n in mn}
            m["xin"] = [sem(f"moe{L}_xin{p}") for p in range(2)]
            m["stored"] = [sem(f"moe{L}_stored{p}") for p in range(2)]
            m["gathered"] = [sem(f"moe{L}_gathered{i}") for i in range(B // 2)]
            M.append(m)

        block = ctx.enter_context(nc.Block())

        class Chain:

            def __init__(self, eng, s):
                self.eng, self.s, self.n, self.dyn = eng, s, 0, 0

            def link(self, ins):
                self.n += 1
                ins.then_inc(self.s, 1)
                self.eng.wait_ge(self.s, self.dyn + self.n)

        def stack_load(sp, b, p, wait=True):
            if wait:
                sp.wait_ge(S["s_done"], 16 * b - 15)
            ts = slice(P * b, P * b + P) if isinstance(b, int) else bass.ds(b * P, P)
            sp.dma_start(k_stack[p][0:6 * HD].rearrange("p g s t -> p (g s) t"),
                         kd[:, :, :, :, ts].rearrange("r d g s t -> (r d) (g s) t")).then_inc(stack_in[p], 16)
            for r0, n in ((0, 3), (24, 2), (40, 1)):
                sp.dma_start(q_stack[p][r0:r0 + HD * n, :].rearrange("p (h t) -> p h t", h=H0),
                             qd[0:n, :, :, ts].rearrange("j d h t -> (j d) h t")).then_inc(stack_in[p], 16)

        STACKED = 16 * 4

        def rows_out(sp, n):
            for b in range(0, B, 2):
                sp.wait_ge(S["h_done"], n * B + b + 2)
                sp.dma_start(hd[P * b:P * (b + 2), :].rearrange("(b p) d -> p b d", p=P), h_sb[:, b:b + 2, :]
                             ).then_inc(S["h_out"], 16)

        def results_in(sp, L):
            m, n = M[L], MOE[L]["tiles"]
            sp.wait_ge(m["stored"][0], 16 * ((n + 1) // 2))
            sp.wait_ge(m["stored"][1], 16 * (n // 2))
            for b in range(0, B, 2):
                for k in range(2):
                    sp.dma_start(y_in[k][:, b:b + 2, :],
                                 yd[T * k + P * b:T * k + P * (b + 2), :].rearrange("(b p) d -> p b d", p=P)
                                 ).then_inc(m["gathered"][b // 2], 16)

        @block.sync
        def _(sp):
            sp.dma_start(cT[:, :, :], a["ctx_d"]).then_inc(S["ctx_in"], 16)
            sp.dma_start(wq, a["wq"]).then_inc(S["proj_in"], 16)
            sp.dma_start(wk, a["wk"]).then_inc(S["proj_in"], 16)
            for b in range(0, B, 2):
                sp.dma_start(x_sb[:, b:b + 2, :], a["x"][b:b + 2].rearrange("b p d -> p b d")).then_inc(S["x_in"], 16)
            sp.dma_start(identf[:, :], a["identf"]).then_inc(S["const_in"], 16)
            sp.dma_start(wv, a["wv"]).then_inc(S["const_in"], 16)
            sp.dma_start(tri[:, :], a["tri"]).then_inc(S["route_const_in"], 16)
            sp.dma_start(ramp[:, :], a["ramp"]).then_inc(S["route_const_in"], 16)
            sp.dma_start(wo[:, :, :], a["wo"]).then_inc(S["attn_const_in"], 16)
            sp.dma_start(masks[:, :, :], a["masks"]).then_inc(S["attn_const_in"], 16)
            sp.dma_start(identb[:, :], a["identb"]).then_inc(S["attn_const_in"], 16)
            sp.dma_start(router[:, :, :], a["router"]).then_inc(S["attn_const_in"], 16)
            sp.dma_start(router1[:, :, :], a["gate_w"]).then_inc(S["attn_const_in"], 16)
            sp.wait_ge(S["stack_zero"], 2)
            for p in range(BUFS):
                sp.dma_start(q_stack[p][SLOPE:SLOPE + 3, :], a["slope_rows"]).then_inc(S["const_rows"], 16)
                sp.dma_start(k_stack[p][SLOPE:SLOPE + 3], a["key_rows"][0:3]).then_inc(S["const_rows"], 16)
                sp.dma_start(k_stack[p][NS:NQ], a["key_rows"][3:6]).then_inc(S["const_rows"], 16)
            sp.dma_start(kpad, a["kpad"]).then_inc(S["kpad_in"], 16)
            sp.dma_start(d_col, a["D"]).then_inc(S["kpad_in"], 16)
            for u in range(6):
                hf, m = divmod(u, 3)
                ts = slice(HALF * hf, HALF * (hf + 1))
                sp.wait_ge(S["qk_split"], u + 1)
                if m < 2:
                    sp.dma_start(qd[:, 4 * m:4 * m + 4, :, ts].rearrange("j d h t -> (d h) j t"),
                                 q_parts[:, :, m, ts]).then_inc(parts_out[hf], 16)
                else:
                    for j, r0, n in ((0, 0, 3), (1, 3, 2), (2, 5, 1)):
                        sp.dma_start(kd[r0:r0 + n, :, :, :, ts].rearrange("r d g s t -> (d g s) r t"),
                                     k_parts[:, j, ts].unsqueeze(1).to_broadcast([P, n, HALF])
                                     ).then_inc(parts_out[hf], 16)
                if u == 2:
                    sp.wait_ge(parts_out[0], 5 * 16)
                    stack_load(sp, 0, 0, wait=False)
                    stack_load(sp, 1, 1, wait=False)
            sp.wait_ge(parts_out[1], 5 * 16)
            sp.wait_ge(S["kpad_done"], 1)
            sp.dma_start(kc, kpad).then_inc(S["kpad_out"], 16)
            sp.wait_ge(S["kpad_out"], 16)

            def experts(e, n):
                es = slice(e, e + n) if isinstance(e, int) else bass.ds(e, n)
                sp.dma_start(moe_w[0][:, es, :], a["w_moe0"][:, es, :]).then_inc(expert_in, 16)

            experts(0, 3)
            with sp.Fori(0, 2) as i:
                stack_load(sp, 2 + BUFS * i, 2)
                stack_load(sp, 3 + BUFS * i, 0)
                experts(3 * i + 3, 3)
                stack_load(sp, 4 + BUFS * i, 1)
            sp.wait_ge(S["pv_done"], 2 * B)
            experts(9, 3)
            rows_out(sp, 1)
            experts(12, 4)
            sp.wait_ge(S["x_added"], B)
            sp.dma_start(ctx_l, a["ctx_l"]).then_inc(S["ctxl_in"], 16)
            sp.wait_ge(M[0]["w2_done"], MOE[0]["tiles"])

            def toep_load(h, p, first=False):
                if not first:
                    sp.wait_ge(S["conv_done"], 2 * h - 6)
                src = bass.AP(tensor=kc.tensor, offset=h * (P - 1 + LC), ap=[[1, P], [1, LC]])
                sp.dma_start(toep[p], src).then_inc(toep_in[p], 16)

            for h in range(TB):
                toep_load(h, h, True)
            results_in(sp, 0)
            sp.dma_start(moe_w[1], a["w_moe1"]).then_inc(S["lay1_in"], 16)
            sp.dma_start(sgu, a["sgu"]).then_inc(S["lay1_in"], 16)
            sp.dma_start(sdn, a["sdn"]).then_inc(S["lay1_in"], 16)
            with sp.Fori(1, HC // TB) as i:
                for k in range(TB):
                    toep_load(TB * i + k, k)
            rows_out(sp, 3)
            results_in(sp, 1)
            for b in range(B):
                sp.wait_ge(M[1]["combined"], 2 * (b - b % 2) + 3 + b % 2)
                sp.dma_start(out[b], x_sb[:, b, :]).then_inc(S["out_done"], 16)
            sp.wait_ge(S["out_done"], 16 * B)

        NORM_PARTS = [(0, 0, B), (1, 0, B - 1), (1, B - 1, B), (2, 0, B // 2), (2, B // 2, B),
                      (3, 0, B // 2), (3, B // 2, B)]

        def pow_rstd(pool, n):
            for i, (norm, lo, hi) in enumerate(NORM_PARTS):
                if norm == n:
                    pool.wait_ge(S["var_done"], i + 1)
                    pool.tensor_tensor(rstd[:, lo:hi], vare[:, lo:hi], neghalf[:, lo:hi], ALU.pow
                                       ).then_inc(S["rstd_done"], 1)

        def moe_pool(pool, L):
            m, n = M[L], MOE[L]["tiles"]
            pool.wait_ge(S["h_out"], 16 * 4 * (L + 1))
            pool.wait_ge(m["slot_done"], 1)

            def gather(t):
                to, ready = (xt[t % 2], m["xin"][t % 2]) if L == 0 else (x_tiles[:, t, :], m["rows_in"])
                if L == 0 and t >= 2:
                    pool.wait_ge(m["xT_done"], t - 1)
                pool.indirect_dma_start(to, None, hd[:, :], bass.IndirectOffsetOnAxis(src_row[:, t:t + 1], 0)
                                        ).then_inc(ready, 16)

            def scatter(t):
                p = t % 2
                pool.wait_ge(m["y_done"], t + 1)
                pool.indirect_dma_start(yd[:, :], bass.IndirectOffsetOnAxis(dst_row[:, t:t + 1], 0), y_sb[p], None
                                        ).then_inc(m["stored"][p], 16)

            if L == 0:
                for t in range(3):
                    gather(t)
                for t in range(n):
                    if t + 3 < n:
                        gather(t + 3)
                    scatter(t)
            else:
                for t in range(n):
                    gather(t)
                for t in range(n):
                    scatter(t)

        @block.gpsimd
        def _(pool):
            pool.memset(neghalf[:, :], -0.5).then_inc(S["neg_set"], 1)
            pool.memset(onesb[:, :], 1.0).then_inc(S["neg_set"], 1)
            pool.memset(v_buf[:, :, :, :, HD + 1:VC], 0.0).then_inc(S["neg_set"], 1)
            pool.memset(v_buf[:, :, :, :, HD:HD + 1], 1.0).then_inc(S["neg_set"], 1)
            pool.memset(wall[:, att:at_k], 0.0).then_inc(S["stack_zero"], 1)
            pool.memset(wall[:, at_k:at_p], 0.0).then_inc(S["stack_zero"], 1)
            pool.wait_ge(S["neg_set"], 1)
            pow_rstd(pool, 0)
            pool.wait_ge(S["neg_set"], 4)

            def v_copy(b, p, first=False):
                if not first:
                    pool.wait_ge(S["pv_done"], 2 * b - 3)
                src = (v_all[:, b] if isinstance(b, int)
                       else v_all[:, bass.ds(b, 1)].rearrange("p o s g d -> p (o s) g d"))
                pool.tensor_copy(v_buf[:, p, :, :, 0:HD], src).then_inc(S["v_ready"], 1)

            pool.wait_ge(S["v_copied"], 2 * B)
            v_copy(0, 0, True)
            v_copy(1, 1, True)
            with pool.Fori(0, 2) as i:
                for o in (2, 3, 4):
                    v_copy(o + BUFS * i, o % BUFS)
            pow_rstd(pool, 1)
            moe_pool(pool, 0)
            pool.wait_ge(S["ctxl_in"], 16)
            pool.wait_ge(M[0]["w2_done"], MOE[0]["tiles"])

            def products(h, p, first=False):
                if not first:
                    pool.wait_ge(S["conv_done"], 2 * (h - 1))
                cols = slice(CW * h, CW * h + CW) if isinstance(h, int) else bass.ds(h * CW, CW)
                for c in range(2):
                    k = ctx_l[:, c, :, cols]
                    pool.tensor_tensor(kv[p][:, c, :].rearrange("p (b i j) -> p b i j", b=B, i=CW),
                                       k.unsqueeze(3).to_broadcast([P, B, CW, CW]),
                                       k.unsqueeze(2).to_broadcast([P, B, CW, CW]),
                                       ALU.mult).then_inc(S["kv_done"], 1)

            products(0, 0, True)
            products(1, 1, True)
            products(2, 0)
            pow_rstd(pool, 2)
            with pool.Fori(1, HC // 2 - 1) as i:
                products(2 * i + 1, 1)
                products(2 * i + 2, 0)
            products(HC - 1, 1)
            pow_rstd(pool, 3)
            moe_pool(pool, 1)

        UNITS = [4, 4, 4, 4, 0, 0, 0, 0]
        UNITS_FIRST = [10, 2, 2, 2, 0, 0, 0, 0]

        class Norm:

            def __init__(self, dve):
                self.dve, self.n_stats, self.n_var, self.n_h = dve, 0, 0, 0

            def statistics(self, b):
                self.dve.bn_stats(stats[:, b, :], x_sb[:, b, :]).then_inc(S["stats_done"], 1)
                self.n_stats += 1

            def variance(self):
                lo, hi = NORM_PARTS[self.n_var][1:]
                self.dve.wait_ge(S["stats_done"], self.n_stats)
                for b in range(lo, hi):
                    self.dve.bn_aggr(mv[:, b, :], stats[:, b, :]).then_inc(S["stats_done"], 1)
                self.n_stats += hi - lo
                self.dve.wait_ge(S["stats_done"], self.n_stats)
                self.dve.tensor_scalar(vare[:, lo:hi], mv[:, lo:hi, 1], EPS, None, ALU.add
                                       ).then_inc(S["var_done"], 1)
                self.n_var += 1

            def rescale(self):
                lo, hi = NORM_PARTS[self.n_h][1:]
                self.n_h += 1
                self.dve.wait_ge(S["rstd_done"], self.n_h)
                for b in range(lo, hi):
                    self.dve.tensor_scalar(h_sb[:, b, :], x_sb[:, b, :], mv[:, b, 0:1], rstd[:, b:b + 1],
                                           ALU.subtract, ALU.mult).then_inc(S["h_done"], 1)

        def add_and_norm(norm, add):
            half, three = B // 2, 3 * B // 4
            add(0, half)
            for b in range(half):
                norm.statistics(b)
            norm.variance()
            add(half, three)
            norm.rescale()
            add(three, B)
            for b in range(half, B):
                norm.statistics(b)
            norm.variance()
            norm.rescale()

        def moe_vector(dve, chain, L):
            m, E, n = M[L], MOE[L]["E"], MOE[L]["tiles"]
            lg, ho, hb, ba = logits[:, :, 0:E], hot[:, :, :, 0:E], hotb[:, :, 0:E], base[:, :, 0:E]

            def over_e(ap):
                return ap.unsqueeze(2).to_broadcast([P, B, E])

            dve.wait_ge(S["route_const_in"], 32)
            dve.wait_ge(m["logit_done"], B)
            src = bk(0)[:, 0:B * E].rearrange("p (b e) -> p b e", b=B)
            if L == 0:
                chain.link(dve.tensor_copy(lg, src))
            else:
                chain.link(dve.tensor_reduce(ptmp[:, 0, :], src, AX.X, ALU.max))
                chain.link(dve.tensor_tensor(ba, src, over_e(ptmp[:, 0, :]), ALU.subtract))
                dve.tensor_copy(ptmp[:, 1, :], ptmp[:, 0, :]).then_inc(m["logit_copied"], 1)
                dve.wait_ge(m["prob_exp"], 1)
                chain.link(dve.tensor_reduce(ptmp[:, 2, :], lg, AX.X, ALU.add))
                chain.link(dve.reciprocal(ptmp[:, 3, :], ptmp[:, 2, :]))
                chain.link(dve.tensor_tensor(lg, lg, over_e(ptmp[:, 3, :]), ALU.mult))
            for b in range(B):
                dve.max(top[:, b, :], logits[:, b, 0:E]).then_inc(m["top_done"], 1)
            dve.wait_ge(m["top_done"], B)
            for b in range(B):
                dve.max_index(topi[:, b, :], top[:, b, :], logits[:, b, 0:E]).then_inc(m["top_done"], 1)
            dve.wait_ge(m["top_done"], 2 * B)
            if L == 0:
                dve.tensor_tensor(ptmp[:, 0, :], top[:, :, 1], top[:, :, 0], ALU.subtract
                                  ).then_inc(m["logit_copied"], 1)
            else:
                chain.link(dve.tensor_copy(pw[:, 0, :], top[:, :, 0]))
                chain.link(dve.tensor_copy(pw[:, 1, :], top[:, :, 1]))
            for k in range(2):
                chain.link(dve.tensor_copy(idxf[:, k, :], topi[:, :, k]))
                chain.link(dve.tensor_tensor(ho[:, k], iota[:, 0:E].unsqueeze(1).to_broadcast([P, B, E]),
                                             over_e(idxf[:, k, :]), ALU.is_equal))
            dve.tensor_tensor(hb, ho[:, 0], ho[:, 1], ALU.add).then_inc(m["hot_done"], 1)
            if L == 0:
                dve.wait_ge(m["prob_exp"], 1)
                chain.link(dve.tensor_scalar(ptmp[:, 2, :], ptmp[:, 1, :], 1.0, None, ALU.add))
                chain.link(dve.reciprocal(pw[:, 0, :], ptmp[:, 2, :]))
                chain.link(dve.tensor_tensor(pw[:, 1, :], ptmp[:, 1, :], pw[:, 0, :], ALU.mult))
            nst = T // P
            if L == 0:
                chain.link(dve.tensor_copy(iotab[:, :], iota[:, :]))
            dve.wait_ge(m["cnt_done"], 1)
            chain.link(dve.tensor_copy(cnt[:, 0, 0:E], bk(2)[:, 0:E]))
            if L == 1:
                shared_gate(dve, 0)
                shared_gate(dve, 1)
            c3 = cmp[:, 0:E * nst].rearrange("p (e s) -> p e s", e=E)
            chain.link(dve.tensor_scalar(cnt[:, 1, 0:nst], iota[:, 0:nst], float(P), None, ALU.mult))
            chain.link(dve.tensor_tensor(c3, cnt[:, 0, 0:E].unsqueeze(2).to_broadcast([P, E, nst]),
                                         cnt[:, 1, 0:nst].unsqueeze(1).to_broadcast([P, E, nst]), ALU.is_gt))
            chain.link(dve.tensor_reduce(cnt[:, 2, 0:E], c3, AX.X, ALU.add))
            chain.link(dve.tensor_tensor_scan(cnt[:, 3, 0:E], cnt[:, 2, 0:E], cnt[:, 2, 0:E], 0.0,
                                              ALU.add, ALU.bypass))
            chain.link(dve.tensor_tensor(cnt[:, 2, 0:E], cnt[:, 3, 0:E], cnt[:, 2, 0:E], ALU.subtract))
            chain.link(dve.tensor_scalar(cnt[:, 2, 0:E], cnt[:, 2, 0:E], float(P), None, ALU.mult))
            dve.wait_ge(m["rank_done"], 1)
            rank = bk(1)[:, 0:B * E].rearrange("p (b e) -> p b e", b=B)
            chain.link(dve.tensor_tensor(ba, rank, cnt[:, 2, 0:E].unsqueeze(1).to_broadcast([P, B, E]), ALU.add))
            for k in range(2):
                chain.link(dve.tensor_tensor(ho[:, k], ho[:, k], ba, ALU.mult))
                chain.link(dve.tensor_reduce(slotf[:, k, :], ho[:, k], AX.X, ALU.add))
            sl = slotf[:, :, :].rearrange("p k b -> p (k b)")
            chain.link(dve.tensor_scalar(in_tile[:, 1, :], sl, -(P - 1) / 2.0, 1.0 / P, ALU.add, ALU.mult))
            chain.link(dve.tensor_scalar(in_tile[:, 0, :], in_tile[:, 1, :], 1.5 * 2 ** 23, None, ALU.add))
            chain.link(dve.tensor_scalar(in_tile[:, 0, :], in_tile[:, 0, :], -1.5 * 2 ** 23, None, ALU.add))
            chain.link(dve.scalar_tensor_tensor(in_tile[:, 1, :], in_tile[:, 0, :], -float(P), sl,
                                                ALU.mult, ALU.add))
            dve.tensor_tensor(tile_hot[:, :, 0:n], iota[:, 0:n].unsqueeze(1).to_broadcast([P, 2 * B, n]),
                              in_tile[:, 0, :].unsqueeze(2).to_broadcast([P, 2 * B, n]), ALU.is_equal
                              ).then_inc(m["places_done"], 1)
            for c in range(B):
                dve.tensor_scalar(place_hot[:, c, :], iotab[:, :], in_tile[:, 1, c:c + 1], None, ALU.is_equal
                                  ).then_inc(m["places_done"], 1)
            dve.wait_ge(m["places_done"], 1)
            dve.tensor_scalar(tile_rows[:, :, 0, 0:n], tile_hot[:, :, 0:n], row_no, None, ALU.mult
                              ).then_inc(m["places_done"], 1)
            dve.tensor_tensor(tile_rows[:, :, 1, 0:n], tile_hot[:, :, 0:n],
                              choice_no.unsqueeze(2).to_broadcast([P, 2 * B, n]), ALU.mult
                              ).then_inc(m["places_done"], 1)
            for c in range(B, 2 * B):
                dve.tensor_scalar(place_hot[:, c, :], iotab[:, :], in_tile[:, 1, c:c + 1], None, ALU.is_equal
                                  ).then_inc(m["places_done"], 1)
            dve.wait_ge(m["rows_done"], 1)
            by = [by_slot[:, i, 0:n] for i in range(6)]
            chain.link(dve.tensor_copy(by_slot[:, 0:2, 0:n], bk(3)[:, 0:2 * n].rearrange("p (v n) -> p v n", v=2)))
            chain.link(dve.scalar_tensor_tensor(by[2], by[1], float(P), by[0], ALU.mult, ALU.add))
            chain.link(dve.scalar_tensor_tensor(by[3], by[1], 0.0, unused[:, 0:n], ALU.is_equal, ALU.mult))
            chain.link(dve.scalar_tensor_tensor(dst_row[:, 0:n], by[2], -float(P), by[3], ALU.add, ALU.add))
            chain.link(dve.tensor_scalar(by[4], by[2], float(T + P), float(-T), ALU.is_ge, ALU.mult))
            chain.link(dve.scalar_tensor_tensor(by[5], by[2], -float(P), by[4], ALU.add, ALU.add))
            dve.tensor_scalar(src_row[:, 0:n], by[5], 0.0, None, ALU.max).then_inc(m["slot_done"], 1)
            c3 = cmp[:, 0:n * E].rearrange("p (t e) -> p t e", t=n)
            chain.link(dve.tensor_tensor(c3, cnt[:, 3, 0:E].unsqueeze(1).to_broadcast([P, n, E]),
                                         iota[:, 0:n].unsqueeze(2).to_broadcast([P, n, E]), ALU.is_le))
            chain.link(dve.tensor_reduce(etf[:, 0:n], c3, AX.X, ALU.add))
            chain.link(dve.tensor_scalar(etf[:, 0:n], etf[:, 0:n], float(E - 1), None, ALU.min))
            dve.tensor_copy(et[:, 0:n], etf[:, 0:n]).then_inc(m["experts_found"], 1)
            if L == 0:
                def stage_w1(t, p, first=False):
                    e = dve.value_load(et[0:1, t:t + 1] if isinstance(t, int) else et[0:1, bass.ds(t, 1)],
                                       min_val=0, max_val=E - 1)
                    if not first:
                        dve.wait_ge(m["w1_done"], t - 1)
                    dve.tensor_copy(w1_now[p], moe_w[0][:, bass.ds(e, 1), 0:KD * 512].rearrange("p o n -> p (o n)")
                                    ).then_inc(m["w1_staged"], 1)

                dve.wait_ge(m["experts_found"], 1)
                dve.wait_ge(expert_in, 16 * 5)
                dve.wait_ge(S["h_out"], 16 * 4)
                stage_w1(0, 0, True)
                stage_w1(1, 1, True)
                with dve.Fori(1, n // 2) as i:
                    stage_w1(2 * i, 0)
                    stage_w1(2 * i + 1, 1)
                stage_w1(n - 1, 0)
                return
            shared_vector(dve)

            def hT_copy(t, p, first=False):
                dve.wait_ge(m["hT_done"], t + 1)
                if not first:
                    dve.wait_ge(m["w2_done"], t - 1)
                dve.tensor_copy(hTs[p][:, 0:P], bk(2 + p)[:, 0:P]).then_inc(m["hT_copied"], 1)
                dve.tensor_copy(hTs[p][0:48, P:2 * P], bk(2 + p)[0:48, P:2 * P]).then_inc(m["hT_copied"], 1)

            def gate(t, p, first=False):
                dve.wait_ge(m["sil_done"], t + 1)
                if not first:
                    dve.wait_ge(m["hT_done"], t - 1)
                dve.tensor_tensor(act_h[p][:, 0:176], gs[p], bk(p)[:, 176:352], ALU.mult
                                  ).then_inc(m["act_done"], 1)

            def step(t, p, first=False, last=False):
                hT_copy(t, p, first)
                if not last:
                    gate(t + 1, 1 - p, first and p == 0)

            gate(0, 0, True)
            for t in range(TU):
                step(t, t % 2, t < 2)
            with dve.Fori(1, n // TU) as i:
                for k in range(TU):
                    step(TU * i + k, k % 2)
            for t in range(n - 3, n):
                step(t, t % 2, last=(t == n - 1))

        def combine(dve, L, lo, hi):
            m = M[L]
            for k in range(2):
                for b in range(lo, hi):
                    dve.wait_ge(m["gathered"][b // 2], 32)
                    if k == 1:
                        dve.wait_ge(m["combined"], lo + b + 1)
                    dve.scalar_tensor_tensor(x_sb[:, b, :], y_in[k][:, b, :], pw[:, k, b:b + 1],
                                             x_sb[:, b, :], ALU.mult, ALU.add).then_inc(m["combined"], 1)
            dve.wait_ge(m["combined"], 2 * hi)

        def shared_vector(dve):
            shared_add(dve, 0)
            for b in range(2, B):
                shared_gate(dve, b)
                shared_add(dve, b - 1)
            shared_add(dve, B - 1)

        def shared_gate(dve, b):
            p = b % 2
            dve.wait_ge(S["sh_sil"], b + 1)
            if b >= 2:
                dve.wait_ge(S["sh_tr"], b - 1)
            dve.tensor_tensor(sh_h[p], sh_g[p], bk(4 + 2 * p)[:, 0:352], ALU.mult).then_inc(S["sh_act"], 1)

        def shared_add(dve, b):
            dve.wait_ge(S["sh_dn"], b + 1)
            dve.tensor_tensor(x_sb[:, b, :], x_sb[:, b, :], bk(0)[:, 256:512], ALU.add
                              ).then_inc(S["sh_dn_used"], 1)

        @block.vector
        def _(dve):
            chain = Chain(dve, S["dve_chain"])
            dve.wait_ge(S["x_in"], 16 * B // 2)
            norm = Norm(dve)
            for b in range(B):
                norm.statistics(b)
            norm.variance()
            norm.rescale()
            for u in range(6):
                hf, m = divmod(u, 3)
                ts = slice(HALF * hf, HALF * (hf + 1))
                part = [q_parts[:, j, m, ts] if m < 2 else k_parts[:, j, ts] for j in range(3)]
                dve.wait_ge(S["qk_copied"], u + 1)
                chain.link(dve.tensor_copy(part[0], pf[u % 2]))
                chain.link(dve.tensor_tensor(pr[u % 2], pf[u % 2], part[0], ALU.subtract))
                chain.link(dve.tensor_copy(part[1], pr[u % 2]))
                dve.tensor_tensor(part[2], pr[u % 2], part[1], ALU.subtract).then_inc(S["qk_split"], 1)
            for u in range(2):
                dve.wait_ge(S["v_proj"], u + 1)
                for b in range(4 * u, 4 * u + 4):
                    for s in range(2):
                        dve.tensor_copy(v_all[:, b, s, :, :],
                                        bk(6 + u)[:, P * (b % 4) + 64 * s: P * (b % 4) + 64 * s + 64]
                                        .rearrange("p (g d) -> p g d", g=G0)).then_inc(S["v_copied"], 1)

            dve.wait_ge(S["kpad_in"], 32)
            dve.tensor_tensor(kpad[:, P - 1:P], kpad[:, P - 1:P], d_col, ALU.add).then_inc(S["kpad_done"], 1)

            def reduce(b, p, u):
                dve.wait_ge(S["s_done"], 16 * b + u + 1)
                dve.tensor_reduce(mx[:, p, 2 * u:2 * u + 2],
                                  bk(u % 2).rearrange("p (h k) -> p h k", h=2), AX.X, ALU.max
                                  ).then_inc(S["s_reduced"], 1)

            def split_max(b, p):
                dve.wait_ge(S["mT_done"], b + 1)
                ins = dve.tensor_scalar(mneg[:, :], bk(3)[0:H0, 0:P], -1.0, None, ALU.mult)
                ins.then_inc(S["mneg_done"], 1)
                dve.wait_ge(S["mneg_done"], b + 1)
                chain.link(dve.tensor_copy(msplit[:, p, 0, :], mneg[:, :]))
                chain.link(dve.tensor_tensor(mres[:, :], mneg[:, :], msplit[:, p, 0, :], ALU.subtract))
                chain.link(dve.tensor_copy(msplit[:, p, 1, :], mres[:, :]))
                dve.tensor_tensor(msplit[:, p, 2, :], mres[:, :], msplit[:, p, 1, :],
                                  ALU.subtract).then_inc(S["m_split"], 1)

            def normalise(b, hh):
                o = bk(2).rearrange("p (j g d) -> p g j d", j=HG, g=4)
                dve.wait_ge(S["half_turned"], 2 * b + hh + 1)
                if hh == 0:
                    dve.wait_ge(S["oT_done"], b)
                rd = rden[:, 16 * hh:16 * hh + 16].rearrange("p (g j) -> p g j", g=4)
                chain.link(dve.reciprocal(rd, o[:, :, :, HD]))
                dve.tensor_tensor(onorm[:, 16 * hh:16 * hh + 16, :].rearrange("p (g j) d -> p g j d", g=4),
                                  o[:, :, :, 0:HD], rd.unsqueeze(3).to_broadcast([P, 4, HG, HD]), ALU.mult
                                  ).then_inc(S["norm_done"], 1)

            def add_attention(b):
                dve.wait_ge(S["wo_done"], b + 1)
                xb = x_sb[:, b, :] if isinstance(b, int) else x_sb[:, bass.ds(b, 1), :].rearrange("p o d -> p (o d)")
                dve.tensor_tensor(xb, xb, bk(3)[:, 256:512], ALU.add).then_inc(S["x_added"], 1)

            def count_in(b):
                dve.wait_ge(S["x_added"], b + 1)
                at_b = slice(b, b + 1) if isinstance(b, int) else bass.ds(b, 1)
                dve.bn_stats(stats[:, at_b, :].rearrange("p o s -> p (o s)"),
                             x_sb[:, at_b, :].rearrange("p o d -> p (o d)")).then_inc(S["stats_done"], 1)

            def body(b, o, first=False, last=False):
                pn = (o + 1) % BUFS
                u = 0
                for g in range(G0):
                    if not last:
                        for _ in range((UNITS_FIRST if first else UNITS)[g]):
                            reduce(b + 1, pn, u)
                            u += 1
                    if g == 1 and not first:
                        normalise(b - 1, 1)
                    if g == 3 and not first:
                        add_attention(b - 1)
                    if g == 4 and not last:
                        split_max(b + 1, pn)
                    if g == 4 and not first:
                        count_in(b - 1)
                    if g == 5:
                        normalise(b, 0)

            for u in range(16):
                reduce(0, 0, u)
            split_max(0, 0)
            body(0, 0, first=True)
            n0 = chain.n
            with dve.Fori(0, 2) as i:
                per = 15
                chain.dyn = i * per
                for o in (1, 2, 3):
                    body(o + BUFS * i, o)
                assert chain.n == n0 + per, (chain.n, n0)
            chain.n, chain.dyn = n0 + 2 * per, 0
            body(7, 1, last=True)
            norm.n_stats += B - 1
            norm.variance()
            norm.rescale()
            normalise(7, 1)
            add_attention(7)
            dve.wait_ge(S["x_added"], B)
            norm.statistics(B - 1)
            norm.variance()
            norm.rescale()
            moe_vector(dve, chain, 0)
            add_and_norm(norm, lambda lo, hi: combine(dve, 0, lo, hi))

            def weigh(h, k):
                cols = slice(CW * h, CW * h + CW) if isinstance(h, int) else bass.ds(h * CW, CW)
                pv = [prod[c].rearrange("p (b j i) -> p b j i", b=B, j=CW) for c in range(2)]
                for c in range(2):
                    dve.wait_ge(S["conv_done"], 2 * h + c + 1)
                    if not (isinstance(h, int) and h == 0):
                        dve.wait_ge(S["convT_done"], 2 * h - 1 + c)
                    q = hT[:, c, :].rearrange("p (b n) -> p b n", b=B)[:, :, cols]
                    y = bk(2 * k + c).rearrange("p (b i j) -> p b j i", b=B, i=CW)
                    dve.tensor_tensor(pv[c], y, q.unsqueeze(2).to_broadcast([P, B, CW, CW]), ALU.mult
                                      ).then_inc(S["conv_used"], 1)
                for c in range(2):
                    dve.wait_ge(S["conv_used"], 2 * h + c + 1)
                    dve.tensor_reduce(convT[:, c, :, cols], pv[c], AX.X, ALU.add).then_inc(S["convT_done"], 1)

            dve.wait_ge(S["tr_copied"], 3 * B)
            for h in range(TB):
                weigh(h, h)
            with dve.Fori(1, HC // TB) as i:
                for k in range(TB):
                    weigh(TB * i + k, k)

            def add_conv(lo, hi):
                for b in range(lo, hi):
                    dve.wait_ge(S["back_done"], b + 1)
                    dve.tensor_tensor(x_sb[:, b, :], x_sb[:, b, :], bk(4 + b % 2)[:, 0:D], ALU.add
                                      ).then_inc(S["back_added"], 1)
                dve.wait_ge(S["back_added"], hi)

            add_and_norm(norm, add_conv)
            moe_vector(dve, chain, 1)
            for b in range(0, B, 2):
                combine(dve, 1, b, b + 2)

        def copy_rows(act, n, batches=range(B)):
            for b in batches:
                act.wait_ge(S["tr_done"], n * B + b + 1)
                act.activation(hT[:, :, P * b:P * (b + 1)],
                               bk(6 + b % 2)[:, 0:2 * P].rearrange("p (c t) -> p c t", c=KD),
                               ACT.Copy).then_inc(S["tr_copied"], 1)

        def moe_scalar(act, L):
            m, n, E = M[L], MOE[L]["tiles"], MOE[L]["E"]
            act.wait_ge(m["logit_copied"], 1)
            if L == 0:
                act.activation(ptmp[:, 1, :], ptmp[:, 0, :], ACT.Exp).then_inc(m["prob_exp"], 1)
            else:
                act.activation(logits[:, :, 0:E], base[:, :, 0:E], ACT.Exp).then_inc(m["prob_exp"], 1)

                def shared_silu(b):
                    act.wait_ge(S["sh_up"], b + 1)
                    if b >= 2:
                        act.wait_ge(S["sh_act"], b - 1)
                    act.activation(sh_g[b % 2], bk(5 + 2 * (b % 2))[:, 0:352], ACT.Silu).then_inc(S["sh_sil"], 1)

                shared_silu(0)
                shared_silu(1)
                for b in range(B):
                    p = b % 2
                    act.wait_ge(S["sh_tr"], b + 1)
                    if b >= 2:
                        act.wait_ge(S["sh_dn"], b - 1)
                    act.activation(sh_T[p][:, 0:2 * P], bk(2)[:, 0:2 * P], ACT.Copy).then_inc(S["sh_trc"], 1)
                    act.activation(sh_T[p][0:96, 2 * P:3 * P], bk(2)[0:96, 2 * P:3 * P], ACT.Copy
                                   ).then_inc(S["sh_trc"], 1)
                    if b + 2 < B:
                        shared_silu(b + 2)

            def stage(t, p, first=False):
                if not first:
                    act.wait_ge(m["xT_done"], t - 1)
                src = (x_tiles[:, t, :] if isinstance(t, int)
                       else x_tiles[:, bass.ds(t, 1), :].rearrange("p o d -> p (o d)"))
                act.activation(xt[p], src, ACT.Copy).then_inc(m["xin"][p], 1)

            def xT_copy(t, p, first=False):
                act.wait_ge(m["xT_done"], t + 1)
                if not first:
                    act.wait_ge(m["w1_done"], t - 1)
                act.activation(xTs[p], bk(4 + p)[:, 0:D], ACT.Copy).then_inc(m["xT_copied"], 1)

            def silu(t, p, first=False):
                act.wait_ge(m["w1_done"], t + 1)
                if L == 0:
                    if not first:
                        act.wait_ge(m["w2_done"], t - 1)
                    act.activation(act_h[p], bk(p), ACT.Silu).then_inc(m["act_done"], 1)
                else:
                    if not first:
                        act.wait_ge(m["act_done"], t - 1)
                    act.activation(gs[p], bk(p)[:, 0:176], ACT.Silu).then_inc(m["sil_done"], 1)

            def y_copy(t, j, p, first=False):
                act.wait_ge(m["w2_done"], t + 1)
                if not first:
                    act.wait_ge(m["stored"][p], 16 * j)
                act.activation(y_sb[p], bk(6 + p)[:, 0:D], ACT.Copy).then_inc(m["y_done"], 1)

            def step(t, j, p, first=False, left=9):
                if left > 1:
                    silu(t + 1, 1 - p, first and p == 0)
                if left > 2:
                    xT_copy(t + 2, p)
                if L == 1 and left > 3:
                    stage(t + 3, 1 - p)
                y_copy(t, j, p, first)

            if L == 1:
                act.wait_ge(m["rows_in"], 16 * n)
                stage(0, 0, True)
                stage(1, 1, True)
            xT_copy(0, 0, True)
            if L == 1:
                stage(2, 0)
            silu(0, 0, True)
            xT_copy(1, 1, True)
            for t in range(TU):
                step(t, t // 2, t % 2, t < 2)
            with act.Fori(1, n // TU) as i:
                for k in range(TU):
                    step(TU * i + k, TU // 2 * i + k // 2, k % 2)
            for t in range(n - 3, n):
                step(t, t // 2, t % 2, left=n - t)

        @block.scalar
        def _(act):
            copy_rows(act, 0)
            for u in range(6):
                hf, m = divmod(u, 3)
                act.wait_ge(S["qk_proj"], u + 1)
                if u >= 2:
                    act.wait_ge(S["qk_split"], u - 1)
                act.activation(pf[u % 2], bk(u), ACT.Copy, scale=SCALE if m < 2 else 1.0
                               ).then_inc(S["qk_copied"], 1)
            act.wait_ge(S["qk_split"], 6)

            def exps(b, g):
                act.wait_ge(S["st_done"], 8 * b + g + 1)
                if not (isinstance(b, int) and b == 0):
                    act.wait_ge(S["pv_done"], 2 * b - 1 + g // 4)
                act.activation(p_buf[g], st_ps[g % 2][:, :, :].rearrange("p s n -> p (s n)"), ACT.Exp
                               ).then_inc(S["exp_done"], 1)

            def m_rows(b, p):
                act.wait_ge(S["m_split"], b + 1)
                for r in range(3):
                    act.dma_start(q_stack[p][NS + r:NS + r + 1, :].rearrange("o (h t) -> o h t", h=H0),
                                   msplit[:, p, r, :]).then_inc(m_in[p], 16)

            def copy_half(b, hh, first=False):
                act.wait_ge(S["pv_done"], 2 * b + hh + 1)
                if not first:
                    act.wait_ge(S["half_turned"], 2 * b + hh)
                act.activation(half_T, bk(2), ACT.Copy).then_inc(S["half_copied"], 1)

            def copy_oT(b):
                act.wait_ge(S["oT_done"], b + 1)
                if not (isinstance(b, int) and b == 0):
                    act.wait_ge(S["wo_done"], b)
                act.activation(oTs[:, :, :].rearrange("p c t -> p (c t)"), bk(3)[:, 0:2 * P], ACT.Copy
                               ).then_inc(S["oT_copied"], 1)

            def body(b, o, first=False, last=False):
                for g in range(G0):
                    exps(b, g)
                    if g == 0 and not first:
                        copy_half(b - 1, 1)
                    if g == 2 and not first:
                        copy_oT(b - 1)
                    if g == 4:
                        copy_half(b, 0, first)
                    if g == 5 and not last:
                        m_rows(b + 1, (o + 1) % BUFS)

            m_rows(0, 0)
            body(0, 0, first=True)
            with act.Fori(0, 2) as i:
                for o in (1, 2, 3):
                    body(o + BUFS * i, o)
            body(7, 1, last=True)
            copy_half(7, 1)
            copy_rows(act, 1, range(4))
            copy_oT(7)
            copy_rows(act, 1, range(4, B))
            moe_scalar(act, 0)
            copy_rows(act, 2)
            copy_rows(act, 3)
            moe_scalar(act, 1)

        def turn_rows(pe, n, batches=range(B), after=None):
            for b in batches:
                pe.wait_ge(S["h_done"], n * B + b + 1)
                if n * B + b >= 2:
                    pe.wait_ge(S["tr_copied"], n * B + b - 1)
                for c in range(KD):
                    ins = pe.transpose(bk(6 + b % 2)[:, P * c:P * (c + 1)], h_sb[:, b, P * c:P * (c + 1)],
                                       identf[:, :])
                ins.then_inc(S["tr_done"], 1)
                if after and b >= 1:
                    after(b - 1)

        def logits_of(pe, L, b):
            E, rw = MOE[L]["E"], router if L == 0 else router1
            pe.wait_ge(S["tr_copied"], (1 + 2 * L) * B + b + 1)
            for c in range(KD):
                ins = pe.matmul(bk(0)[:, E * b:E * (b + 1)], hT[:, c, P * b:P * (b + 1)], rw[:, c, :],
                                start=(c == 0), stop=(c == KD - 1))
            ins.then_inc(M[L]["logit_done"], 1)

        def moe_tensor(pe, L):
            m, E, n = M[L], MOE[L]["E"], MOE[L]["tiles"]
            rows, W = MOE[L]["rows"], MOE[L]["W"]
            weights = moe_w[L]
            hidden = act_h if L == 0 else hTs
            pe.wait_ge(S["route_const_in"], 32)

            if L == 1:
                turn_rows(pe, 3, after=lambda b: logits_of(pe, 1, b))
            logits_of(pe, L, B - 1)
            if L == 1:
                pe.wait_ge(S["lay1_in"], 48)
                pe.wait_ge(S["tr_copied"], 4 * B)
                shared_up(pe, 0)
                shared_up(pe, 1)
            pe.wait_ge(m["hot_done"], 1)
            hb = hotb[:, :, 0:E]
            rk = bk(1)[:, 0:B * E].rearrange("p (b e) -> p b e", b=B)
            pe.matmul(rk, tri[:, :], hb, start=True, stop=True)
            for s in range(1, B):
                ins = pe.matmul(rk[:, s:B, :], onesb[:, :], hb[:, 0:B - s, :], start=False, stop=True,
                                skip_group_check=True)
            ins.then_inc(m["rank_done"], 1)
            for b in range(B):
                ins = pe.matmul(bk(2)[:, 0:E], onesb[:, :], hb[:, b, :], start=(b == 0), stop=(b == B - 1))
            ins.then_inc(m["cnt_done"], 1)
            if L == 1:
                shared_turn(pe, 0)
                shared_down(pe, 0)
                shared_turn(pe, 1)
            for c in range(2 * B):
                pe.wait_ge(m["places_done"], B + 3 + max(0, c - B + 1))
                ins = pe.matmul(bk(3)[:, 0:2 * n].rearrange("p (v n) -> p v n", v=2), place_hot[:, c, :],
                                tile_rows[:, c, :, 0:n], start=(c == 0), stop=(c == 2 * B - 1))
            ins.then_inc(m["rows_done"], 1)
            if L == 1:
                for b in range(1, B):
                    shared_down(pe, b)
                    if b + 1 < B:
                        shared_turn(pe, b + 1)
                pe.wait_ge(S["sh_dn_used"], B)
            pe.wait_ge(m["experts_found"], 1)
            if L == 0:
                pe.wait_ge(expert_in, 16 * 5)

            def turn_x(t, j, p, first=False):
                pe.wait_ge(m["xin"][p], (16 if L == 0 else 1) * (j + 1))
                if not first:
                    pe.wait_ge(m["xT_copied"], t - 1)
                for c in range(KD):
                    ins = pe.transpose(bk(4 + p)[:, P * c:P * (c + 1)], xt[p][:, P * c:P * (c + 1)], identf[:, :])
                ins.then_inc(m["xT_done"], 1)

            def expert(t):
                col = et[0:1, t:t + 1] if isinstance(t, int) else et[0:1, bass.ds(t, 1)]
                return pe.value_load(col, min_val=0, max_val=E - 1)

            def up(t, e, p, first=False):
                pe.wait_ge(m["xT_copied"], t + 1)
                if not first:
                    pe.wait_ge(m["act_done"], t - 1)
                if L == 0:
                    pe.wait_ge(m["w1_staged"], t + 1)
                    for i in range(len(rows)):
                        for c in range(KD):
                            w0 = W * c + P * i
                            ins = pe.matmul(bk(p)[:, P * i:P * (i + 1)], w1_now[p][:, w0:w0 + P],
                                            xTs[p][:, P * c:P * (c + 1)], start=(c == 0), stop=(c == KD - 1))
                    ins.then_inc(m["w1_done"], 1)
                    return
                for c in range(KD):
                    ins = pe.matmul(bk(p)[:, 0:W], xTs[p][:, P * c:P * (c + 1)],
                                    weights[:, bass.ds(e, 1), W * c:W * (c + 1)].rearrange("p o n -> p (o n)"),
                                    start=(c == 0), stop=(c == KD - 1))
                ins.then_inc(m["w1_done"], 1)

            def turn_h(t, p, first=False):
                pe.wait_ge(m["act_done"], t + 1)
                if not first:
                    pe.wait_ge(m["hT_copied"], (t - 1) * 2)
                for c, r in enumerate(rows):
                    ins = pe.transpose(bk(2 + p)[0:r, P * c:P * (c + 1)], act_h[p][:, P * c:P * c + r], identf[:, :])
                ins.then_inc(m["hT_done"], 1)

            def down(t, e, p, first=False):
                if L == 0:
                    pe.wait_ge(m["act_done"], t + 1)
                else:
                    pe.wait_ge(m["hT_copied"], (t + 1) * 2)
                if not first:
                    pe.wait_ge(m["y_done"], t - 1)
                for c, r in enumerate(rows):
                    w0 = KD * W + D * c
                    ins = pe.matmul(bk(6 + p)[:, 0:D], hidden[p][0:r, P * c:P * (c + 1)],
                                    weights[0:r, bass.ds(e, 1), w0:w0 + D].rearrange("p o n -> p (o n)"),
                                    start=(c == 0), stop=(c == len(rows) - 1))
                ins.then_inc(m["w2_done"], 1)

            def step(t, j, p, first=False, left=9):
                e_up = expert(t + 1) if left > 1 and L == 1 else None
                e_down = expert(t)
                if L == 1:
                    turn_h(t, p, first)
                if left > 1:
                    up(t + 1, e_up, 1 - p, first and p == 0)
                if left > 2:
                    turn_x(t + 2, j + 1, p)
                down(t, e_down, p, first)

            turn_x(0, 0, 0, True)
            up(0, expert(0) if L == 1 else None, 0, True)
            turn_x(1, 0, 1, True)
            for t in range(TU):
                step(t, t // 2, t % 2, t < 2)
            with pe.Fori(1, n // TU) as i:
                for k in range(TU):
                    step(TU * i + k, TU // 2 * i + k // 2, k % 2)
            for t in range(n - 3, n):
                step(t, t // 2, t % 2, left=n - t)

        def shared_up(pe, b):
            if b >= 2:
                pe.wait_ge(S["sh_act"], b - 1)
            for n in range(2):
                for c in range(KD):
                    ins = pe.matmul(bk(4 + 2 * (b % 2) + 1 - n)[:, 0:352], hT[:, c, P * b:P * (b + 1)],
                                    sgu[:, c, 352 * n:352 * (n + 1)], start=(c == 0), stop=(c == KD - 1))
            ins.then_inc(S["sh_up"], 1)

        def shared_turn(pe, b):
            pe.wait_ge(S["sh_act"], b + 1)
            if b >= 1:
                pe.wait_ge(S["sh_trc"], 2 * b)
            for c, r in enumerate([P, P, 96]):
                ins = pe.transpose(bk(2)[0:r, P * c:P * (c + 1)], sh_h[b % 2][:, P * c:P * c + r], identf[:, :])
            ins.then_inc(S["sh_tr"], 1)
            if b + 2 < B:
                shared_up(pe, b + 2)

        def shared_down(pe, b):
            pe.wait_ge(S["sh_trc"], 2 * b + 2)
            if b >= 1:
                pe.wait_ge(S["sh_dn_used"], b)
            for c, r in enumerate([P, P, 96]):
                ins = pe.matmul(bk(0)[:, 256:512], sh_T[b % 2][0:r, P * c:P * (c + 1)], sdn[0:r, c, :],
                                start=(c == 0), stop=(c == 2))
            ins.then_inc(S["sh_dn"], 1)

        @block.tensor
        def _(pe):
            def src(c):
                return cT[:, c, :] if c < 2 else hT[:, c - 2, :]

            def project(chunks):
                for u in range(6):
                    hf, m = divmod(u, 3)
                    w = wq[:, :, P * m:P * (m + 1)] if m < 2 else wk
                    for c in chunks:
                        ins = pe.matmul(bk(u), w[:, c, :], src(c)[:, HALF * hf:HALF * (hf + 1)],
                                        start=(c == 0), stop=(c == 3))
                    if 3 in chunks:
                        ins.then_inc(S["qk_proj"], 1)

            pe.wait_ge(S["ctx_in"], 16)
            pe.wait_ge(S["proj_in"], 32)
            project([0, 1])
            pe.wait_ge(S["const_in"], 32)
            turn_rows(pe, 0)
            pe.wait_ge(S["tr_copied"], B)
            project([2, 3])
            for u in range(2):
                for b in range(4 * u, 4 * u + 4):
                    for s in range(2):
                        for c in range(2):
                            ins = pe.matmul(bk(6 + u)[:, P * (b % 4) + 64 * s:P * (b % 4) + 64 * s + 64],
                                            src(2 * s + c)[:, P * b:P * (b + 1)], wv[:, 2 * s + c, :],
                                            start=(c == 0), stop=(c == 1))
                ins.then_inc(S["v_proj"], 1)

            pe.wait_ge(S["attn_const_in"], 80)
            pe.wait_ge(S["const_rows"], 16 * 3 * BUFS)
            pe.wait_ge(S["qk_copied"], 6)
            pe.wait_ge(S["v_copied"], 2 * B)

            def scores_q(b, p, u, first=False):
                if not (first and u < 2):
                    pe.wait_ge(S["s_reduced"], 16 * b + u - 1)
                o = bk(u % 2)
                pe.matmul(o, identb[:, :], masks[:, 0, :], start=True, stop=True)
                for h in (2 * u, 2 * u + 1):
                    ins = pe.matmul(o[:, 256 * (h % 2):256 * (h % 2) + 256],
                                    q_stack[p][0:NS, P * h:P * (h + 1)],
                                    k_stack[p][0:NS, h // HG].rearrange("p s t -> p (s t)"),
                                    start=False, stop=True, skip_group_check=True)
                ins.then_inc(S["s_done"], 1)

            def turn_max(b, p, first=False):
                pe.wait_ge(S["s_reduced"], 16 * b + 16)
                if not first:
                    if not (isinstance(b, int) and b == 1):
                        pe.wait_ge(S["x_added"], b - 1)
                    pe.wait_ge(S["mneg_done"], b)
                pe.transpose(bk(3)[0:H0, 0:P], mx[:, p, :], identf[:, :]).then_inc(S["mT_done"], 1)

            def scores_k(b, p, g, step, first=False):
                if step == 0 and not (first and g < 2):
                    pe.wait_ge(S["exp_done"], 8 * b + g - 1)
                s = step // 2
                if step % 2 == 0:
                    pe.matmul(st_ps[g % 2][:, s, :], identb[:, :], masks[:, 1 + s, :], start=True, stop=False)
                    return
                ins = pe.matmul(st_ps[g % 2][:, s, :], k_stack[p][0:NQ, g, s, :],
                                q_stack[p][0:NQ, 512 * g:512 * (g + 1)], start=False, stop=True)
                if s == 1:
                    ins.then_inc(S["st_done"], 1)

            def values(b, p, hh, first=False):
                pe.wait_ge(S["exp_done"], 8 * b + 4 * hh + 4)
                if hh == 0:
                    pe.wait_ge(S["v_ready"], b + 1)
                if not first:
                    pe.wait_ge(S["norm_done"], 2 * b + hh)
                for s in range(2):
                    for c in range(4):
                        g = 4 * hh + c
                        ins = pe.matmul(bk(2)[VC * c:VC * (c + 1), :], v_buf[:, p, s, g, :],
                                        p_buf[g][:, 512 * s:512 * (s + 1)], start=(s == 0), stop=(s == 1))
                ins.then_inc(S["pv_done"], 1)

            def turn_half(b, hh):
                pe.wait_ge(S["half_copied"], 2 * b + hh + 1)
                for j in range(HG):
                    ins = pe.transpose(bk(2)[:, P * j:P * (j + 1)], half_T[:, P * j:P * (j + 1)], identf[:, :])
                ins.then_inc(S["half_turned"], 1)

            def turn_o(b):
                pe.wait_ge(S["norm_done"], 2 * b + 2)
                pe.wait_ge(S["mneg_done"], b + 2 if not (isinstance(b, int) and b == B - 1) else B)
                for c in range(KD):
                    ins = pe.transpose(bk(3)[:, P * c:P * (c + 1)],
                                       onorm[:, 16 * c:16 * c + 16, :].rearrange("p h d -> p (h d)"), identf[:, :])
                ins.then_inc(S["oT_done"], 1)

            def project_o(b):
                pe.wait_ge(S["oT_copied"], b + 1)
                for c in range(KD):
                    ins = pe.matmul(bk(3)[:, 256:512], oTs[:, c, :], wo[:, c, :], start=(c == 0), stop=(c == 1))
                ins.then_inc(S["wo_done"], 1)

            def body(b, i, o, first=False, last=False):
                p, pn = o % BUFS, (o + 1) % BUFS
                u = 0
                for g in range(G0):
                    if not last:
                        if g == 0:
                            pe.wait_ge(stack_in[pn], STACKED * (i + (o + 1) // BUFS + 1))
                    n = 0 if last else (UNITS_FIRST if first else UNITS)[g]
                    done = 0
                    for k in range(n):
                        scores_q(b + 1, pn, u)
                        u += 1
                        if g > 0 and k >= n - 4:
                            scores_k(b, p, g, done, first)
                            done += 1
                    if g == 0:
                        pe.wait_ge(m_in[p], 48 * (i + o // BUFS + 1))
                    for step in range(done, 4):
                        if g == 4 and step == 3 and not last:
                            turn_max(b + 1, pn)
                        scores_k(b, p, g, step, first)
                    if g == 0 and not first:
                        values(b - 1, (o - 1) % BUFS, 1)
                    if g == 1 and not first:
                        turn_half(b - 1, 1)
                    if g == 4:
                        values(b, p, 0, first)
                    if g == 5:
                        turn_half(b, 0)
                    if g == 2 and not first:
                        turn_o(b - 1)
                    if g == 3 and not first:
                        project_o(b - 1)

            pe.wait_ge(stack_in[0], STACKED)
            for u in range(16):
                scores_q(0, 0, u, first=True)
            turn_max(0, 0, first=True)
            body(0, 0, 0, first=True)
            with pe.Fori(0, 2) as i:
                for o in (1, 2, 3):
                    body(o + BUFS * i, i, o)
            body(7, 2, 1, last=True)
            values(7, 1, 1)

            def next_rows(lo, hi):
                turn_rows(pe, 1, range(lo, hi), lambda b: logits_of(pe, 0, b))

            next_rows(0, 2)
            turn_half(7, 1)
            next_rows(2, 4)
            turn_o(7)
            next_rows(4, 6)
            project_o(7)
            next_rows(6, 8)
            moe_tensor(pe, 0)

            def convolve(h, i, k, first=False):
                p = k % 2
                pe.wait_ge(toep_in[k], 16 * (i + 1))
                pe.wait_ge(S["kv_done"], 2 * h + 2)
                if not first:
                    pe.wait_ge(S["conv_used"], 2 * h - 6)
                pe.matmul(bk(2 * k), toep[k][:, 0:P], kv[p][:, 0, :], start=True, stop=True
                          ).then_inc(S["conv_done"], 1)
                pe.matmul(bk(2 * k + 1), toep[k][:, P:2 * P], kv[p][:, 0, :], start=True, stop=False)
                pe.matmul(bk(2 * k + 1), toep[k][:, 0:P], kv[p][:, 1, :], start=False, stop=True
                          ).then_inc(S["conv_done"], 1)

            pe.wait_ge(M[0]["y_done"], MOE[0]["tiles"])
            for h in range(3):
                convolve(h, 0, h, first=True)
            turn_rows(pe, 2)
            pe.wait_ge(S["tr_copied"], 3 * B)
            convolve(3, 0, 3, first=True)
            with pe.Fori(1, HC // TB) as i:
                for k in range(TB):
                    convolve(TB * i + k, i, k)
            pe.wait_ge(S["convT_done"], 2 * HC)
            for b in range(B):
                if b >= 2:
                    pe.wait_ge(S["back_added"], b - 1)
                for c in range(2):
                    ins = pe.transpose(bk(4 + b % 2)[:, P * c:P * (c + 1)], convT[:, c, b, :], identf[:, :])
                ins.then_inc(S["back_done"], 1)
            moe_tensor(pe, 1)


def constants():
    bf = np.dtype("bfloat16")
    c = {}
    c["identf"] = np.eye(P, dtype=np.float32)
    c["identb"] = np.eye(P).astype(bf)
    q, k = np.arange(P)[:, None], np.arange(P)[None, :]
    ssm = np.where((q - k >= 0) & (q - k < WIN_SSM), 0.0, NEG)
    att = np.where((q - k >= 0) & (q - k < WIN_ATT), 0.0, NEG)
    c["masks"] = np.stack([np.concatenate([ssm, att, ssm, att], 1), np.tile(ssm.T, (1, 4)),
                           np.tile(att.T, (1, 4))], 1).astype(bf)
    c["tri"] = (np.arange(P)[:, None] < np.arange(P)[None, :]).astype(bf)
    rows, one = np.arange(P)[:, None], np.ones((P, 1))
    c["ramp"] = np.concatenate([one * np.arange(P), rows, one * (np.arange(2 * B) + 1),
                                2 * T + P + P * np.arange(NT) + rows], 1).astype(np.float32)
    slopes = np.power(np.float32(2.0), -8.0 * np.arange(H0, dtype=np.float32) / H0).astype(np.float32)
    parts, left = [], slopes.copy()
    for _ in range(3):
        parts.append(left.astype(bf))
        left = left - parts[-1].astype(np.float32)
    c["slope_rows"] = np.stack([np.repeat(s, P) for s in parts]).astype(bf)
    pos = np.arange(P) - P // 2
    c["key_rows"] = np.concatenate([np.tile(pos, (3, G0, 2, 1)), np.ones((3, G0, 2, P))]).astype(bf)
    return c


def layouts(i):
    f = {k: np.asarray(v) for k, v in i.items()}
    ctx = f["ctx_2048"]
    w = {"x": f["x"]}

    def chunked(m, rows=P):
        return m.reshape(-1, rows, m.shape[-1]).transpose(1, 0, 2)

    w["ctx_d"] = ctx.reshape(T, KD, P).transpose(2, 1, 0)
    w["ctx_l"] = ctx.reshape(B, P, 2, P)[:, :, :, ::-1].transpose(3, 2, 0, 1)
    w["wq"] = chunked(f["L0_xattn_Wq"].reshape(2 * D, H0, HD).transpose(0, 2, 1).reshape(2 * D, D))
    wk = np.zeros((2, D, HD, G0, 2), np.float32)
    for s, name in enumerate(("L0_xattn_Wsk", "L0_xattn_Wk")):
        wk[s, :, :, :, s] = f[name].reshape(D, G0, HD).transpose(0, 2, 1)
    w["wk"] = chunked(wk.reshape(2 * D, P))
    w["wv"] = np.concatenate([chunked(f["L0_xattn_Wsv"]), chunked(f["L0_xattn_Wv"])], 1)
    w["wo"] = chunked(f["L0_xattn_Wo"])
    w["router"] = chunked(f["L0_ffn_router_w"])
    w1 = f["L0_ffn_W1"].reshape(16, 2, P, 512).transpose(2, 0, 1, 3).reshape(P, 16, 1024)
    w2 = f["L0_ffn_W2"].reshape(16, 4, P, D).transpose(2, 0, 1, 3).reshape(P, 16, 1024)
    w["w_moe0"] = np.concatenate([w1, w2], 2)
    w["kpad"] = np.pad(f["L1_xattn_ssm_kernel"], ((0, 0), (P - 1, 0)))
    w["D"] = f["L1_xattn_D"][:, None]
    w["gate_w"] = chunked(f["L1_ffn_gate_w"])
    gu = np.concatenate([f["L1_ffn_w_gate"], f["L1_ffn_w_up"]], 2)
    gu = gu.reshape(8, 2, P, 352).transpose(2, 0, 1, 3).reshape(P, 8, 704)
    dn = np.pad(f["L1_ffn_w_down"], ((0, 0), (0, 2 * P - 176), (0, 0)))
    dn = dn.reshape(8, 2, P, D).transpose(2, 0, 1, 3).reshape(P, 8, 512)
    w["w_moe1"] = np.concatenate([gu, dn], 2)
    w["sgu"] = chunked(np.concatenate([f["L1_ffn_sw_gate"], f["L1_ffn_sw_up"]], 1))
    w["sdn"] = chunked(np.pad(f["L1_ffn_sw_down"], ((0, 3 * P - 352), (0, 0))))
    w.update(constants())
    return {k: np.ascontiguousarray(v) for k, v in w.items()}


def kernel(**inputs):
    import concourse.bacc as bacc
    from concourse.bass_utils import run_bass_kernel_spmd

    arrays = layouts(inputs)
    nc = bacc.Bacc("TRN2", target_bir_lowering=False, num_devices=1)
    aps = {k: nc.dram_tensor(f"in_{k}", v.shape, mybir.dt.from_np(v.dtype), kind="ExternalInput").ap()
           for k, v in arrays.items()}
    out = nc.dram_tensor("out", (B, P, D), F32, kind="ExternalOutput").ap()
    build(nc, aps, out)
    r = run_bass_kernel_spmd(nc, [{f"in_{k}": v for k, v in arrays.items()}], core_ids=[0])
    return r.results[0]["out"]
```
